# Optimizing a Trainium2 kernel written in Bass

```python
import numpy as np
import jax
import jax.numpy as jnp

def _softmax(x, axis=-1):
    return jax.nn.softmax(x, axis=axis)

def _gelu(x):
    return jax.nn.gelu(x, approximate=True)

def _silu(x):
    return jax.nn.silu(x)

def _sigmoid(x):
    return jax.nn.sigmoid(x)

def _layernorm(x, axis=-1, eps=1e-05):
    m = jnp.mean(x, axis=axis, keepdims=True)
    v = jnp.var(x, axis=axis, keepdims=True)
    return (x - m) / jnp.sqrt(v + eps)

def _scatter_add(tgt, idx, src, axis=0):
    return tgt.at[idx].add(src)

def _segment_sum(src, seg, n):
    return jax.ops.segment_sum(src, seg, n)
kernel_name = 'mk_recurrent_d2_jaxref_r8_4ca49e'

def setup_inputs(seed: int=0):
    np.random.seed(seed)
    _w = jnp.asarray

    def _L0_attn_setup():
        import jax, jax.numpy as jnp
        import numpy as np
        EMB = 256
        HEADS = 16
        G = 2
        HEAD_DIM = EMB // HEADS
        KV = HEADS // G
        B = 2
        S = 256

        def compute_rope(x):
            D = x.shape[2]
            half = D // 2
            inv_freq = 1.0 / 10000.0 ** (jnp.arange(0, half, dtype=jnp.float32) * 2.0 / D)
            pos = jnp.arange(x.shape[1], dtype=jnp.float32)
            ang = pos[:, None] * inv_freq[None, :]
            cos = jnp.concatenate([jnp.cos(ang), jnp.cos(ang)], axis=-1)[None, :, :, None]
            sin = jnp.concatenate([jnp.sin(ang), jnp.sin(ang)], axis=-1)[None, :, :, None]
            x1, x2 = (x[:, :, :half], x[:, :, half:])
            rot = jnp.concatenate([-x2, x1], axis=2)
            return x * cos + rot * sin
        key = jax.random.key(seed)
        ks = jax.random.split(key, 5)
        sc = 0.02
        return {'x': jax.random.normal(ks[0], (B, S, EMB), dtype=jnp.float32), 'W_Q': jax.random.normal(ks[1], (EMB, EMB), dtype=jnp.float32) * sc, 'W_K': jax.random.normal(ks[2], (EMB // G, EMB), dtype=jnp.float32) * sc, 'W_V': jax.random.normal(ks[3], (EMB // G, EMB), dtype=jnp.float32) * sc, 'W_O': jax.random.normal(ks[4], (EMB, EMB), dtype=jnp.float32) * sc}
    _L0_attn_in = _L0_attn_setup()

    def _L0_ffn_setup():
        import jax, jax.numpy as jnp
        import numpy as np
        HIDDEN = 256
        INTER = 688
        LUT_SIZE = 16

        def _ghost_linear(x, idx, lut):
            w = lut[idx]
            return jnp.einsum('bsh,oh->bso', x, w)
        key = jax.random.key(seed)
        k_x, k_lut, k_g, k_u, k_d = jax.random.split(key, 5)
        x = jax.random.normal(k_x, (2, 512, HIDDEN), dtype=jnp.float32)
        lut = jax.random.normal(k_lut, (LUT_SIZE,), dtype=jnp.float32) * 0.02
        gate_idx = jax.random.randint(k_g, (INTER, HIDDEN), 0, LUT_SIZE, dtype=jnp.int32)
        up_idx = jax.random.randint(k_u, (INTER, HIDDEN), 0, LUT_SIZE, dtype=jnp.int32)
        down_idx = jax.random.randint(k_d, (HIDDEN, INTER), 0, LUT_SIZE, dtype=jnp.int32)
        return {'x': x, 'lut': lut, 'gate_idx': gate_idx, 'up_idx': up_idx, 'down_idx': down_idx}
    _L0_ffn_in = _L0_ffn_setup()

    def _L1_attn_setup():
        import jax, jax.numpy as jnp
        import numpy as np
        D_MODEL = 256
        HEAD_SIZE = 64
        N_HEAD = D_MODEL // HEAD_SIZE
        B, T = (2, 128)

        def _layernorm(x, gamma, beta, eps=1e-05):
            mu = jnp.mean(x, axis=-1, keepdims=True)
            var = jnp.var(x, axis=-1, keepdims=True)
            return (x - mu) * jax.lax.rsqrt(var + eps) * gamma + beta

        def _reference_tuple_inner(x, Wx, Ww, bw, Wk, Wv, Wr, Wout, gamma, beta):
            b, t, c = x.shape
            h, n = (N_HEAD, HEAD_SIZE)
            xn = _layernorm(x, gamma, beta)
            w = jax.nn.sigmoid(jnp.einsum('btc,cd->btd', jnp.einsum('btc,cd->btd', xn, Wx), Ww) + bw)
            k = jnp.einsum('btc,cd->btd', xn, Wk)
            v = jnp.einsum('btc,cd->btd', xn, Wv)
            r = jax.nn.sigmoid(jnp.einsum('btc,cd->btd', xn, Wr))

            def tm(a):
                return a.reshape(b, t, h, n).transpose(1, 0, 2, 3)
            k, v, w, r = (tm(k), tm(v), tm(w), tm(r))
            state0 = jnp.zeros((b, h, n, n), x.dtype)

            def step(state, inp):
                k_t, v_t, w_t, r_t = inp
                kv = k_t[..., :, None] * v_t[..., None, :]
                state = (1.0 - w_t)[..., :, None] * state + kv
                y_t = jnp.einsum('bhi,bhij->bhj', r_t, state)
                return (state, y_t)
            state, ys = jax.lax.scan(step, state0, (k, v, w, r))
            y = ys.transpose(1, 0, 2, 3).reshape(b, t, c)
            out = jnp.einsum('btc,cd->btd', y, Wout)
            return (out, state)
        key = jax.random.key(seed)
        ks = jax.random.split(key, 8)
        s = 1.0 / np.sqrt(D_MODEL)
        return {'x': jax.random.normal(ks[0], (B, T, D_MODEL), jnp.float32), 'Wx': jax.random.normal(ks[1], (D_MODEL, D_MODEL), jnp.float32) * s, 'Ww': jax.random.normal(ks[2], (D_MODEL, D_MODEL), jnp.float32) * s, 'bw': jnp.zeros((D_MODEL,), jnp.float32), 'Wk': jax.random.normal(ks[3], (D_MODEL, D_MODEL), jnp.float32) * s, 'Wv': jax.random.normal(ks[4], (D_MODEL, D_MODEL), jnp.float32) * s, 'Wr': jax.random.normal(ks[5], (D_MODEL, D_MODEL), jnp.float32) * s, 'Wout': jax.random.normal(ks[6], (D_MODEL, D_MODEL), jnp.float32) * s, 'gamma': jnp.ones((D_MODEL,), jnp.float32), 'beta': jnp.zeros((D_MODEL,), jnp.float32)}
    _L1_attn_in = _L1_attn_setup()

    def _L1_ffn_setup():
        import jax, jax.numpy as jnp
        import numpy as np
        H = 256
        I = 176
        E = 8
        TOP_K = 2
        N_SHARED = 2
        I_SH = I * N_SHARED
        NORM_TOPK = True

        def _moe_forward(hidden_states, gate_w, expert_gate, expert_up, expert_down, shared_gate, shared_up, shared_down):
            bsz, seq_len, hdim = hidden_states.shape
            x = hidden_states.reshape(-1, hdim)
            logits = x @ gate_w.T
            probs = jax.nn.softmax(logits, axis=-1)
            routing_weights, selected = jax.lax.top_k(probs, TOP_K)
            if NORM_TOPK:
                routing_weights = routing_weights / (routing_weights.sum(axis=-1, keepdims=True) + 1e-20)
            combine = jnp.sum(jax.nn.one_hot(selected, E, dtype=routing_weights.dtype) * routing_weights[..., None], axis=1)
            g_sh = x @ shared_gate.T
            u_sh = x @ shared_up.T
            out = jax.nn.silu(g_sh) * u_sh @ shared_down.T
            g = jnp.einsum('nh,eih->nei', x, expert_gate)
            u = jnp.einsum('nh,eih->nei', x, expert_up)
            y = jnp.einsum('nei,ehi->neh', jax.nn.silu(g) * u, expert_down)
            out = out + jnp.einsum('neh,ne->nh', y, combine)
            return out.reshape(bsz, seq_len, hdim)
        key = jax.random.key(seed)
        ks = jax.random.split(key, 8)
        s = 0.02
        return {'hidden_states': jax.random.normal(ks[0], (1, 128, H), dtype=jnp.float32), 'gate_w': jax.random.normal(ks[1], (E, H), dtype=jnp.float32) * s, 'expert_gate': jax.random.normal(ks[2], (E, I, H), dtype=jnp.float32) * s, 'expert_up': jax.random.normal(ks[3], (E, I, H), dtype=jnp.float32) * s, 'expert_down': jax.random.normal(ks[4], (E, H, I), dtype=jnp.float32) * s, 'shared_gate': jax.random.normal(ks[5], (I_SH, H), dtype=jnp.float32) * s, 'shared_up': jax.random.normal(ks[6], (I_SH, H), dtype=jnp.float32) * s, 'shared_down': jax.random.normal(ks[7], (H, I_SH), dtype=jnp.float32) * s}
    _L1_ffn_in = _L1_ffn_setup()
    _d = {'L0_attn_x': _L0_attn_in['x'], 'L0_attn_W_Q': _L0_attn_in['W_Q'], 'L0_attn_W_K': _L0_attn_in['W_K'], 'L0_attn_W_V': _L0_attn_in['W_V'], 'L0_attn_W_O': _L0_attn_in['W_O'], 'L0_ffn_lut': _L0_ffn_in['lut'], 'L0_ffn_gate_idx': _L0_ffn_in['gate_idx'], 'L0_ffn_up_idx': _L0_ffn_in['up_idx'], 'L0_ffn_down_idx': _L0_ffn_in['down_idx'], 'L1_attn_Wx': _L1_attn_in['Wx'], 'L1_attn_Ww': _L1_attn_in['Ww'], 'L1_attn_bw': _L1_attn_in['bw'], 'L1_attn_Wk': _L1_attn_in['Wk'], 'L1_attn_Wv': _L1_attn_in['Wv'], 'L1_attn_Wr': _L1_attn_in['Wr'], 'L1_attn_Wout': _L1_attn_in['Wout'], 'L1_attn_gamma': _L1_attn_in['gamma'], 'L1_attn_beta': _L1_attn_in['beta'], 'L1_ffn_gate_w': _L1_ffn_in['gate_w'], 'L1_ffn_expert_gate': _L1_ffn_in['expert_gate'], 'L1_ffn_expert_up': _L1_ffn_in['expert_up'], 'L1_ffn_expert_down': _L1_ffn_in['expert_down'], 'L1_ffn_shared_gate': _L1_ffn_in['shared_gate'], 'L1_ffn_shared_up': _L1_ffn_in['shared_up'], 'L1_ffn_shared_down': _L1_ffn_in['shared_down']}
    _x0 = _d['L0_attn_x']
    _d['L0_attn_x'] = jax.random.normal(jax.random.fold_in(jax.random.key(seed), 1), (2, 1024, 256), dtype=_x0.dtype)
    del _x0
    return _d

def reference(L0_attn_x, L0_attn_W_Q, L0_attn_W_K, L0_attn_W_V, L0_attn_W_O, L0_ffn_lut, L0_ffn_gate_idx, L0_ffn_up_idx, L0_ffn_down_idx, L1_attn_Wx, L1_attn_Ww, L1_attn_bw, L1_attn_Wk, L1_attn_Wv, L1_attn_Wr, L1_attn_Wout, L1_attn_gamma, L1_attn_beta, L1_ffn_gate_w, L1_ffn_expert_gate, L1_ffn_expert_up, L1_ffn_expert_down, L1_ffn_shared_gate, L1_ffn_shared_up, L1_ffn_shared_down):

    def _L0_attn_ref(x, W_Q, W_K, W_V, W_O):
        import jax, jax.numpy as jnp
        import numpy as np
        EMB = 256
        HEADS = 16
        G = 2
        HEAD_DIM = EMB // HEADS
        KV = HEADS // G
        B = 2
        S = 256

        def compute_rope(x):
            D = x.shape[2]
            half = D // 2
            inv_freq = 1.0 / 10000.0 ** (jnp.arange(0, half, dtype=jnp.float32) * 2.0 / D)
            pos = jnp.arange(x.shape[1], dtype=jnp.float32)
            ang = pos[:, None] * inv_freq[None, :]
            cos = jnp.concatenate([jnp.cos(ang), jnp.cos(ang)], axis=-1)[None, :, :, None]
            sin = jnp.concatenate([jnp.sin(ang), jnp.sin(ang)], axis=-1)[None, :, :, None]
            x1, x2 = (x[:, :, :half], x[:, :, half:])
            rot = jnp.concatenate([-x2, x1], axis=2)
            return x * cos + rot * sin
        Bsz, Sl, E = x.shape
        q = (x @ W_Q.T).reshape(Bsz, Sl, HEAD_DIM, HEADS)
        k = (x @ W_K.T).reshape(Bsz, Sl, HEAD_DIM, KV)
        v = (x @ W_V.T).reshape(Bsz, Sl, HEAD_DIM, KV)
        q = compute_rope(q)
        k = compute_rope(k)
        q = q.reshape(Bsz, Sl, HEAD_DIM, KV, G)
        scores = jnp.einsum('bsdkg,btdk->bkgst', q, k) / jnp.sqrt(jnp.float32(E))
        w = jax.nn.softmax(scores, axis=-1)
        ctx = jnp.einsum('bkgst,btdk->bkgsd', w, v)
        ctx = ctx.reshape(Bsz, HEADS, Sl, HEAD_DIM).transpose(0, 2, 1, 3).reshape(Bsz, Sl, E)
        return ctx @ W_O.T

    def _L0_ffn_ref(x, lut, gate_idx, up_idx, down_idx):
        import jax, jax.numpy as jnp
        import numpy as np
        HIDDEN = 256
        INTER = 688
        LUT_SIZE = 16

        def _ghost_linear(x, idx, lut):
            w = lut[idx]
            return jnp.einsum('bsh,oh->bso', x, w)
        gate = _ghost_linear(x, gate_idx, lut)
        up = _ghost_linear(x, up_idx, lut)
        h = jax.nn.silu(gate) * up
        return _ghost_linear(h, down_idx, lut)

    def _L1_attn_ref(x, Wx, Ww, bw, Wk, Wv, Wr, Wout, gamma, beta):
        import jax, jax.numpy as jnp
        import numpy as np
        D_MODEL = 256
        HEAD_SIZE = 64
        N_HEAD = D_MODEL // HEAD_SIZE
        B, T = (2, 128)

        def _layernorm(x, gamma, beta, eps=1e-05):
            mu = jnp.mean(x, axis=-1, keepdims=True)
            var = jnp.var(x, axis=-1, keepdims=True)
            return (x - mu) * jax.lax.rsqrt(var + eps) * gamma + beta

        def _reference_tuple_inner(x, Wx, Ww, bw, Wk, Wv, Wr, Wout, gamma, beta):
            b, t, c = x.shape
            h, n = (N_HEAD, HEAD_SIZE)
            xn = _layernorm(x, gamma, beta)
            w = jax.nn.sigmoid(jnp.einsum('btc,cd->btd', jnp.einsum('btc,cd->btd', xn, Wx), Ww) + bw)
            k = jnp.einsum('btc,cd->btd', xn, Wk)
            v = jnp.einsum('btc,cd->btd', xn, Wv)
            r = jax.nn.sigmoid(jnp.einsum('btc,cd->btd', xn, Wr))

            def tm(a):
                return a.reshape(b, t, h, n).transpose(1, 0, 2, 3)
            k, v, w, r = (tm(k), tm(v), tm(w), tm(r))
            state0 = jnp.zeros((b, h, n, n), x.dtype)

            def step(state, inp):
                k_t, v_t, w_t, r_t = inp
                kv = k_t[..., :, None] * v_t[..., None, :]
                state = (1.0 - w_t)[..., :, None] * state + kv
                y_t = jnp.einsum('bhi,bhij->bhj', r_t, state)
                return (state, y_t)
            state, ys = jax.lax.scan(step, state0, (k, v, w, r))
            y = ys.transpose(1, 0, 2, 3).reshape(b, t, c)
            out = jnp.einsum('btc,cd->btd', y, Wout)
            return (out, state)
        return _reference_tuple_inner(x, Wx, Ww, bw, Wk, Wv, Wr, Wout, gamma, beta)[0]

    def _L1_ffn_ref(hidden_states, gate_w, expert_gate, expert_up, expert_down, shared_gate, shared_up, shared_down):
        import jax, jax.numpy as jnp
        import numpy as np
        H = 256
        I = 176
        E = 8
        TOP_K = 2
        N_SHARED = 2
        I_SH = I * N_SHARED
        NORM_TOPK = True

        def _moe_forward(hidden_states, gate_w, expert_gate, expert_up, expert_down, shared_gate, shared_up, shared_down):
            bsz, seq_len, hdim = hidden_states.shape
            x = hidden_states.reshape(-1, hdim)
            logits = x @ gate_w.T
            probs = jax.nn.softmax(logits, axis=-1)
            routing_weights, selected = jax.lax.top_k(probs, TOP_K)
            if NORM_TOPK:
                routing_weights = routing_weights / (routing_weights.sum(axis=-1, keepdims=True) + 1e-20)
            combine = jnp.sum(jax.nn.one_hot(selected, E, dtype=routing_weights.dtype) * routing_weights[..., None], axis=1)
            g_sh = x @ shared_gate.T
            u_sh = x @ shared_up.T
            out = jax.nn.silu(g_sh) * u_sh @ shared_down.T
            g = jnp.einsum('nh,eih->nei', x, expert_gate)
            u = jnp.einsum('nh,eih->nei', x, expert_up)
            y = jnp.einsum('nei,ehi->neh', jax.nn.silu(g) * u, expert_down)
            out = out + jnp.einsum('neh,ne->nh', y, combine)
            return out.reshape(bsz, seq_len, hdim)
        return _moe_forward(hidden_states, gate_w, expert_gate, expert_up, expert_down, shared_gate, shared_up, shared_down)
    x = L0_attn_x
    xn = _layernorm(x, axis=-1)
    s = _L0_attn_ref(xn, L0_attn_W_Q, L0_attn_W_K, L0_attn_W_V, L0_attn_W_O)
    g = _silu(_L0_ffn_ref(xn, L0_ffn_lut, L0_ffn_gate_idx, L0_ffn_up_idx, L0_ffn_down_idx))
    x = x + s * g
    xn = _layernorm(x, axis=-1)
    s = _L1_attn_ref(xn, L1_attn_Wx, L1_attn_Ww, L1_attn_bw, L1_attn_Wk, L1_attn_Wv, L1_attn_Wr, L1_attn_Wout, L1_attn_gamma, L1_attn_beta)
    g = _silu(_L1_ffn_ref(xn, L1_ffn_gate_w, L1_ffn_expert_gate, L1_ffn_expert_up, L1_ffn_expert_down, L1_ffn_shared_gate, L1_ffn_shared_up, L1_ffn_shared_down))
    x = x + s * g
    return x

_drawn_inputs = setup_inputs


def setup_inputs(seed=0):
    import zlib

    import numpy as np

    out = dict(_drawn_inputs(seed))
    spreads = {'L1_attn_bw': (0.0, 0.1), 'L1_attn_gamma': (1.0, 0.2), 'L1_attn_beta': (0.0, 0.1)}
    factors = {}
    for name, (base, spread) in spreads.items():
        noise = np.random.default_rng([zlib.crc32(name.encode()), seed]).standard_normal(out[name].shape)
        drawn = base * np.exp(spread * noise) if base else spread * noise
        out[name] = jnp.asarray(drawn.astype(out[name].dtype))
    for name, factor in factors.items():
        out[name] = (out[name] * factor).astype(out[name].dtype)
    return out
```

```python
from contextlib import ExitStack

import concourse.bass as bass
from concourse import mybir

F32 = mybir.dt.float32
F32R = mybir.dt.float32r
BF16 = mybir.dt.bfloat16
I32 = mybir.dt.int32
ALU = mybir.AluOpType
ACT = mybir.ActivationFunctionType
AX_X = mybir.AxisListType.X
AX_XY = mybir.AxisListType.XY

P = 128
B, S, E = 2, 1024, 256
T = B * S
NT = T // P
KC = E // P
BLK = 512
NB = T // BLK
TPB = BLK // P

HEADS, G, HD = 16, 2, 16
KV = HEADS // G
HALF = HD // 2
SLOTS = ((0, 0), (0, 1), (0, 2), (1, 0), (1, 1), (2, 0))
NROW = HD * len(SLOTS)
NAUG = NROW + 3
VW = 32

INTER = 688
LUT = 16
NI = (INTER + P - 1) // P

EPS = 1e-5


class Mem:
    pass


def parts(n, size):
    return [(i, min(size, n - i)) for i in range(0, n, size)]


def program(nc, a):
    with ExitStack() as ctx:
        m = Mem()
        off = [16512]

        def at(name, shape, dt, offset):
            return nc.alloc_sbuf_tensor_at(name, shape, dt, offset=offset)

        def sem(name):
            return ctx.enter_context(nc.semaphore(name))

        m.at, m.sem = at, sem
        m.psum = ctx.enter_context(nc.psum_tensor("psum", [P, 8, BLK], F32))
        m.bank = [m.psum[:, i, :] for i in range(8)]
        base = 16512
        m.x = at("x_tok", [P, NT, E], F32, base)
        m.base = base + NT * E * 4
        b = m.base
        m.xTh = at("xTh", [P, KC, T], F32R, b)
        m.xTl = at("xTl", [P, KC, T], F32R, b + KC * T * 4)
        b += 2 * KC * T * 4
        m.ident = at("ident", [P, P], F32, b)
        m.rstd = at("rstd", [P, NT], F32, b + 512)
        m.mv = at("mv", [P, NT, 2], F32, b + 640)
        b += 1024
        m.l0 = b
        m.q_parts = nc.dram_tensor("q_parts", (3, 2, P, T), BF16, kind="Internal").ap()
        m.k_parts = nc.dram_tensor("k_parts", (3, 2, P // 2, T), BF16, kind="Internal").ap()
        m.m_rows = nc.dram_tensor("m_rows", (B * KV, 3, G * S), BF16, kind="Internal").ap()
        m.den_rows = nc.dram_tensor("den_rows", (B * KV, G * S), F32, kind="Internal").ap()
        m.rec_rows = nc.dram_tensor("rec_rows", (B * KV, G * S), F32, kind="Internal").ap()
        qkv_stage(nc, m, a)
        attention_stage(nc, m, a)
        ffn_stage(nc, m, a)
        time_mix_in_stage(nc, m, a)
        time_mix_stage(nc, m, a)
        experts_stage(nc, m, a)


def qkv_stage(nc, m, a):
    at, sem, bank = m.at, m.sem, m.bank
    b = m.l0
    m.VS = at("VS", [P, NT, KV, VW], F32, b); b += NT * KV * VW * 4
    m.wo = at("wo_raw", [P, KC, E], F32, b); b += KC * E * 4
    m.p0 = b
    NQ = E + 2 * P + P
    wraw = at("wqkv_raw", [P, KC, NQ], F32, b); b += KC * NQ * 4
    wh = at("wqkv_h", [P, KC, NQ], F32R, b); b += KC * NQ * 4
    wl = at("wqkv_l", [P, KC, NQ], F32R, b); b += KC * NQ * 4
    cos = at("cos", [P, S], F32, b); b += S * 4
    sin = at("sin", [P, S], F32, b); b += S * 4
    sink = at("sink", [P, S], F32, b); b += S * 4
    xn = at("xn", [P, 2, TPB, E], F32, b); b += 2 * TPB * E * 4
    prod = at("rope_prod", [P, 6, BLK], F32, b); b += 6 * BLK * 4
    rot = at("rotated", [P, 3, BLK], F32, b); b += 3 * BLK * 4
    res = at("residue", [P, 3, BLK], F32, b); b += 3 * BLK * 4
    part = at("part", [P, 2, 3, 3, BLK], BF16, b); b += 18 * BLK * 2
    st = at("bn_st", [P, NT, 6], F32, b); b += NT * 6 * 4
    ve = at("var_eps", [P, NT], F32, b); b += NT * 4
    mhalf = at("minus_half", [P, TPB], F32, b); b += 32
    assert b <= nc.sbuf_usable_end, b

    x_in = [sem(f"x_in{g}") for g in range(NB)]
    w_in, tab_in, id_in, wo_in = sem("w_in"), sem("tab_in"), sem("id_in"), sem("wo_in")
    w_ready, stats, var_ready, rstd_ready = sem("w_ready"), sem("stats"), sem("var_ready"), sem("rstd_ready")
    const_ready, xn_ready, xt_ps, xt_hi, xt_lo = sem("const_ready"), sem("xn_ready"), sem("xt_ps"), sem("xt_hi"), sem("xt_lo")
    q_ps, k_ps, v_ps, v_out = sem("q_ps"), sem("k_ps"), sem("v_ps"), sem("v_out")
    prod_q, prod_k, rot_ready, part1, resid, part2, part3 = (
        sem(n) for n in ("prod_q", "prod_k", "rot_ready", "part1", "resid", "part2", "part3"))
    part_out = [sem("part_out0"), sem("part_out1")]
    wh_ready = sem("wh_ready")

    with nc.Block() as block:
        @block.sync
        def _(sp):
            for g in range(NB):
                sp.dma_start(m.x[:, g * TPB:(g + 1) * TPB, :],
                             a["x"].rearrange("(n p) f -> p n f", p=P)[:, g * TPB:(g + 1) * TPB, :]).then_inc(x_in[g], 16)
            sp.dma_start(cos[:], a["cos"]).then_inc(tab_in, 16)
            sp.dma_start(sin[:], a["sin"]).then_inc(tab_in, 16)
            sp.dma_start(sink[:], a["sink"]).then_inc(tab_in, 16)
            sp.dma_start(m.wo[:], a["wo"].rearrange("(c p) n -> p c n", p=P)).then_inc(wo_in, 16)
            for tb in range(NB):
                cols = slice(tb * BLK, (tb + 1) * BLK)
                for i in range(3):
                    for u in range(3):
                        if i == 0:
                            sp.wait_ge(part1, 3 * tb + u + 1)
                        elif i == 1:
                            sp.wait_ge(part2, 3 * tb + u + 1)
                        else:
                            sp.wait_ge(part3, 3 * tb + u + 1)
                        if u < 2:
                            sp.dma_start(m.q_parts[i, u, :, cols], part[:, tb % 2, u, i, :]).then_inc(part_out[tb % 2], 16)
                        else:
                            sp.dma_start(m.k_parts[i].rearrange("u r t -> (u r) t")[:, cols],
                                         part[:, tb % 2, u, i, :]).then_inc(part_out[tb % 2], 16)
            sp.wait_ge(wo_in, 16)
            sp.wait_ge(part_out[0], 16 * 9 * NB // 2)
            sp.wait_ge(part_out[1], 16 * 9 * NB // 2)

        @block.scalar
        def _(act):
            act.dma_start(m.ident[:], a["ident"]).then_inc(id_in, 16)
            act.dma_start(wraw[:], a["wqkv"].rearrange("(c p) n -> p c n", p=P)).then_inc(w_in, 16)
            act.wait_ge(w_in, 16)
            nc.scalar.activation(wh[:], wraw[:], ACT.Copy).then_inc(wh_ready, 1)

            def take_xt(g):
                for kc in range(KC):
                    act.wait_ge(xt_ps, g * KC + kc + 1)
                    nc.scalar.activation(m.xTh[:, kc, g * BLK:(g + 1) * BLK], bank[kc][:], ACT.Copy).then_inc(xt_hi, 1)

            def cut(tb):
                for u in range(3):
                    act.wait_ge(rot_ready, 3 * tb + u + 1)
                    if tb >= 2:
                        act.wait_ge(part_out[tb % 2], 16 * 9 * (tb // 2))
                    nc.scalar.activation(part[:, tb % 2, u, 0, :], rot[:, u, :], ACT.Copy).then_inc(part1, 1)
                for u in range(3):
                    act.wait_ge(resid, 3 * tb + u + 1)
                    nc.scalar.activation(part[:, tb % 2, u, 1, :], res[:, u, :], ACT.Copy).then_inc(part2, 1)

            def take_v(tb):
                act.wait_ge(v_ps, tb + 1)
                act.wait_ge(const_ready, 2)
                for i in range(TPB):
                    nc.scalar.activation(m.VS[:, tb * TPB + i, :, 0:HD],
                                         bank[2 + tb % 2][:, i * P:(i + 1) * P].rearrange("p (k d) -> p k d", k=KV),
                                         ACT.Copy).then_inc(v_out, 1)
            for g in range(NB):
                take_xt(g)
                if g >= 1:
                    take_v(g - 1)
                    cut(g - 1)
            take_v(NB - 1)
            cut(NB - 1)

        def third_parts(pool, tb):
            for u in range(3):
                pool.wait_ge(part2, 3 * tb + u + 1)
                nc.gpsimd.tensor_tensor(part[:, tb % 2, u, 2, :], res[:, u, :], part[:, tb % 2, u, 1, :],
                                        ALU.subtract).then_inc(part3, 1)

        @block.gpsimd
        def _(pool):
            nc.gpsimd.memset(mhalf[:], -0.5).then_inc(const_ready, 1)
            nc.gpsimd.memset(m.VS[:], 1.0).then_inc(const_ready, 1)
            for g in range(NB):
                pool.wait_ge(const_ready, 1)
                pool.wait_ge(var_ready, g + 1)
                nc.gpsimd.tensor_tensor(m.rstd[:, g * TPB:(g + 1) * TPB], ve[:, g * TPB:(g + 1) * TPB], mhalf[:],
                                        ALU.pow).then_inc(rstd_ready, 1)
                if g == 0:
                    pool.wait_ge(wh_ready, 1)
                    nc.gpsimd.tensor_tensor(wl[:], wraw[:], wh[:], ALU.subtract).then_inc(w_ready, 1)
                if g >= 1:
                    third_parts(pool, g - 1)
            third_parts(pool, NB - 1)

        @block.vector
        def _(dve):
            def norm(g):
                dve.wait_ge(x_in[g], 16)
                for i in range(g * TPB, (g + 1) * TPB):
                    nc.vector.bn_stats(st[:, i, :], m.x[:, i, :]).then_inc(stats, 1)
                dve.wait_ge(stats, (2 * g + 1) * TPB)
                for i in range(g * TPB, (g + 1) * TPB):
                    nc.vector.bn_aggr(m.mv[:, i, :], st[:, i, :]).then_inc(stats, 1)
                dve.wait_ge(stats, (2 * g + 2) * TPB)
                nc.vector.tensor_scalar(ve[:, g * TPB:(g + 1) * TPB], m.mv[:, g * TPB:(g + 1) * TPB, 1], EPS, None,
                                        ALU.add).then_inc(var_ready, 1)
                dve.wait_ge(rstd_ready, g + 1)
                if g >= 2:
                    dve.wait_ge(xt_ps, KC * (g - 1))
                for i in range(TPB):
                    n = g * TPB + i
                    nc.vector.tensor_scalar(xn[:, g % 2, i, :], m.x[:, n, :], m.mv[:, n, 0:1], m.rstd[:, n:n + 1],
                                            ALU.subtract, ALU.mult).then_inc(xn_ready, 1)

            def low(g):
                for kc in range(KC):
                    dve.wait_ge(xt_hi, g * KC + kc + 1)
                    cols = slice(g * BLK, (g + 1) * BLK)
                    nc.vector.tensor_tensor(m.xTl[:, kc, cols], bank[kc][:], m.xTh[:, kc, cols],
                                            ALU.subtract).then_inc(xt_lo, 1)

            def rope(tb):
                pos = slice((tb % (S // BLK)) * BLK, (tb % (S // BLK) + 1) * BLK)
                if tb == 0:
                    dve.wait_ge(tab_in, 48)
                if tb >= 1:
                    dve.wait_ge(rot_ready, 3 * tb)
                dve.wait_ge(q_ps, tb + 1)
                nc.vector.tensor_tensor(prod[:, 0, :], bank[4][:], cos[:, pos], ALU.mult).then_inc(prod_q, 1)
                nc.vector.tensor_tensor(prod[:, 1, :], bank[5][:], sin[:, pos], ALU.mult).then_inc(prod_q, 1)
                nc.vector.tensor_tensor(prod[:, 2, :], bank[5][:], cos[:, pos], ALU.mult).then_inc(prod_q, 1)
                nc.vector.tensor_tensor(prod[:, 3, :], bank[4][:], sin[:, pos], ALU.mult).then_inc(prod_q, 1)
                dve.wait_ge(k_ps, tb + 1)
                nc.vector.tensor_tensor(prod[:, 4, :], bank[6][:], cos[:, pos], ALU.mult).then_inc(prod_k, 1)
                nc.vector.tensor_tensor(prod[:, 5, :], bank[7][:], sink[:, pos], ALU.mult).then_inc(prod_k, 1)
                if tb >= 1:
                    dve.wait_ge(part1, 3 * tb)
                    dve.wait_ge(resid, 3 * tb)
                dve.wait_ge(prod_q, 4 * tb + 4)
                nc.vector.tensor_tensor(rot[:, 0, :], prod[:, 0, :], prod[:, 1, :], ALU.subtract).then_inc(rot_ready, 1)
                nc.vector.tensor_tensor(rot[:, 1, :], prod[:, 2, :], prod[:, 3, :], ALU.add).then_inc(rot_ready, 1)
                dve.wait_ge(prod_k, 2 * tb + 2)
                nc.vector.tensor_tensor(rot[:, 2, :], prod[:, 4, :], prod[:, 5, :], ALU.add).then_inc(rot_ready, 1)
                for u in range(3):
                    dve.wait_ge(part1, 3 * tb + u + 1)
                    if tb >= 1:
                        dve.wait_ge(part3, 3 * (tb - 1) + u + 1)
                    nc.vector.tensor_tensor(res[:, u, :], rot[:, u, :], part[:, tb % 2, u, 0, :],
                                            ALU.subtract).then_inc(resid, 1)

            norm(0)
            for g in range(NB):
                low(g)
                if g + 1 < NB:
                    norm(g + 1)
                rope(g)

        @block.tensor
        def _(pe):
            pe.wait_ge(id_in, 16)

            def turn(g):
                pe.wait_ge(xn_ready, TPB * (g + 1))
                for kc in range(KC):
                    if g >= 1:
                        pe.wait_ge(xt_lo, (g - 1) * KC + kc + 1)
                    for i in range(TPB):
                        mm = nc.tensor.transpose(bank[kc][:, i * P:(i + 1) * P], xn[:, g % 2, i, kc * P:(kc + 1) * P],
                                                 m.ident[:])
                    mm.then_inc(xt_ps, 1)

            def project(tb):
                cols = slice(tb * BLK, (tb + 1) * BLK)
                pe.wait_ge(xt_lo, KC * (tb + 1))
                if tb == 0:
                    pe.wait_ge(w_ready, 1)
                for j in range(4):
                    if tb >= 1 and j == 0:
                        pe.wait_ge(prod_q, 4 * tb)
                    if tb >= 1 and j == 2:
                        pe.wait_ge(prod_k, 2 * tb)
                    mm = three(nc, bank[4 + j][:], [(wh[:, kc, j * P:(j + 1) * P], wl[:, kc, j * P:(j + 1) * P],
                                                     m.xTh[:, kc, cols], m.xTl[:, kc, cols]) for kc in range(KC)])
                    if j == 1:
                        mm.then_inc(q_ps, 1)
                    if j == 3:
                        mm.then_inc(k_ps, 1)
                if tb >= 2:
                    pe.wait_ge(v_out, TPB * (tb - 1))
                for i in range(TPB):
                    tok = slice(tb * BLK + i * P, tb * BLK + (i + 1) * P)
                    mm = three(nc, bank[2 + tb % 2][:, i * P:(i + 1) * P],
                               [(m.xTh[:, kc, tok], m.xTl[:, kc, tok], wh[:, kc, 4 * P:], wl[:, kc, 4 * P:])
                                for kc in range(KC)])
                mm.then_inc(v_ps, 1)

            turn(0)
            for g in range(NB):
                if g + 1 < NB:
                    turn(g + 1)
                project(g)


def three(nc, out, operands, start=True, stop=True):
    n = len(operands)
    for i, (lh, ll, rh, rl) in enumerate(operands):
        nc.tensor.matmul(out, ll, rh, start=start and i == 0, stop=False)
        nc.tensor.matmul(out, lh, rl, start=False, stop=False)
        mm = nc.tensor.matmul(out, lh, rh, start=False, stop=stop and i == n - 1)
    return mm


def attention_stage(nc, m, a):
    at, sem, bank = m.at, m.sem, m.bank
    NG = B * KV
    NTT = S // P
    NJ = G * S // BLK
    NST = G * S // P
    b = m.p0
    QS = [at(f"QS{i}", [NAUG, G * S], BF16, b + i * G * S * 2) for i in range(3)]; b += 3 * G * S * 2
    KS = [at(f"KS{i}", [NAUG, S], BF16, b + i * S * 2) for i in range(3)]; b += 3 * S * 2
    NPT = 2 * NJ
    pt = at("probs_t", [P, NPT, BLK], F32, b); b += NPT * BLK * 4
    osb = at("o_sb", [P, 2, BLK], F32, b); b += 2 * BLK * 4
    m.ctxT = at("ctxT", [P, KC, T], F32, b); b += KC * T * 4
    m.after_ctx = b
    rec = at("rec_b", [P, 2, S], F32, b); b += 2 * S * 4
    mx = at("row_max", [P, 2, 32], F32, b); b += 2 * 32 * 4
    mT = at("row_max_t", [P, 32], F32, b); b += 32 * 4
    mres = at("max_res", [P, 2, 32], F32, b); b += 2 * 32 * 4
    mpt = at("max_parts", [P, 3, 32], BF16, b); b += 3 * 32 * 2
    den = at("den", [P, NST], F32, b); b += NST * 4
    rden = at("rden", [P, NST], F32, b); b += NST * 4
    m.p1 = b
    NLUT = m.NLUT = KC * 2 * INTER + NI * E
    NPIECE = 4
    PIECE = NLUT // NPIECE
    idx = at("lut_idx", [P, NLUT], I32, b)
    m.fl = at("ffn_l", [P, NLUT], F32R, b); b += NLUT * 4
    m.fh = at("ffn_h", [P, NLUT], F32R, b); b += NLUT * 4
    wsum = at("lut_sum", [P, NLUT], F32, b); b += NLUT * 4
    wtmp = at("lut_tmp", [P, 3, PIECE], F32, b); b += 3 * PIECE * 4
    m.woh = at("wo_h", [P, KC, E], F32R, b); b += KC * E * 4
    m.wol = at("wo_l", [P, KC, E], F32R, b); b += KC * E * 4
    lut = at("lut", [P, LUT], F32, b); b += LUT * 4
    assert b <= nc.sbuf_usable_end, b
    lut_in, idx_in, lut_prod, lut_add, f_hi, f_lo = (
        sem(n) for n in ("lut_in", "idx_in", "lut_prod", "lut_add", "f_hi", "f_lo"))

    qk_in = [sem(f"qk_in{i}") for i in range(3)]
    ones_ready, mx_zero = sem("ones_ready"), sem("mx_zero")
    max_ps, max_done, mt_done, mp_done, mp_out, m_in = (
        sem(n) for n in ("max_ps", "max_done", "mt_done", "mp_done", "mp_out", "m_in"))
    s_ps, p_ready, pv_done, o_done = sem("s_ps"), sem("p_ready"), sem("pv_done"), sem("o_done")
    o_out, den_out, den_in, rden_ready, rden_out, rec_in, norm_done = (
        sem(n) for n in ("o_out", "den_out", "den_in", "rden_ready", "rden_out", "rec_in", "norm_done"))
    mres_done = sem("mres_done")
    MX = [bank[0:2], bank[2:4]]
    SP = bank[4:7]
    OB = bank[7]
    def ring(i):
        return SP[i % 3]

    with nc.Block() as block:
        @block.sync
        def _(sp):
            def load_qk(n):
                bb, kv = divmod(n, KV)
                if n >= 3:
                    sp.wait_ge(s_ps, (n - 2) * NTT * NJ)
                for u in range(2):
                    r = u * NROW // 2
                    for slot, (qi, ki) in enumerate(SLOTS):
                        rows = slice(r + slot * HALF, r + (slot + 1) * HALF)
                        q = m.q_parts[qi, u, kv * G * HALF:(kv + 1) * G * HALF, bb * S:(bb + 1) * S]
                        sp.dma_start(QS[n % 3][rows, :].rearrange("d (g c) -> d g c", g=G),
                                     q.rearrange("(g d) c -> d g c", g=G)).then_inc(qk_in[n % 3], 16)
                        sp.dma_start(KS[n % 3][rows, :],
                                     m.k_parts[ki, u, kv * HALF:(kv + 1) * HALF, bb * S:(bb + 1) * S]
                                     ).then_inc(qk_in[n % 3], 16)

            def place_max(n):
                sp.wait_ge(mp_done, 3 * (n + 1))
                for q in range(4):
                    sp.dma_start(m.m_rows[n].rearrange("i (c q s) -> q c i s", q=4, s=32)[q],
                                 mpt[32 * q:32 * q + NST, :, :]).then_inc(mp_out, 16)
                sp.wait_ge(mp_out, 64 * (n + 1))
                sp.dma_start(QS[n % 3][NROW:NAUG, :], m.m_rows[n]).then_inc(m_in, 16)

            def leave(n):
                bb, kv = divmod(n, KV)
                sp.wait_ge(o_done, n + 1)
                ct, r = kv // 4, kv % 4 * G * HD
                for j in range(NJ):
                    g, half = divmod(j, NJ // G)
                    sp.dma_start(m.ctxT[r + g * HD:r + (g + 1) * HD, ct,
                                        bb * S + half * BLK:bb * S + (half + 1) * BLK],
                                 osb[32 * j:32 * j + HD, n % 2, :]).then_inc(o_out, 16)
                    sp.dma_start(m.den_rows[n, j * BLK:(j + 1) * BLK].rearrange("(o s) -> o s", o=1),
                                 osb[32 * j + HD:32 * j + HD + 1, n % 2, :]).then_inc(den_out, 16)
                sp.wait_ge(den_out, 16 * NJ * (n + 1))
                sp.wait_ge(o_out, 16 * NJ * (n + 1))
                if n >= 1:
                    sp.wait_ge(rden_ready, n)
                sp.dma_start(den[:], m.den_rows[n].rearrange("(p c) -> p c", p=P)).then_inc(den_in, 16)

            def spread(n):
                bb, kv = divmod(n, KV)
                r = kv % 4 * G * HD
                sp.wait_ge(rden_ready, n + 1)
                if n >= 1:
                    sp.wait_ge(rec_in, 16 * G * n)
                sp.dma_start(m.rec_rows[n].rearrange("(p c) -> p c", p=P), rden[:]).then_inc(rden_out, 16)
                sp.wait_ge(rden_out, 16 * (n + 1))
                if n >= 8:
                    sp.wait_ge(norm_done, n // 4 - 1)
                for g in range(G):
                    sp.dma_start(rec[r + g * HD:r + (g + 1) * HD, (n // 4) % 2, :],
                                 m.rec_rows[n, g * S:(g + 1) * S].rearrange("(o s) -> o s", o=1)
                                 .broadcast_to([HD, S])).then_inc(rec_in, 16)

            for n in range(3):
                load_qk(n)
            sp.dma_start(lut[:], a["lut"].rearrange("(o s) -> o s", o=1).broadcast_to([P, LUT])).then_inc(lut_in, 16)
            sp.dma_start(idx[:, 0:KC * 2 * INTER].rearrange("p (c n) -> p c n", c=KC),
                         a["gu_idx"].rearrange("(c p) n -> p c n", p=P)).then_inc(idx_in, 16)
            sp.dma_start(idx[:, KC * 2 * INTER:].rearrange("p (c n) -> p c n", c=NI),
                         a["down_idx"].rearrange("(c p) n -> p c n", p=P)).then_inc(idx_in, 16)
            place_max(0)
            for n in range(NG):
                if n >= 1:
                    if n + 2 < NG:
                        load_qk(n + 2)
                    leave(n - 1)
                    spread(n - 1)
                if n + 1 < NG:
                    place_max(n + 1)
            leave(NG - 1)
            spread(NG - 1)
            sp.wait_ge(o_out, 16 * NJ * NG)
            sp.wait_ge(rec_in, 16 * G * NG)

        def normalize(pool, c):
            bb, ct = divmod(c, KC)
            pool.wait_ge(o_out, 16 * NJ * 4 * (c + 1))
            pool.wait_ge(rec_in, 16 * G * 4 * (c + 1))
            v = m.ctxT[:, ct, bb * S:(bb + 1) * S]
            nc.gpsimd.tensor_tensor(v, v, rec[:, c % 2, :], ALU.mult).then_inc(norm_done, 1)

        def low_part(pool, c):
            cols = slice(c * PIECE, (c + 1) * PIECE)
            if c == 0:
                pool.wait_ge(f_hi, 1)
                nc.gpsimd.tensor_tensor(m.wol[:], m.wo[:], m.woh[:], ALU.subtract).then_inc(f_lo, 1)
            pool.wait_ge(f_hi, c + 2)
            nc.gpsimd.tensor_tensor(m.fl[:, cols], wsum[:, cols], m.fh[:, cols], ALU.subtract).then_inc(f_lo, 1)

        @block.gpsimd
        def _(pool):
            nc.gpsimd.memset(KS[0][NROW:NAUG, :], 1.0).then_inc(ones_ready, 1)
            nc.gpsimd.memset(KS[1][NROW:NAUG, :], 1.0).then_inc(ones_ready, 1)
            nc.gpsimd.memset(KS[2][NROW:NAUG, :], 1.0).then_inc(ones_ready, 1)
            for c in range(NG // 4):
                cols = slice(c * PIECE, (c + 1) * PIECE)
                for v in range(1, LUT):
                    k = c * (LUT - 1) + v - 1
                    pool.wait_ge(lut_prod, c * LUT + v + 1)
                    if k >= 1:
                        pool.wait_ge(lut_add, k)
                    nc.gpsimd.tensor_tensor(wsum[:, cols], wsum[:, cols], wtmp[:, k % 3, :],
                                            ALU.add).then_inc(lut_add, 1)
                if c >= 1:
                    low_part(pool, c - 1)
                    normalize(pool, c - 1)
            low_part(pool, NPIECE - 1)
            normalize(pool, NPIECE - 1)

        def take_high(act, c):
            cols = slice(c * PIECE, (c + 1) * PIECE)
            act.wait_ge(lut_add, (c + 1) * (LUT - 1))
            nc.scalar.activation(m.fh[:, cols], wsum[:, cols], ACT.Copy).then_inc(f_hi, 1)

        @block.scalar
        def _(act):
            for n in range(NG):
                if n == 2 or n >= 4 and n % 4 == 0:
                    if n == 2:
                        nc.scalar.activation(m.woh[:], m.wo[:], ACT.Copy).then_inc(f_hi, 1)
                    else:
                        take_high(act, n // 4 - 1)
                for i in range(NTT * NJ):
                    k = n * NTT * NJ + i
                    act.wait_ge(s_ps, k + 1)
                    if k >= NPT:
                        act.wait_ge(pv_done, k - NPT + 1)
                    nc.scalar.activation(pt[:, k % NPT, :], ring(k)[:], ACT.Exp,
                                         scale=float(E) ** -0.5).then_inc(p_ready, 1)
            take_high(act, NPIECE - 1)

        @block.vector
        def _(dve):
            nc.vector.memset(mx[:], 0.0).then_inc(mx_zero, 1)
            dve.wait_ge(mx_zero, 1)

            def row_max(n, i):
                k = n * NST + i
                dve.wait_ge(max_ps, k + 1)
                if i == 0 and n >= 2:
                    dve.wait_ge(mt_done, n - 1)
                nc.vector.tensor_reduce(mx[:, n % 2, i:i + 1], m.psum[:, 2 * (k % 2):2 * (k % 2) + 2, :], AX_XY, ALU.max).then_inc(max_done, 1)

            def max_parts(n):
                dve.wait_ge(max_done, NST * (n + 1))
                if n >= 1:
                    dve.wait_ge(mp_done, 3 * n)
                nc.vector.transpose(mT[:], mx[:, n % 2, :]).then_inc(mt_done, 1)
                dve.wait_ge(mt_done, n + 1)
                if n >= 1:
                    dve.wait_ge(mp_out, 64 * n)
                nc.vector.tensor_scalar(mpt[:, 0, :], mT[:], -1.0, None, ALU.mult).then_inc(mp_done, 1)
                dve.wait_ge(mp_done, 3 * n + 1)
                nc.vector.scalar_tensor_tensor(mres[:, 0, :], mT[:], -1.0, mpt[:, 0, :], ALU.mult,
                                               ALU.subtract).then_inc(mres_done, 1)
                dve.wait_ge(mres_done, n + 1)
                nc.vector.tensor_copy(mpt[:, 1, :], mres[:, 0, :]).then_inc(mp_done, 1)
                dve.wait_ge(mp_done, 3 * n + 2)
                nc.vector.tensor_tensor(mpt[:, 2, :], mres[:, 0, :], mpt[:, 1, :], ALU.subtract).then_inc(mp_done, 1)

            def look_up(k):
                c, v = divmod(k, LUT)
                cols = slice(c * PIECE, (c + 1) * PIECE)
                if k == 0:
                    dve.wait_ge(lut_in, 16)
                    dve.wait_ge(idx_in, 32)
                slot = c * (LUT - 1) + v - 1
                if v >= 1 and slot >= 3:
                    dve.wait_ge(lut_add, slot - 2)
                nc.vector.tensor_scalar(wsum[:, cols] if v == 0 else wtmp[:, slot % 3, :], idx[:, cols], float(v),
                                        lut[:, v:v + 1], ALU.is_equal, ALU.mult).then_inc(lut_prod, 1)

            def take_o(n):
                dve.wait_ge(pv_done, NTT * NJ * (n + 1))
                if n >= 2:
                    dve.wait_ge(o_out, 16 * NJ * (n - 1))
                    dve.wait_ge(den_out, 16 * NJ * (n - 1))
                nc.vector.tensor_copy(osb[:, n % 2, :], OB[:]).then_inc(o_done, 1)

            def invert(n):
                dve.wait_ge(den_in, 16 * (n + 1))
                if n >= 1:
                    dve.wait_ge(rden_out, 16 * n)
                nc.vector.reciprocal(rden[:], den[:]).then_inc(rden_ready, 1)

            for i in range(NST):
                row_max(0, i)
            max_parts(0)
            for n in range(NG):
                for i in range(NST):
                    if i == 2 and n >= 1:
                        take_o(n - 1)
                    if n + 1 < NG:
                        row_max(n + 1, i)
                    if i == 11 and n >= 1:
                        invert(n - 1)
                    if i % 3 == 1 and 5 * n + i // 3 < LUT * NPIECE:
                        look_up(5 * n + i // 3)
                if n + 1 < NG:
                    max_parts(n + 1)
            take_o(NG - 1)
            invert(NG - 1)

        @block.tensor
        def _(pe):
            pe.wait_ge(ones_ready, 3)

            def maxima(n, i):
                k = n * NST + i
                if i == 0:
                    pe.wait_ge(qk_in[n % 3], 16 * 4 * len(SLOTS) * (n // 3 + 1))
                if k >= 2:
                    pe.wait_ge(max_done, k - 1)
                for h in range(2):
                    mm = nc.tensor.matmul(MX[k % 2][h][:], QS[n % 3][0:NROW, i * P:(i + 1) * P],
                                          KS[n % 3][0:NROW, h * BLK:(h + 1) * BLK], start=True, stop=True)
                mm.then_inc(max_ps, 1)

            def scores(n, t, j):
                k = (n * NTT + t) * NJ + j
                if t == 0 and j == 0:
                    pe.wait_ge(m_in, 16 * (n + 1))
                if k >= 3:
                    pe.wait_ge(p_ready, k - 2)
                nc.tensor.matmul(ring(k)[:], KS[n % 3][:, t * P:(t + 1) * P], QS[n % 3][:, j * BLK:(j + 1) * BLK],
                                 start=True, stop=True).then_inc(s_ps, 1)

            def weigh(n, t):
                bb, kv = divmod(n, KV)
                for j in range(NJ):
                    k = (n * NTT + t) * NJ + j
                    pe.wait_ge(p_ready, k + 1)
                    if t == 0 and j == 0 and n >= 1:
                        pe.wait_ge(o_done, n)
                    nc.tensor.matmul(OB[32 * j:32 * (j + 1), :], m.VS[:, bb * NTT + t, kv, :], pt[:, k % NPT, :],
                                     start=(t == 0), stop=(t == NTT - 1)).then_inc(pv_done, 1)

            for i in range(NST):
                maxima(0, i)
            for n in range(NG):
                for t in range(NTT):
                    scores(n, t, 0)
                    if n + 1 < NG:
                        maxima(n + 1, 2 * t)
                    scores(n, t, 1)
                    scores(n, t, 2)
                    if t >= 1:
                        weigh(n, t - 1)
                    elif n >= 1:
                        weigh(n - 1, NTT - 1)
                    scores(n, t, 3)
                    if n + 1 < NG:
                        maxima(n + 1, 2 * t + 1)
            weigh(NG - 1, NTT - 1)




def ffn_stage(nc, m, a):
    at, sem, bank = m.at, m.sem, m.bank
    b = m.l0
    ch = at("ctx_h", [P, KC, T], F32R, b); b += KC * T * 4
    cl = at("ctx_l", [P, KC, T], F32R, b); b += KC * T * 4
    sg = at("f_silu", [P, 2, BLK], F32, b); b += 2 * BLK * 4
    hf = at("f_h", [P, 2, BLK], F32, b); b += 2 * BLK * 4
    hh = at("f_hh", [P, 3, BLK], F32R, b); b += 3 * BLK * 4
    hl = at("f_hl", [P, 3, BLK], F32R, b); b += 3 * BLK * 4
    gate = at("f_gate", [P, TPB, E], F32, b); b += TPB * E * 4
    assert b <= m.after_ctx - KC * T * 4
    b = m.after_ctx
    gs = at("f_gs", [P, TPB, E], F32, b); b += TPB * E * 4
    ctx_hi, ctx_lo, gu_ps, silu_done, h_done, hi_done, lo_done, down_done, s_done = (
        sem(n) for n in ("ctx_hi", "ctx_lo", "gu_ps", "f_silu_done", "h_done", "hi_done", "lo_done", "down_done", "s_done"))
    gate_done, gs_done, x_done = sem("gate_done"), sem("gs_done"), sem("x_done")
    NQ = NI + 1
    fh = m.fh[:, 0:KC * 2 * INTER].rearrange("p (c n) -> p c n", c=KC)
    fl = m.fl[:, 0:KC * 2 * INTER].rearrange("p (c n) -> p c n", c=KC)
    dh = m.fh[:, KC * 2 * INTER:].rearrange("p (c n) -> p c n", c=NI)
    dl = m.fl[:, KC * 2 * INTER:].rearrange("p (c n) -> p c n", c=NI)
    pieces = parts(INTER, P)

    with nc.Block() as block:
        @block.scalar
        def _(act):
            for tb in range(NB):
                cols = slice(tb * BLK, (tb + 1) * BLK)
                nc.scalar.activation(ch[:, :, cols], m.ctxT[:, :, cols], ACT.Copy).then_inc(ctx_hi, 1)
                for c, (i0, n) in enumerate(pieces):
                    k = tb * NI + c
                    act.wait_ge(gu_ps, k + 1)
                    if k >= 2:
                        act.wait_ge(h_done, k - 1)
                    nc.scalar.activation(sg[0:n, k % 2, :], bank[(tb * NQ + c) % 2 * 2][0:n, :],
                                         ACT.Silu).then_inc(silu_done, 1)
                    act.wait_ge(h_done, k + 1)
                    if k >= 3:
                        act.wait_ge(down_done, k - 2)
                    nc.scalar.activation(hh[0:n, k % 3, :], hf[0:n, k % 2, :], ACT.Copy).then_inc(hi_done, 1)
                act.wait_ge(down_done, (tb + 1) * NI)
                if tb >= 1:
                    act.wait_ge(gs_done, tb)
                nc.scalar.activation(gate[:], m.psum[:, 4:8, 0:E], ACT.Silu).then_inc(gate_done, 1)

        @block.vector
        def _(dve):
            for tb in range(NB):
                cols = slice(tb * BLK, (tb + 1) * BLK)
                dve.wait_ge(ctx_hi, tb + 1)
                nc.vector.tensor_tensor(cl[:, :, cols], m.ctxT[:, :, cols], ch[:, :, cols],
                                        ALU.subtract).then_inc(ctx_lo, 1)
                for c, (i0, n) in enumerate(pieces):
                    k = tb * NI + c
                    dve.wait_ge(silu_done, k + 1)
                    if k >= 2:
                        dve.wait_ge(lo_done, k - 1)
                        dve.wait_ge(hi_done, k - 1)
                    nc.vector.tensor_tensor(hf[0:n, k % 2, :], bank[(tb * NQ + c) % 2 * 2 + 1][0:n, :],
                                            sg[0:n, k % 2, :], ALU.mult).then_inc(h_done, 1)
                    dve.wait_ge(hi_done, k + 1)
                    nc.vector.tensor_tensor(hl[0:n, k % 3, :], hf[0:n, k % 2, :], hh[0:n, k % 3, :],
                                            ALU.subtract).then_inc(lo_done, 1)
                dve.wait_ge(gate_done, tb + 1)
                dve.wait_ge(s_done, tb + 1)
                if tb >= 1:
                    dve.wait_ge(x_done, tb)
                slot = (tb * NQ + NI) % 2 * 2
                nc.vector.tensor_tensor(gs[:], m.psum[:, slot:slot + 2, :].rearrange("p b (n e) -> p (b n) e", e=E),
                                        gate[:], ALU.mult).then_inc(gs_done, 1)
                xt = m.x[:, tb * TPB:(tb + 1) * TPB, :]
                dve.wait_ge(gs_done, tb + 1)
                nc.vector.tensor_tensor(xt, xt, gs[:], ALU.add).then_inc(x_done, 1)

        @block.tensor
        def _(pe):
            def slot_free(tb, c):
                q = tb * NQ + c - 2
                if q >= 0:
                    t0, c0 = divmod(q, NQ)
                    if c0 < NI:
                        pe.wait_ge(h_done, t0 * NI + c0 + 1)
                    else:
                        pe.wait_ge(gs_done, t0 + 1)
                return (q + 2) % 2 * 2

            def up(tb, c):
                i0, n = pieces[c]
                cols = slice(tb * BLK, (tb + 1) * BLK)
                s = slot_free(tb, c)
                for w in range(2):
                    i = w * INTER + i0
                    mm = three(nc, bank[s + w][0:n, :], [(fh[:, kc, i:i + n], fl[:, kc, i:i + n],
                                                          m.xTh[:, kc, cols], m.xTl[:, kc, cols]) for kc in range(KC)])
                mm.then_inc(gu_ps, 1)

            def down(tb, c):
                i0, n = pieces[c]
                k = tb * NI + c
                pe.wait_ge(lo_done, k + 1)
                if c == 0 and tb >= 1:
                    pe.wait_ge(gate_done, tb)
                for i in range(TPB):
                    tok = slice(i * P, (i + 1) * P)
                    mm = three(nc, bank[4 + i][:, 0:E], [(hh[0:n, k % 3, tok], hl[0:n, k % 3, tok],
                                                          dh[0:n, c, :], dl[0:n, c, :])],
                               start=(c == 0), stop=(c == NI - 1))
                mm.then_inc(down_done, 1)

            def attn_out(tb):
                pe.wait_ge(ctx_lo, tb + 1)
                s = slot_free(tb, NI)
                for i in range(TPB):
                    tok = slice(tb * BLK + i * P, tb * BLK + (i + 1) * P)
                    mm = three(nc, bank[s + i // 2][:, i % 2 * E:(i % 2 + 1) * E],
                               [(ch[:, kc, tok], cl[:, kc, tok], m.woh[:, kc, :], m.wol[:, kc, :])
                                for kc in range(KC)])
                mm.then_inc(s_done, 1)

            for tb in range(NB):
                for c in range(NI):
                    up(tb, c)
                    if c >= 1:
                        down(tb, c - 1)
                attn_out(tb)
                down(tb, NI - 1)


LH, LD = 4, 64
NCH = 2 * B
CH = 128
NC = S // CH
SMALL = 5
QB = 32


def time_mix_in_stage(nc, m, a):
    at, sem, bank = m.at, m.sem, m.bank
    b = m.base
    m.D = at("decay", [P, KC, T], F32, b); b += KC * T * 4
    m.K = at("key", [P, KC, T], F32, b); b += KC * T * 4
    m.R = at("recept", [P, KC, T], F32, b); b += KC * T * 4
    m.V = at("value", [P, NT, E], F32, b); b += NT * E * 4
    m.woh1 = at("wout_h", [P, KC, E], F32R, b); b += KC * E * 4
    m.wol1 = at("wout_l", [P, KC, E], F32R, b); b += KC * E * 4
    m.mv1 = at("mv1", [P, NT, 2], F32, b); b += NT * 8
    m.rstd1 = at("rstd1", [P, NT], F32, b); b += NT * 4
    m.ident1 = at("ident1", [P, P], F32, b); b += P * 4
    m.mhalf1 = at("minus_half1", [P, TPB], F32, b); b += 32
    m.p3 = b
    yh = at("y_h", [P, KC, T], F32R, b); b += KC * T * 4
    yl = at("y_l", [P, KC, T], F32R, b); b += KC * T * 4
    raw = at("w1_raw", [P, 6, KC, E], F32, b); b += 6 * KC * E * 4
    wh = at("w1_h", [P, 4, KC, E], F32R, b); b += 4 * KC * E * 4
    wl = at("w1_l", [P, 4, KC, E], F32R, b); b += 4 * KC * E * 4
    xa = at("x_norm", [P, 2, TPB, E], F32, b); b += 2 * TPB * E * 4
    xb = at("x_norm2", [P, 2, TPB, E], F32, b); b += 2 * TPB * E * 4
    yf = at("y_f", [P, 2, KC, BLK], F32, b); b += 2 * KC * BLK * 4
    cols3 = at("cols3", [P, 3, KC], F32, b); b += 32
    nbw = at("nbw", [P, KC], F32, b); b += 32
    st = at("bn_st1", [P, 2, NT, 6], F32, b); b += 2 * NT * 24
    ve = at("var_eps1", [P, 2, NT], F32, b); b += 2 * NT * 4
    mv2 = at("mv2", [P, NT, 2], F32, b); b += NT * 8
    rstd2 = at("rstd2", [P, NT], F32, b); b += NT * 4
    assert b <= nc.sbuf_usable_end, b
    names = ("t_w_in", "t_c_in", "t_const", "t_stats", "t_var", "t_rstd", "t_xa", "t_xb", "t_ps", "t_yf", "t_yh",
             "t_yl", "wc_ps", "t_wh", "t_wl", "t_nbw", "pr_ps", "act_out", "dve_out")
    (w_in, c_in, const, stats, var, rstd, xa_ready, xb_ready, t_ps, yf_ready, yh_ready, yl_ready, wc_ps, wh_ready,
     wl_ready, nbw_ready, pr_ps, act_out, dve_out) = (sem(n) for n in names)

    ITEMS = [("w", 0), ("k", 0), ("r", 0), ("w", 1), ("k", 1), ("r", 1), ("v", 0), ("v", 1)]
    NIT = len(ITEMS)

    def taken_by(kind):
        return "act" if kind in "wr" else "dve"

    def order(k):
        who = taken_by(ITEMS[k % NIT][0])
        per = sum(taken_by(x[0]) == who for x in ITEMS)
        return k // NIT * per + sum(taken_by(x[0]) == who for x in ITEMS[:k % NIT + 1])

    def rbank(k):
        return bank[2 + k % 6]

    def take(eng, k, tb):
        kind, i = ITEMS[k % NIT]
        cols = slice(tb * BLK, (tb + 1) * BLK)
        eng.wait_ge(pr_ps, k + 1)
        if kind == "w":
            nc.scalar.activation(m.D[:, i, cols], rbank(k), ACT.Sigmoid, bias=nbw[:, i:i + 1],
                                 scale=-1.0).then_inc(act_out, 1)
        elif kind == "r":
            nc.scalar.activation(m.R[:, i, cols], rbank(k), ACT.Sigmoid).then_inc(act_out, 1)
        elif kind == "k":
            nc.vector.tensor_copy(m.K[:, i, cols], rbank(k)).then_inc(dve_out, 1)
        else:
            n = tb * TPB + 2 * i
            nc.vector.tensor_copy(m.V[:, n:n + 2, :], rbank(k).rearrange("p (n e) -> p n e", n=2)).then_inc(dve_out, 1)

    with nc.Block() as block:
        @block.sync
        def _(sp):
            for j, n in enumerate(("wx_t", "ww", "wk", "wr", "wv", "wout")):
                sp.dma_start(raw[:, j, :, :], a[n].rearrange("(c p) n -> p c n", p=P)).then_inc(w_in, 16)
            sp.dma_start(m.ident1[:], a["ident"]).then_inc(c_in, 16)
            for j, n in enumerate(("gamma", "beta", "bw")):
                sp.dma_start(cols3[:, j, :], a[n]).then_inc(c_in, 16)

        @block.gpsimd
        def _(pool):
            nc.gpsimd.memset(m.mhalf1[:], -0.5).then_inc(const, 1)
            pool.wait_ge(const, 1)
            for g in range(NB):
                ts = slice(g * TPB, (g + 1) * TPB)
                for i in range(2):
                    pool.wait_ge(var, 2 * g + i + 1)
                    nc.gpsimd.tensor_tensor((m.rstd1 if i == 0 else rstd2)[:, ts], ve[:, i, ts], m.mhalf1[:],
                                            ALU.pow).then_inc(rstd, 1)

        @block.scalar
        def _(act):
            act.wait_ge(w_in, 16 * 6)
            nc.scalar.activation(wh[:, 1:4, :, :], raw[:, 2:5, :, :], ACT.Copy).then_inc(wh_ready, 1)
            nc.scalar.activation(m.woh1[:], raw[:, 5, :, :], ACT.Copy).then_inc(wh_ready, 1)
            act.wait_ge(wc_ps, 2)
            nc.scalar.activation(wh[:, 0, :, :], m.psum[:, 6:8, 0:E], ACT.Copy).then_inc(wh_ready, 1)
            act.wait_ge(c_in, 64)
            act.wait_ge(nbw_ready, 1)

            def turn_out(g):
                for kc in range(KC):
                    act.wait_ge(t_ps, g * KC + kc + 1)
                    if g >= 2:
                        act.wait_ge(yl_ready, g - 1)
                    nc.scalar.activation(yf[:, g % 2, kc, :], bank[kc], ACT.Identity, bias=cols3[:, 1, kc:kc + 1],
                                         scale=cols3[:, 0, kc:kc + 1]).then_inc(yf_ready, 1)
                act.wait_ge(yf_ready, KC * (g + 1))
                nc.scalar.activation(yh[:, :, g * BLK:(g + 1) * BLK], yf[:, g % 2, :, :], ACT.Copy).then_inc(yh_ready, 1)

            turn_out(0)
            for g in range(NB):
                if g + 1 < NB:
                    turn_out(g + 1)
                for i in range(NIT):
                    if taken_by(ITEMS[i][0]) == "act":
                        take(act, g * NIT + i, g)

        @block.vector
        def _(dve):
            dve.wait_ge(c_in, 64)
            nc.vector.tensor_scalar(nbw[:], cols3[:, 2, :], -1.0, None, ALU.mult).then_inc(nbw_ready, 1)
            dve.wait_ge(wh_ready, 2)
            nc.vector.tensor_tensor(wl[:, 1:4, :, :], raw[:, 2:5, :, :], wh[:, 1:4, :, :], ALU.subtract).then_inc(wl_ready, 1)
            nc.vector.tensor_tensor(m.wol1[:], raw[:, 5, :, :], m.woh1[:], ALU.subtract).then_inc(wl_ready, 1)
            dve.wait_ge(wh_ready, 3)
            nc.vector.tensor_tensor(wl[:, 0, :, :], m.psum[:, 6:8, 0:E], wh[:, 0, :, :], ALU.subtract).then_inc(wl_ready, 1)

            def norm(g):
                ts = slice(g * TPB, (g + 1) * TPB)
                for i, (src, mv, rs, dst, ready) in enumerate(((m.x[:, ts, :], m.mv1, m.rstd1, xa, xa_ready),
                                                               (xa[:, g % 2, :, :], mv2, rstd2, xb, xb_ready))):
                    done = (2 * g + i) * 2 * TPB
                    if i == 1:
                        dve.wait_ge(xa_ready, TPB * (g + 1))
                    for j in range(TPB):
                        nc.vector.bn_stats(st[:, i, g * TPB + j, :], src[:, j, :]).then_inc(stats, 1)
                    dve.wait_ge(stats, done + TPB)
                    for j in range(TPB):
                        nc.vector.bn_aggr(mv[:, g * TPB + j, :], st[:, i, g * TPB + j, :]).then_inc(stats, 1)
                    dve.wait_ge(stats, done + 2 * TPB)
                    nc.vector.tensor_scalar(ve[:, i, ts], mv[:, ts, 1], EPS, None, ALU.add).then_inc(var, 1)
                    dve.wait_ge(rstd, 2 * g + i + 1)
                    if i == 1 and g >= 2:
                        dve.wait_ge(t_ps, KC * (g - 1))
                    if i == 0 and g >= 2:
                        dve.wait_ge(xb_ready, TPB * (g - 1))
                    for j in range(TPB):
                        n = g * TPB + j
                        nc.vector.tensor_scalar(dst[:, g % 2, j, :], src[:, j, :], mv[:, n, 0:1], rs[:, n:n + 1],
                                                ALU.subtract, ALU.mult).then_inc(ready, 1)

            def low(g):
                dve.wait_ge(yh_ready, g + 1)
                cols = slice(g * BLK, (g + 1) * BLK)
                nc.vector.tensor_tensor(yl[:, :, cols], yf[:, g % 2, :, :], yh[:, :, cols],
                                        ALU.subtract).then_inc(yl_ready, 1)
            norm(0)
            norm(1)
            low(0)
            for g in range(NB):
                if g + 2 < NB:
                    norm(g + 2)
                if g + 1 < NB:
                    low(g + 1)
                for i in range(NIT):
                    if taken_by(ITEMS[i][0]) == "dve":
                        take(dve, g * NIT + i, g)

        @block.tensor
        def _(pe):
            pe.wait_ge(w_in, 16 * 6)
            for i in range(KC):
                for mc in range(KC):
                    mm = nc.tensor.matmul(bank[6 + i][:, 0:E], raw[:, 0, mc, i * P:(i + 1) * P], raw[:, 1, mc, :],
                                          start=(mc == 0), stop=(mc == KC - 1))
                mm.then_inc(wc_ps, 1)

            def turn(g):
                if g == 0:
                    pe.wait_ge(c_in, 64)
                pe.wait_ge(xb_ready, TPB * (g + 1))
                for kc in range(KC):
                    if g >= 1:
                        pe.wait_ge(yf_ready, (g - 1) * KC + kc + 1)
                    for i in range(TPB):
                        mm = nc.tensor.transpose(bank[kc][:, i * P:(i + 1) * P], xb[:, g % 2, i, kc * P:(kc + 1) * P],
                                                 m.ident1[:])
                    mm.then_inc(t_ps, 1)

            def project(g):
                cols = slice(g * BLK, (g + 1) * BLK)
                pe.wait_ge(yl_ready, g + 1)
                if g == 0:
                    pe.wait_ge(wl_ready, 3)
                for i, (kind, c) in enumerate(ITEMS):
                    k = g * NIT + i
                    if k >= 6:
                        pe.wait_ge(act_out if taken_by(ITEMS[(k - 6) % NIT][0]) == "act" else dve_out, order(k - 6))
                    if kind == "v":
                        for j in range(2):
                            tok = slice(g * BLK + (2 * c + j) * P, g * BLK + (2 * c + j + 1) * P)
                            mm = three(nc, rbank(k)[:, j * E:(j + 1) * E],
                                       [(yh[:, kc, tok], yl[:, kc, tok], wh[:, 3, kc, :], wl[:, 3, kc, :])
                                        for kc in range(KC)])
                    else:
                        w = "wkr".index(kind)
                        ch = slice(c * P, (c + 1) * P)
                        mm = three(nc, rbank(k), [(wh[:, w, kc, ch], wl[:, w, kc, ch], yh[:, kc, cols], yl[:, kc, cols])
                                                  for kc in range(KC)])
                    mm.then_inc(pr_ps, 1)

            turn(0)
            turn(1)
            for g in range(NB):
                project(g)
                if g + 2 < NB:
                    turn(g + 2)


def time_mix_stage(nc, m, a):
    at, sem, bank = m.at, m.sem, m.bank
    NH = 2
    NS = NC * NH
    b = m.p3
    A = [at(f"A{g}", [P, NS, CH], F32, b + g * NS * CH * 4) for g in range(NCH)]; b += NCH * NS * CH * 4
    AD = [at(f"AD{g}", [P, NS, QB], F32, b + g * NS * QB * 4) for g in range(NCH)]; b += NCH * NS * QB * 4
    TOT = {1: None}
    for s in (2, 4, 8, 16, 32, 64, 128):
        TOT[s] = at(f"tot{s}", [P, NCH, S // s], F32, b); b += NCH * (S // s) * 4
    kT = [at(f"kT{i}", [P, NC, P], F32, b + i * NC * P * 4) for i in range(2)]; b += 2 * NC * P * 4
    ST = [at(f"state{i}", [P, NC, LD], F32, b + i * NC * LD * 4) for i in range(2)]; b += 2 * NC * LD * 4
    yl = at("ty_l", [P, KC, T], F32R, b); b += KC * T * 4
    masks = at("masks", [P, SMALL + 1, QB], I32, b); b += (SMALL + 1) * QB * 4
    diag = at("diag", [P, QB], F32, b); b += QB * 4
    assert b <= nc.sbuf_usable_end, b
    yh = at("ty_h", [P, KC, T], F32R, m.base)
    m.s = at("s_tok", [P, NT, E], F32, m.base + KC * T * 4)
    names = ("mask_in", "a_zero", "tot_done", "lev_ps", "lev_take", "r_done", "k_done", "ad_put", "kt_ps", "kt_done",
             "u_ps", "st_done", "ty_ps", "tyh_done", "tyl_done", "so_ps", "so_done")
    (mask_in, a_zero, tot_done, lev_ps, lev_take, r_done, k_done, ad_put, kt_ps, kt_done, u_ps, st_done, ty_ps,
     tyh_done, tyl_done, so_ps, so_done) = (sem(n) for n in names)
    HALVES = [1, 2, 4, 8, 16, 32, 64]
    NL = 1 + len(HALVES)

    def group(t, g):
        ct, bb = divmod(g, B)
        return t[:, ct, bb * S:(bb + 1) * S]

    def tot(s, g):
        return group(m.D, g) if s == 1 else TOT[s][:, g, :]

    def lbanks(l, g):
        j = (l * NCH + g) % 4 * 2
        return m.psum[:, j:j + 2, :].rearrange("p b (n q) -> p (b n) q", q=2 * QB)

    with nc.Block() as block:
        @block.sync
        def _(sp):
            sp.dma_start(masks[:], a["masks"]).then_inc(mask_in, 16)
            sp.dma_start(diag[:], a["diag"]).then_inc(mask_in, 16)

        @block.gpsimd
        def _(pool):
            n = 0
            for s in (1, 2, 4, 8, 16, 32, 64):
                for g in range(NCH):
                    v = tot(s, g).rearrange("p (n two) -> p n two", two=2)
                    if s > 1:
                        pool.wait_ge(tot_done, n - NCH + 1)
                    nc.gpsimd.tensor_tensor(TOT[2 * s][:, g, :], v[:, :, 0], v[:, :, 1], ALU.mult).then_inc(tot_done, 1)
                    n += 1
                if s == 1:
                    for g in range(NCH):
                        nc.gpsimd.memset(A[g][:], 0.0).then_inc(a_zero, 1)
                for g in range(NCH):
                    k = group(m.K, g).rearrange("p (n two s) -> p n two s", two=2, s=s)
                    t = tot(s, g).rearrange("p (n two) -> p n two", two=2)
                    l = HALVES.index(s) + 1
                    pool.wait_ge(lev_ps, l * NCH + g + 1)
                    if l >= 2:
                        pool.wait_ge(k_done, (l - 2) * NCH + g + 1)
                    nc.gpsimd.tensor_tensor(k[:, :, 0, :], k[:, :, 0, :],
                                            t[:, :, 1].unsqueeze(2).broadcast_to([P, S // (2 * s), s]),
                                            ALU.mult).then_inc(k_done, 1)

        def take_y(act, g):
            act.wait_ge(ty_ps, g + 1)
            ct, bb = divmod(g, B)
            nc.scalar.activation(yh[:, ct, bb * S:(bb + 1) * S], m.psum[:, 2 * (g % 2):2 * (g % 2) + 2, :]
                                 .rearrange("p b c -> p (b c)"), ACT.Copy).then_inc(tyh_done, 1)



        @block.scalar
        def _(act):
            for g in range(NCH):
                act.wait_ge(a_zero, g + 1)
                act.wait_ge(lev_take, SMALL * NCH + g + 1)
                for q in range(4):
                    r = slice(QB * q, QB * (q + 1))
                    nc.scalar.activation(A[g][r, :, r], AD[g][r, :, :], ACT.Copy).then_inc(ad_put, 1)
            for g in range(NCH):
                act.wait_ge(kt_ps, g + 1)
                if g >= 2:
                    act.wait_ge(u_ps, g - 1)
                nc.scalar.activation(kT[g % 2][:], m.psum[:, 4:6, :].rearrange("p b (n c) -> p (b n) c", c=P),
                                     ACT.Copy).then_inc(kt_done, 1)
                if g >= 1:
                    take_y(act, g - 1)
            take_y(act, NCH - 1)

        def low_y(dve, g):
            dve.wait_ge(tyh_done, g + 1)
            ct, bb = divmod(g, B)
            v = slice(bb * S, (bb + 1) * S)
            nc.vector.tensor_tensor(yl[:, ct, v], m.psum[:, 2 * (g % 2):2 * (g % 2) + 2, :].rearrange("p b c -> p (b c)"),
                                    yh[:, ct, v], ALU.subtract).then_inc(tyl_done, 1)


        @block.vector
        def _(dve):
            dve.wait_ge(mask_in, 32)

            def take_level(l, g):
                k = l * NCH + g
                dve.wait_ge(lev_ps, k + 1)
                ps = lbanks(l, g)
                if l == 0:
                    nc.vector.tensor_tensor(AD[g][:], ps[:, :, 0:QB], diag[:].unsqueeze(1).broadcast_to([P, NS, QB]),
                                            ALU.mult).then_inc(lev_take, 1)
                elif l <= SMALL:
                    dve.wait_ge(lev_take, k - NCH + 1)
                    nc.vector.copy_predicated(AD[g][:], masks[:, l, :].unsqueeze(1).broadcast_to([P, NS, QB]),
                                              ps[:, :, 0:QB]).then_inc(lev_take, 1)
                elif l == SMALL + 1:
                    dve.wait_ge(a_zero, g + 1)
                    nc.vector.tensor_copy(A[g][0:QB, :, QB:2 * QB], ps[0:QB, :, 0:QB])
                    nc.vector.tensor_copy(A[g][2 * QB:3 * QB, :, 3 * QB:], ps[2 * QB:3 * QB, :, 0:QB]
                                          ).then_inc(lev_take, 1)
                else:
                    nc.vector.tensor_copy(A[g][0:2 * QB, :, 2 * QB:], ps[0:2 * QB]).then_inc(lev_take, 1)

            def scale_r(l, g):
                dve.wait_ge(lev_ps, l * NCH + g + 1)
                if l >= 1:
                    dve.wait_ge(r_done, (l - 1) * NCH + g + 1)
                r = group(m.R, g)
                if l == 0:
                    nc.vector.tensor_tensor(r, r, group(m.D, g), ALU.mult).then_inc(r_done, 1)
                    return
                s = HALVES[l - 1]
                if s > 1:
                    dve.wait_ge(tot_done, (l - 2) * NCH + g + 1)
                v = r.rearrange("p (n two s) -> p n two s", two=2, s=s)
                t = tot(s, g).rearrange("p (n two) -> p n two", two=2)
                nc.vector.tensor_tensor(v[:, :, 1, :], v[:, :, 1, :],
                                        t[:, :, 0].unsqueeze(2).broadcast_to([P, S // (2 * s), s]),
                                        ALU.mult).then_inc(r_done, 1)

            for l in range(NL):
                for g in range(NCH):
                    scale_r(l, g)
                    take_level(l, g)
            done = 0
            for g in range(NCH):
                dve.wait_ge(u_ps, g + 1)
                u = bank[6 + g % 2]
                if g >= 2:
                    dve.wait_ge(ty_ps, g - 1)
                if g == 0:
                    dve.wait_ge(tot_done, NCH * len(HALVES))
                nc.vector.tensor_copy(ST[g % 2][:, 1, :], u[:, 0:LD]).then_inc(st_done, 1)
                for c in range(1, NC - 1):
                    dve.wait_ge(st_done, g * (NC - 1) + c)
                    nc.vector.scalar_tensor_tensor(ST[g % 2][:, c + 1, :], ST[g % 2][:, c, :], TOT[128][:, g, c:c + 1],
                                                   u[:, c * LD:(c + 1) * LD], ALU.mult, ALU.add).then_inc(st_done, 1)
                if g >= 1:
                    low_y(dve, g - 1)
            low_y(dve, NCH - 1)
            for n in range(0, NT, 2):
                dve.wait_ge(so_ps, n // 2 + 1)
                nc.vector.tensor_copy(m.s[:, n:n + 2, :], bank[4 + n // 2 % 4].rearrange("p (n e) -> p n e", n=2)
                                      ).then_inc(so_done, 1)

        @block.tensor
        def _(pe):
            def level(l, g):
                k = l * NCH + g
                if k >= 4:
                    pe.wait_ge(lev_take, k - 3)
                if l >= 1:
                    pe.wait_ge(r_done, (l - 1) * NCH + g + 1)
                if l >= 2:
                    pe.wait_ge(k_done, (l - 2) * NCH + g + 1)
                kk, rr, ps = group(m.K, g), group(m.R, g), lbanks(l, g)
                for n in range(NS):
                    h, c = divmod(n, NC)
                    ch = slice(h * LD, (h + 1) * LD)
                    if l <= SMALL:
                        for q in range(4):
                            t = c * CH + q * QB
                            mm = nc.tensor.matmul(ps[QB * q:QB * (q + 1), n, 0:QB], kk[ch, t:t + QB],
                                                  rr[ch, t:t + QB], start=True, stop=True)
                    elif l == SMALL + 1:
                        for q in (0, 2):
                            t = c * CH + q * QB
                            mm = nc.tensor.matmul(ps[QB * q:QB * (q + 1), n, 0:QB], kk[ch, t:t + QB],
                                                  rr[ch, t + QB:t + 2 * QB], start=True, stop=True)
                    else:
                        t = c * CH
                        mm = nc.tensor.matmul(ps[0:2 * QB, n, :],
                                              kk[ch, t:t + 2 * QB], rr[ch, t + 2 * QB:t + CH], start=True, stop=True)
                mm.then_inc(lev_ps, 1)

            def turn_k(g):
                pe.wait_ge(k_done, (NL - 2) * NCH + g + 1)
                if g == 0:
                    pe.wait_ge(lev_take, NL * NCH)
                if g >= 1:
                    pe.wait_ge(kt_done, g)
                for c in range(NC):
                    mm = nc.tensor.transpose(bank[4 + c // 4][:, c % 4 * P:(c % 4 + 1) * P],
                                             group(m.K, g)[:, c * CH:(c + 1) * CH], m.ident1[:])
                mm.then_inc(kt_ps, 1)

            def update(g):
                ct, bb = divmod(g, B)
                pe.wait_ge(kt_done, g + 1)
                if g >= 2:
                    pe.wait_ge(st_done, (g - 1) * (NC - 1))
                for c in range(NC - 1):
                    for h in range(NH):
                        ch = slice(h * LD, (h + 1) * LD)
                        mm = nc.tensor.matmul(bank[6 + g % 2][ch, c * LD:(c + 1) * LD], kT[g % 2][:, c, ch],
                                              m.V[:, bb * NC + c, ct * P + h * LD:ct * P + (h + 1) * LD],
                                              start=True, stop=True)
                mm.then_inc(u_ps, 1)

            def output(g):
                ct, bb = divmod(g, B)
                pe.wait_ge(st_done, (g + 1) * (NC - 1))
                pe.wait_ge(ad_put, 4 * (g + 1))
                pe.wait_ge(r_done, (NL - 1) * NCH + g + 1)
                if g >= 2:
                    pe.wait_ge(tyl_done, g - 1)
                for c in range(NC):
                    for h in range(NH):
                        ch = slice(h * LD, (h + 1) * LD)
                        out = m.psum[ch, 2 * (g % 2) + c // 4, c % 4 * CH:(c % 4 + 1) * CH]
                        mm = nc.tensor.matmul(out, m.V[:, bb * NC + c, ct * P + h * LD:ct * P + (h + 1) * LD],
                                              A[g][:, h * NC + c, :], start=True, stop=(c == 0))
                        if c:
                            mm = nc.tensor.matmul(out, ST[g % 2][ch, c, :], group(m.R, g)[ch, c * CH:(c + 1) * CH],
                                                  start=False, stop=True)
                mm.then_inc(ty_ps, 1)

            for l in range(NL):
                for g in range(NCH):
                    level(l, g)
            turn_k(0)
            for g in range(NCH):
                update(g)
                if g + 1 < NCH:
                    turn_k(g + 1)
                output(g)
            pe.wait_ge(tyl_done, NCH)
            for n in range(NT):
                if n >= 8 and n % 2 == 0:
                    pe.wait_ge(so_done, n // 2 - 3)
                tok = slice(n * P, (n + 1) * P)
                mm = three(nc, bank[4 + n // 2 % 4][:, n % 2 * E:(n % 2 + 1) * E],
                           [(yh[:, kc, tok], yl[:, kc, tok], m.woh1[:, kc, :], m.wol1[:, kc, :]) for kc in range(KC)])
                if n % 2:
                    mm.then_inc(so_ps, 1)


NE, EI, SI = 8, 176, 352
NEC = NE * EI // P
MI = NE * EI + SI
NMC = (MI + P - 1) // P


def experts_stage(nc, m, a):
    at, sem, bank = m.at, m.sem, m.bank
    b = m.base
    xl = at("x1_l", [P, KC, T], F32R, b); b += KC * T * 4
    b += NT * E * 4
    xh = at("x1_h", [P, KC, T], F32R, b); b += KC * T * 4
    b += NT * E * 4 - KC * T * 4
    m_end = m.p3
    b = m.base + 3 * KC * T * 4
    b = m_end
    NW = KC * 2 * MI + NMC * E
    raw = at("m_raw", [P, NW], F32, b)
    wl = at("m_l", [P, NW], F32R, b); b += NW * 4
    wh = at("m_h", [P, NW], F32R, b); b += NW * 4
    hh = at("m_hh", [P, 3, BLK], F32R, b); b += 3 * BLK * 4
    hl = at("m_hl", [P, 3, BLK], F32R, b); b += 3 * BLK * 4
    c0 = m.base + 3 * KC * T * 4
    xa = at("m_xa", [P, 2, TPB, E], F32, c0); c0 += 2 * TPB * E * 4
    comb = at("comb_b", [P, 4, BLK], F32, c0); c0 += 4 * BLK * 4
    gw = at("gate_w", [P, 3, KC, NE], F32, c0); c0 += 3 * KC * NE * 4
    gwh = at("gate_wh", [P, KC, NE], F32R, c0); c0 += KC * NE * 4
    gwl = at("gate_wl", [P, KC, NE], F32R, c0); c0 += KC * NE * 4
    rank = at("rank", [P, NE], F32, c0); c0 += NE * 4
    assert c0 <= m.base + 4 * KC * T * 4 + 4096, c0
    lg = at("logits", [NE, T], F32, b)
    combT = at("comb_t", [NE, T], F32, b); b += T * 4
    names = ("l", "e", "p", "q1", "s1", "q2", "s2", "sel")
    rt = {}
    for n in names:
        rt[n] = at("rt_" + n, [P, NT, NE], F32, b); b += NT * NE * 4
    r1 = at("rt_r", [P, 8, NT], F32, b); b += 8 * NT * 4
    sg = at("m_silu", [P, 2, BLK], F32, b); b += 2 * BLK * 4
    hf = at("m_h_f", [P, 3, BLK], F32, b); b += 3 * BLK * 4
    gate = at("m_gate", [P, TPB, E], F32, b); b += TPB * E * 4
    assert b <= nc.sbuf_usable_end, b
    gs = gate

    names = ("e_w_in", "e_g_in", "e_xa", "e_t_ps", "e_xh", "e_xl", "e_wh", "e_wl", "e_gw", "e_lg_ps", "e_lg",
             "e_lt_ps", "e_rt", "e_exp", "e_ct_ps", "e_ct", "e_crow", "e_gu_ps", "e_silu", "e_h", "e_hc",
             "e_hi", "e_lo", "e_down", "e_gate", "e_gs", "e_x", "e_out")
    (w_in, g_in, xa_ready, t_ps, xh_ready, xl_ready, wh_ready, wl_ready, gw_ready, lg_ps, lg_ready, lt_ps, rt_done,
     exp_done, ct_ps, ct_ready, crow_out, gu_ps, silu_done, h_done, hc_done, hi_done, lo_done, down_done,
     gate_done, gs_done, x_done, x_out) = (sem(n) for n in names)
    comb_in = [sem(f"comb_in{i}") for i in range(4)]
    comb_rows = nc.dram_tensor("comb_rows", (NE, T), F32, kind="Internal").ap()

    def wview(t, w):
        return t[:, w * KC * MI:(w + 1) * KC * MI].rearrange("p (c n) -> p c n", c=KC)

    def dview(t):
        return t[:, 2 * KC * MI:].rearrange("p (c n) -> p c n", c=NMC)

    ORDER = list(range(NEC, NMC)) + list(range(NEC))
    size = [min(P, MI - P * c) for c in range(NMC)]
    NSTEP = 22
    NX = sum(c < NEC for c in ORDER)

    def ncomb(k):
        return k // NMC * NX + sum(c < NEC for c in ORDER[:k % NMC + 1])

    with nc.Block() as block:
        def store(sp, tb):
            sp.wait_ge(x_done, tb + 1)
            ts = slice(tb * TPB, (tb + 1) * TPB)
            sp.dma_start(a["out"].rearrange("(n p) f -> p n f", p=P)[:, ts, :], m.x[:, ts, :]).then_inc(x_out, 16)


        @block.sync
        def _(sp):
            sp.dma_start(gw[:, 0, :, :], a["gate_w_t"].rearrange("(c p) n -> p c n", p=P)).then_inc(g_in, 16)
            sp.dma_start(rank[:], a["rank"]).then_inc(g_in, 16)
            for w, n in ((0, "gate"), (1, "up")):
                sp.dma_start(wview(raw, w)[:, :, NE * EI:], a["shared_" + n].rearrange("(c p) n -> p c n", p=P)
                             ).then_inc(w_in, 16)
                sp.dma_start(wview(raw, w)[:, :, 0:NE * EI], a["expert_" + n].rearrange("(c p) n -> p c n", p=P)
                             ).then_inc(w_in, 16)
            sp.dma_start(dview(raw)[:, 0:NEC, :], a["expert_down"].rearrange("(c p) n -> p c n", p=P)).then_inc(w_in, 16)
            sp.dma_start(dview(raw)[:, NEC:NMC, :], a["shared_down"].rearrange("(c p) n -> p c n", p=P)).then_inc(w_in, 16)
            sp.wait_ge(ct_ready, 1)
            sp.dma_start(comb_rows, combT[:]).then_inc(crow_out, 16)
            sp.wait_ge(crow_out, 16)
            for tb in range(NB):
                for c in range(NEC):
                    j = tb * NEC + c
                    if j >= 4:
                        sp.wait_ge(hc_done, j - 3)
                    lo = c * P
                    while lo < (c + 1) * P:
                        e = lo // EI
                        hi = min((c + 1) * P, (e + 1) * EI)
                        sp.dma_start(comb[lo - c * P:hi - c * P, j % 4, :],
                                     comb_rows[e:e + 1, tb * BLK:(tb + 1) * BLK].broadcast_to([hi - lo, BLK])
                                     ).then_inc(comb_in[j % 4], 16)
                        lo = hi
                if tb >= 1:
                    store(sp, tb - 1)
            store(sp, NB - 1)
            sp.wait_ge(x_out, 16 * NB)

        def pieces_in(j):
            def count(i):
                c = i % NEC
                return (c * P + P - 1) // EI - c * P // EI + 1
            return sum(count(i) for i in range(j % 4, j + 1, 4))

        @block.gpsimd
        def _(pool):
            for tb in range(NB):
                for c in ORDER:
                    if c >= NEC:
                        continue
                    j = tb * NEC + c
                    k = tb * NMC + ORDER.index(c)
                    pool.wait_ge(comb_in[j % 4], 16 * pieces_in(j))
                    pool.wait_ge(h_done, k + 1)
                    nc.gpsimd.tensor_tensor(hf[:, k % 3, :], hf[:, k % 3, :], comb[:, j % 4, :],
                                            ALU.mult).then_inc(hc_done, 1)

        def high(act, k):
            n = size[ORDER[k % NMC]]
            act.wait_ge(h_done, k + 1)
            if ORDER[k % NMC] < NEC:
                act.wait_ge(hc_done, ncomb(k))
            if k >= 3:
                act.wait_ge(down_done, k - 2)
            nc.scalar.activation(hh[0:n, k % 3, :], hf[0:n, k % 3, :], ACT.Copy).then_inc(hi_done, 1)


        @block.scalar
        def _(act):
            for g in range(NB):
                for kc in range(KC):
                    act.wait_ge(t_ps, g * KC + kc + 1)
                    nc.scalar.activation(xh[:, kc, g * BLK:(g + 1) * BLK], bank[kc], ACT.Copy).then_inc(xh_ready, 1)
            act.wait_ge(g_in, 32)
            nc.scalar.activation(gwh[:], gw[:, 0, :, :], ACT.Copy).then_inc(gw_ready, 1)
            for tb in range(NB):
                act.wait_ge(lg_ps, tb + 1)
                nc.scalar.activation(lg[:, tb * BLK:(tb + 1) * BLK], bank[2 + tb][0:NE, :], ACT.Copy).then_inc(lg_ready, 1)
            act.wait_ge(w_in, 96)
            nc.scalar.activation(wh[:], raw[:], ACT.Copy).then_inc(wh_ready, 1)
            act.wait_ge(rt_done, 2)
            nc.scalar.activation(rt["e"][:], rt["l"][:], ACT.Exp).then_inc(exp_done, 1)
            act.wait_ge(ct_ps, 1)
            nc.scalar.activation(combT[:], m.psum[0:NE, 4:8, :].rearrange("p b c -> p (b c)"), ACT.Copy
                                 ).then_inc(ct_ready, 1)
            for tb in range(NB):
                for i, c in enumerate(ORDER):
                    k, n = tb * NMC + i, size[c]
                    act.wait_ge(gu_ps, k + 1)
                    if k >= 2:
                        act.wait_ge(h_done, k - 1)
                    nc.scalar.activation(sg[0:n, k % 2, :], bank[k % 2 * 2][0:n, :], ACT.Silu).then_inc(silu_done, 1)
                    if i >= 1:
                        high(act, k - 1)
                high(act, tb * NMC + NMC - 1)
                act.wait_ge(down_done, (tb + 1) * NMC)
                if tb >= 1:
                    act.wait_ge(x_done, tb)
                nc.scalar.activation(gate[:], m.psum[:, 4:8, 0:E], ACT.Silu).then_inc(gate_done, 1)

        def low_x(dve, g):
            cols = slice(g * BLK, (g + 1) * BLK)
            for kc in range(KC):
                dve.wait_ge(xh_ready, g * KC + kc + 1)
                nc.vector.tensor_tensor(xl[:, kc, cols], bank[kc], xh[:, kc, cols], ALU.subtract).then_inc(xl_ready, 1)

        def low_h(dve, k):
            n = size[ORDER[k % NMC]]
            dve.wait_ge(hi_done, k + 1)
            nc.vector.tensor_tensor(hl[0:n, k % 3, :], hf[0:n, k % 3, :], hh[0:n, k % 3, :],
                                    ALU.subtract).then_inc(lo_done, 1)

        @block.vector
        def _(dve):
            for g in range(NB):
                if g >= 2:
                    dve.wait_ge(t_ps, KC * (g - 1))
                for j in range(TPB):
                    n = g * TPB + j
                    nc.vector.tensor_scalar(xa[:, g % 2, j, :], m.x[:, n, :], m.mv1[:, n, 0:1], m.rstd1[:, n:n + 1],
                                            ALU.subtract, ALU.mult).then_inc(xa_ready, 1)
                if g >= 1:
                    low_x(dve, g - 1)
            low_x(dve, NB - 1)
            dve.wait_ge(gw_ready, 1)
            nc.vector.tensor_tensor(gwl[:], gw[:, 0, :, :], gwh[:], ALU.subtract).then_inc(gw_ready, 1)

            done = [0]

            def step(ins):
                done[0] += 1
                ins.then_inc(rt_done, 1)
                dve.wait_ge(rt_done, done[0])

            def wide(v):
                return v.unsqueeze(2).broadcast_to([P, NT, NE])
            dve.wait_ge(lt_ps, 1)
            lt = bank[6][:, 0:NT * NE].rearrange("p (n e) -> p n e", e=NE)
            step(nc.vector.tensor_reduce(r1[:, 0, :], lt, AX_X, ALU.max))
            step(nc.vector.tensor_tensor(rt["l"][:], lt, wide(r1[:, 0, :]), ALU.subtract))
            dve.wait_ge(exp_done, 1)
            step(nc.vector.tensor_reduce(r1[:, 1, :], rt["e"][:], AX_X, ALU.add))
            step(nc.vector.reciprocal(r1[:, 2, :], r1[:, 1, :]))
            step(nc.vector.tensor_tensor(rt["p"][:], rt["e"][:], wide(r1[:, 2, :]), ALU.mult))
            left = rt["p"]
            for i in range(2):
                q, s = rt[f"q{i + 1}"], rt[f"s{i + 1}"]
                step(nc.vector.tensor_reduce(r1[:, 3 + 2 * i, :], left[:], AX_X, ALU.max))
                step(nc.vector.tensor_tensor(q[:], left[:], wide(r1[:, 3 + 2 * i, :]), ALU.is_equal))
                step(nc.vector.tensor_tensor(s[:], q[:], rank[:].unsqueeze(1).broadcast_to([P, NT, NE]), ALU.mult))
                step(nc.vector.tensor_reduce(r1[:, 4 + 2 * i, :], s[:], AX_X, ALU.max))
                step(nc.vector.tensor_tensor(q[:], s[:], wide(r1[:, 4 + 2 * i, :]), ALU.is_equal))
                if i == 0:
                    step(nc.vector.scalar_tensor_tensor(rt["sel"][:], q[:], -2.0, rt["p"][:], ALU.mult, ALU.add))
                    left = rt["sel"]
            step(nc.vector.tensor_tensor(rt["e"][:], rt["q1"][:], rt["q2"][:], ALU.add))
            step(nc.vector.tensor_tensor(r1[:, 0, :], r1[:, 3, :], r1[:, 5, :], ALU.add))
            step(nc.vector.tensor_scalar(r1[:, 1, :], r1[:, 0, :], 1e-20, None, ALU.add))
            step(nc.vector.reciprocal(r1[:, 2, :], r1[:, 1, :]))
            step(nc.vector.tensor_tensor(rt["s1"][:], rt["p"][:], rt["e"][:], ALU.mult))
            step(nc.vector.tensor_tensor(rt["l"][:], rt["s1"][:], wide(r1[:, 2, :]), ALU.mult))
            assert done[0] == NSTEP
            dve.wait_ge(wh_ready, 1)
            nc.vector.tensor_tensor(wl[:], raw[:], wh[:], ALU.subtract).then_inc(wl_ready, 1)

            for tb in range(NB):
                for i, c in enumerate(ORDER):
                    k, n = tb * NMC + i, size[c]
                    dve.wait_ge(silu_done, k + 1)
                    if k >= 3:
                        dve.wait_ge(lo_done, k - 2)
                    nc.vector.tensor_tensor(hf[0:n, k % 3, :], bank[k % 2 * 2 + 1][0:n, :], sg[0:n, k % 2, :],
                                            ALU.mult).then_inc(h_done, 1)
                    if k >= 1 and i >= 1:
                        low_h(dve, k - 1)
                low_h(dve, tb * NMC + NMC - 1)
                ts = slice(tb * TPB, (tb + 1) * TPB)
                dve.wait_ge(gate_done, tb + 1)
                nc.vector.tensor_tensor(gs[:], gate[:], m.s[:, ts, :], ALU.mult).then_inc(gs_done, 1)
                dve.wait_ge(gs_done, tb + 1)
                nc.vector.tensor_tensor(m.x[:, ts, :], m.x[:, ts, :], gs[:], ALU.add).then_inc(x_done, 1)

        @block.tensor
        def _(pe):
            for g in range(NB):
                pe.wait_ge(xa_ready, TPB * (g + 1))
                for kc in range(KC):
                    if g >= 1:
                        pe.wait_ge(xl_ready, (g - 1) * KC + kc + 1)
                    for i in range(TPB):
                        mm = nc.tensor.transpose(bank[kc][:, i * P:(i + 1) * P], xa[:, g % 2, i, kc * P:(kc + 1) * P],
                                                 m.ident1[:])
                    mm.then_inc(t_ps, 1)
            pe.wait_ge(gw_ready, 2)
            for tb in range(NB):
                pe.wait_ge(xl_ready, KC * (tb + 1))
                cols = slice(tb * BLK, (tb + 1) * BLK)
                three(nc, bank[2 + tb][0:NE, :], [(gwh[:, kc, :], gwl[:, kc, :], xh[:, kc, cols], xl[:, kc, cols])
                                                  for kc in range(KC)]).then_inc(lg_ps, 1)
            pe.wait_ge(lg_ready, NB)
            for n in range(NT):
                mm = nc.tensor.transpose(bank[6][:, n * NE:(n + 1) * NE], lg[:, n * P:(n + 1) * P], m.ident1[0:NE, 0:NE])
            mm.then_inc(lt_ps, 1)

            def combine_rows():
                pe.wait_ge(rt_done, NSTEP)
                for n in range(NT):
                    mm = nc.tensor.transpose(bank[4 + n // 4][0:NE, n % 4 * P:(n % 4 + 1) * P], rt["l"][:, n, :],
                                             m.ident1[:])
                mm.then_inc(ct_ps, 1)
            combine_rows()
            pe.wait_ge(wl_ready, 1)

            def up(tb, i):
                c = ORDER[i]
                k, n = tb * NMC + i, size[c]
                cols = slice(tb * BLK, (tb + 1) * BLK)
                if k >= 2:
                    pe.wait_ge(h_done, k - 1)
                for w in range(2):
                    h, l = wview(wh, w), wview(wl, w)
                    mm = three(nc, bank[k % 2 * 2 + w][0:n, :], [(h[:, kc, c * P:c * P + n], l[:, kc, c * P:c * P + n],
                                                                  xh[:, kc, cols], xl[:, kc, cols]) for kc in range(KC)])
                mm.then_inc(gu_ps, 1)

            def down(tb, i):
                c = ORDER[i]
                k, n = tb * NMC + i, size[c]
                pe.wait_ge(lo_done, k + 1)
                if i == 0:
                    if tb == 0:
                        pe.wait_ge(ct_ready, 1)
                    else:
                        pe.wait_ge(gate_done, tb)
                for j in range(TPB):
                    tok = slice(j * P, (j + 1) * P)
                    mm = three(nc, bank[4 + j][:, 0:E], [(hh[0:n, k % 3, tok], hl[0:n, k % 3, tok],
                                                          dview(wh)[0:n, c, :], dview(wl)[0:n, c, :])],
                               start=(i == 0), stop=(i == NMC - 1))
                mm.then_inc(down_done, 1)

            for tb in range(NB):
                for i in range(NMC):
                    up(tb, i)
                    if i >= 2:
                        down(tb, i - 2)
                down(tb, NMC - 2)
                down(tb, NMC - 1)


def kernel(**inputs):
    import numpy as np
    import concourse.bacc as bacc
    from concourse.bass_utils import run_bass_kernel_spmd

    i = {n: np.asarray(v) for n, v in inputs.items()}

    def rows(*arrays):
        return np.concatenate(arrays, 0)

    def columns(v):
        return v.reshape(KC, P).T

    q_rows = [(u * HALF + d) * HEADS + h for u in range(2) for h in range(HEADS) for d in range(HALF)]
    k_rows, k_rows_turned = ([((u + turn) % 2 * HALF + d) * KV + kv for u in range(2) for kv in range(KV)
                              for d in range(HALF)] for turn in range(2))
    v_rows = [d * KV + kv for kv in range(KV) for d in range(HD)]

    freq = np.float32(1.0) / np.float32(10000.0) ** (np.arange(HALF, dtype=np.float32) * np.float32(2.0) / np.float32(HD))
    angle = np.arange(S, dtype=np.float32)[:, None] * freq[None, :]
    cos = np.tile(np.cos(angle).T, (P // HALF, 1))
    sin = np.tile(np.sin(angle).T, (P // HALF, 1))
    sin_k = sin.copy()
    sin_k[:P // 2] *= -1
    masks = np.zeros((P, SMALL + 1, QB), np.int32)
    u, t = (np.arange(P) % QB)[:, None], np.arange(QB)[None, :]
    for level in range(SMALL):
        h = 1 << level
        masks[:, level + 1, :] = (u // (2 * h) == t // (2 * h)) & (u % (2 * h) < h) & (t % (2 * h) >= h)

    def gap(v, n):
        return np.zeros((n, v.shape[1]), v.dtype)

    down_idx, shared_down = i["L0_ffn_down_idx"].T, i["L1_ffn_shared_down"].T
    arrays = dict(
        x=i["L0_attn_x"].reshape(T, E), ident=np.eye(P, dtype=np.float32),
        wqkv=rows(i["L0_attn_W_Q"][q_rows], i["L0_attn_W_K"][k_rows], i["L0_attn_W_K"][k_rows_turned],
                  i["L0_attn_W_V"][v_rows]).T,
        cos=cos, sin=sin, sink=sin_k, wo=i["L0_attn_W_O"].T, lut=i["L0_ffn_lut"],
        gu_idx=rows(i["L0_ffn_gate_idx"], i["L0_ffn_up_idx"]).T,
        down_idx=rows(down_idx, gap(down_idx, NI * P - INTER)),
        wx_t=i["L1_attn_Wx"].T, ww=i["L1_attn_Ww"], wk=i["L1_attn_Wk"], wr=i["L1_attn_Wr"], wv=i["L1_attn_Wv"],
        wout=i["L1_attn_Wout"], gamma=columns(i["L1_attn_gamma"]), beta=columns(i["L1_attn_beta"]),
        bw=columns(i["L1_attn_bw"]), masks=masks, diag=(u == t).astype(np.float32),
        gate_w_t=i["L1_ffn_gate_w"].T, rank=np.tile(np.arange(NE, 0, -1, dtype=np.float32), (P, 1)),
        shared_gate=i["L1_ffn_shared_gate"].T, shared_up=i["L1_ffn_shared_up"].T,
        expert_gate=i["L1_ffn_expert_gate"].reshape(NE * EI, E).T,
        expert_up=i["L1_ffn_expert_up"].reshape(NE * EI, E).T,
        expert_down=i["L1_ffn_expert_down"].transpose(0, 2, 1).reshape(NE * EI, E),
        shared_down=rows(shared_down, gap(shared_down, NMC * P - MI)))
    arrays = {n: np.ascontiguousarray(v) for n, v in arrays.items()}

    nc = bacc.Bacc("TRN2", target_bir_lowering=False, num_devices=1)
    a = {n: nc.dram_tensor(n, v.shape, mybir.dt.from_np(v.dtype), kind="ExternalInput").ap()
         for n, v in arrays.items()}
    a["out"] = nc.dram_tensor("out", (T, E), F32, kind="ExternalOutput").ap()
    program(nc, a)
    result = run_bass_kernel_spmd(nc, [arrays], core_ids=[0])
    return result.results[0]["out"].reshape(B, S, E)
```

```python
from contextlib import ExitStack

import concourse.bass as bass
from concourse import mybir

F32 = mybir.dt.float32
F32R = mybir.dt.float32r
BF16 = mybir.dt.bfloat16
I32 = mybir.dt.int32
ALU = mybir.AluOpType
ACT = mybir.ActivationFunctionType
AX_X = mybir.AxisListType.X
AX_XY = mybir.AxisListType.XY

P = 128
B, S, E = 2, 1024, 256
T = B * S
NT = T // P
KC = E // P
BLK = 512
NB = T // BLK
TPB = BLK // P

HEADS, G, HD = 16, 2, 16
KV = HEADS // G
HALF = HD // 2
SLOTS = ((0, 1), (0, 2), (0, 0), (1, 0), (2, 0), (1, 1))
Q_SLOTS = (slice(0, 3), slice(3, 6, 2), slice(4, 5))
K_SLOTS = (slice(2, 5), slice(0, 6, 5), slice(1, 2))
NROW = HD * len(SLOTS)
NAUG = NROW + 3
VW = 32

INTER = 688
LUT = 16
NI = (INTER + P - 1) // P

EPS = 1e-5

NE, EI, SI = 8, 176, 352
MI = NE * EI + SI
NEC = NE * EI // P
NMC = (MI + P - 1) // P
WP = 4 * P + E



class Mem:
    pass


def parts(n, size):
    return [(i, min(size, n - i)) for i in range(0, n, size)]


def program(nc, a):
    with ExitStack() as ctx:
        m = Mem()
        off = [16512]

        def at(name, shape, dt, offset):
            return nc.alloc_sbuf_tensor_at(name, shape, dt, offset=offset)

        def sem(name):
            return ctx.enter_context(nc.semaphore(name))

        m.at, m.sem = at, sem
        m.psum = ctx.enter_context(nc.psum_tensor("psum", [P, 8, BLK], F32))
        m.bank = [m.psum[:, i, :] for i in range(8)]
        base = 16512
        m.x = at("x_tok", [P, NT, E], F32, base)
        m.base = base + NT * E * 4
        b = m.base
        m.xTh = at("xTh", [P, KC, T], F32R, b)
        m.xTl = at("xTl", [P, KC, T], F32R, b + KC * T * 4)
        b += 2 * KC * T * 4
        m.ident = at("ident", [P, P], F32, b)
        m.rstd = at("rstd", [P, NT], F32, b + 512)
        m.mv = at("mv", [P, NT, 2], F32, b + 640)
        b += 1024
        m.l0 = b
        m.q_rows = nc.dram_tensor("q_rows", (len(SLOTS), 2, HEADS, HALF, T), BF16, kind="Internal").ap()
        m.k_rows = nc.dram_tensor("k_rows", (len(SLOTS), 2, KV, HALF, T), BF16, kind="Internal").ap()
        m.m_rows = nc.dram_tensor("m_rows", (B * KV, 3, G * S), BF16, kind="Internal").ap()
        m.den_rows = nc.dram_tensor("den_rows", (B * KV, G * S), F32, kind="Internal").ap()
        m.rec_rows = nc.dram_tensor("rec_rows", (B * KV, G * S), F32, kind="Internal").ap()
        qkv_stage(nc, m, a)
        attention_stage(nc, m, a)
        ffn_stage(nc, m, a)
        time_mix_in_stage(nc, m, a)
        time_mix_stage(nc, m, a)
        experts_stage(nc, m, a)


def qkv_stage(nc, m, a):
    at, sem, bank = m.at, m.sem, m.bank
    b = m.l0
    m.VS = at("VS", [P, NT, KV, VW], F32, b); b += NT * KV * VW * 4
    m.wo = at("wo_raw", [P, KC, E], F32, b); b += KC * E * 4
    m.p0 = b
    NQ = E + 2 * P + P
    wraw = at("wqkv_raw", [P, KC, NQ], F32, b); b += KC * NQ * 4
    wh = at("wqkv_h", [P, KC, NQ], F32R, b); b += KC * NQ * 4
    wl = at("wqkv_l", [P, KC, NQ], F32R, b); b += KC * NQ * 4
    cos = at("cos", [P, S], F32, b); b += S * 4
    sin = at("sin", [P, S], F32, b); b += S * 4
    sink = at("sink", [P, S], F32, b); b += S * 4
    xn = at("xn", [P, 2, TPB, E], F32, b); b += 2 * TPB * E * 4
    prod = at("rope_prod", [P, 6, BLK], F32, b); b += 6 * BLK * 4
    rot = at("rotated", [P, 3, BLK], F32, b); b += 3 * BLK * 4
    res = at("residue", [P, 3, BLK], F32, b); b += 3 * BLK * 4
    st = at("bn_st", [P, NT, 6], F32, b); b += NT * 6 * 4
    ve = at("var_eps", [P, NT], F32, b); b += NT * 4
    mhalf = at("minus_half", [P, TPB], F32, b); b += 32
    assert b <= nc.sbuf_usable_end, b

    x_in = [sem(f"x_in{g}") for g in range(NB)]
    w_in, tab_in, id_in, wo_in = sem("w_in"), sem("tab_in"), sem("id_in"), sem("wo_in")
    w_ready, stats, var_ready, rstd_ready = sem("w_ready"), sem("stats"), sem("var_ready"), sem("rstd_ready")
    const_ready, xn_ready, xt_ps, xt_hi, xt_lo = sem("const_ready"), sem("xn_ready"), sem("xt_ps"), sem("xt_hi"), sem("xt_lo")
    q_ps, k_ps, v_ps, v_out = sem("q_ps"), sem("k_ps"), sem("v_ps"), sem("v_out")
    prod_q, prod_k, rot_ready, part1, resid, part2, part3 = (
        sem(n) for n in ("prod_q", "prod_k", "rot_ready", "part1", "resid", "part2", "part3"))
    part_out = m.part_out = [sem("part_out0"), sem("part_out1")]
    m.qk_in = [sem(f"qk_in{i}") for i in range(3)]
    m.NLUT = KC * 2 * INTER + NI * E
    m.NPIECE = 4
    m.PIECE = m.NLUT // m.NPIECE
    m.qk_at = nc.sbuf_usable_end // 32 * 32 - 3 * (G + 1) * S * 2
    m.QS = [at(f"QS{i}", [NAUG, G * S], BF16, m.qk_at + i * G * S * 2) for i in range(3)]
    m.KS = [at(f"KS{i}", [NAUG, S], BF16, m.qk_at + 3 * G * S * 2 + i * S * 2) for i in range(3)]
    part_at = m.qk_at - 18 * BLK * 2
    assert b <= part_at, b
    part = at("part", [P, 2, 3, 3, BLK], BF16, part_at)

    def load_qk(sp, n):
        bb, kv = divmod(n, KV)
        if n >= 3:
            sp.wait_ge(m.s_ps, (n - 2) * (S // P) * (G * S // BLK))
        seq = slice(bb * S, (bb + 1) * S)
        sp.dma_start(m.KS[n % 3][0:NROW, :],
                     m.k_rows[:, :, kv, :, seq].rearrange("s u d t -> (s u) d t")).then_inc(m.qk_in[n % 3], 16)
        for g in range(G):
            sp.dma_start(m.QS[n % 3][0:NROW, g * S:(g + 1) * S],
                         m.q_rows[:, :, kv * G + g, :, seq].rearrange("s u d t -> (s u) d t")
                         ).then_inc(m.qk_in[n % 3], 16)

    m.load_qk = load_qk
    wh_ready = sem("wh_ready")

    with nc.Block() as block:
        @block.sync
        def _(sp):
            for g in range(NB):
                sp.dma_start(m.x[:, g * TPB:(g + 1) * TPB, :],
                             a["x"].rearrange("(n p) f -> p n f", p=P)[:, g * TPB:(g + 1) * TPB, :]).then_inc(x_in[g], 16)
            sp.dma_start(cos[:], a["cos"]).then_inc(tab_in, 16)
            sp.dma_start(sin[:], a["sin"]).then_inc(tab_in, 16)
            sp.dma_start(sink[:], a["sink"]).then_inc(tab_in, 16)
            sp.dma_start(m.wo[:], a["wo"].rearrange("(c p) n -> p c n", p=P)).then_inc(wo_in, 16)
            for tb in range(NB):
                cols = slice(tb * BLK, (tb + 1) * BLK)
                for i in range(3):
                    for u in range(3):
                        if i == 0:
                            sp.wait_ge(part1, 3 * tb + u + 1)
                        elif i == 1:
                            sp.wait_ge(part2, 3 * tb + u + 1)
                        else:
                            sp.wait_ge(part3, 3 * tb + u + 1)
                        if u < 2:
                            dst = m.q_rows[Q_SLOTS[i], u, :, :, cols].rearrange("s h d t -> (h d) s t")
                        else:
                            dst = m.k_rows[K_SLOTS[i], :, :, :, cols].rearrange("s u h d t -> (u h d) s t")
                        src = part[:, tb % 2, u, i, :].unsqueeze(1).broadcast_to([P, dst.shape[1], BLK])
                        sp.dma_start(dst, src).then_inc(part_out[tb % 2], 16)
                if tb == S // BLK - 1:
                    for i in range(2):
                        sp.wait_ge(part_out[i], 16 * 9 * (tb + 1) // 2)
                    for n in range(3):
                        load_qk(sp, n)
            sp.wait_ge(wo_in, 16)

        @block.scalar
        def _(act):
            act.dma_start(m.ident[:], a["ident"]).then_inc(id_in, 16)
            act.dma_start(wraw[:], a["wqkv"].rearrange("(c p) n -> p c n", p=P)).then_inc(w_in, 16)
            act.wait_ge(w_in, 16)
            nc.scalar.activation(wh[:], wraw[:], ACT.Copy).then_inc(wh_ready, 1)

            def take_xt(g):
                for kc in range(KC):
                    act.wait_ge(xt_ps, g * KC + kc + 1)
                    nc.scalar.activation(m.xTh[:, kc, g * BLK:(g + 1) * BLK], bank[kc][:], ACT.Copy).then_inc(xt_hi, 1)

            def cut(tb):
                for u in range(3):
                    act.wait_ge(rot_ready, 3 * tb + u + 1)
                    if tb >= 2:
                        act.wait_ge(part_out[tb % 2], 16 * 9 * (tb // 2))
                    nc.scalar.activation(part[:, tb % 2, u, 0, :], rot[:, u, :], ACT.Copy).then_inc(part1, 1)
                for u in range(3):
                    act.wait_ge(resid, 3 * tb + u + 1)
                    nc.scalar.activation(part[:, tb % 2, u, 1, :], res[:, u, :], ACT.Copy).then_inc(part2, 1)

            def take_v(tb):
                act.wait_ge(v_ps, tb + 1)
                act.wait_ge(const_ready, 2)
                for i in range(TPB):
                    nc.scalar.activation(m.VS[:, tb * TPB + i, :, 0:HD],
                                         bank[2 + tb % 2][:, i * P:(i + 1) * P].rearrange("p (k d) -> p k d", k=KV),
                                         ACT.Copy).then_inc(v_out, 1)
            for g in range(NB):
                take_xt(g)
                if g >= 1:
                    take_v(g - 1)
                    cut(g - 1)
            take_v(NB - 1)
            cut(NB - 1)

        def third_parts(pool, tb):
            for u in range(3):
                pool.wait_ge(part2, 3 * tb + u + 1)
                nc.gpsimd.tensor_tensor(part[:, tb % 2, u, 2, :], res[:, u, :], part[:, tb % 2, u, 1, :],
                                        ALU.subtract).then_inc(part3, 1)

        @block.gpsimd
        def _(pool):
            nc.gpsimd.memset(mhalf[:], -0.5).then_inc(const_ready, 1)
            nc.gpsimd.memset(m.VS[:], 1.0).then_inc(const_ready, 1)
            for g in range(NB):
                pool.wait_ge(const_ready, 1)
                pool.wait_ge(var_ready, g + 1)
                nc.gpsimd.tensor_tensor(m.rstd[:, g * TPB:(g + 1) * TPB], ve[:, g * TPB:(g + 1) * TPB], mhalf[:],
                                        ALU.pow).then_inc(rstd_ready, 1)
                if g == 0:
                    pool.wait_ge(wh_ready, 1)
                    nc.gpsimd.tensor_tensor(wl[:], wraw[:], wh[:], ALU.subtract).then_inc(w_ready, 1)
                if g >= 2:
                    third_parts(pool, g - 2)
            third_parts(pool, NB - 2)
            third_parts(pool, NB - 1)

        @block.vector
        def _(dve):
            def norm(g):
                dve.wait_ge(x_in[g], 16)
                for i in range(g * TPB, (g + 1) * TPB):
                    nc.vector.bn_stats(st[:, i, :], m.x[:, i, :]).then_inc(stats, 1)
                dve.wait_ge(stats, (2 * g + 1) * TPB)
                for i in range(g * TPB, (g + 1) * TPB):
                    nc.vector.bn_aggr(m.mv[:, i, :], st[:, i, :]).then_inc(stats, 1)
                dve.wait_ge(stats, (2 * g + 2) * TPB)
                nc.vector.tensor_scalar(ve[:, g * TPB:(g + 1) * TPB], m.mv[:, g * TPB:(g + 1) * TPB, 1], EPS, None,
                                        ALU.add).then_inc(var_ready, 1)
                dve.wait_ge(rstd_ready, g + 1)
                if g >= 2:
                    dve.wait_ge(xt_ps, KC * (g - 1))
                for i in range(TPB):
                    n = g * TPB + i
                    nc.vector.tensor_scalar(xn[:, g % 2, i, :], m.x[:, n, :], m.mv[:, n, 0:1], m.rstd[:, n:n + 1],
                                            ALU.subtract, ALU.mult).then_inc(xn_ready, 1)

            def low(g):
                for kc in range(KC):
                    dve.wait_ge(xt_hi, g * KC + kc + 1)
                    cols = slice(g * BLK, (g + 1) * BLK)
                    nc.vector.tensor_tensor(m.xTl[:, kc, cols], bank[kc][:], m.xTh[:, kc, cols],
                                            ALU.subtract).then_inc(xt_lo, 1)

            def rope(tb):
                pos = slice((tb % (S // BLK)) * BLK, (tb % (S // BLK) + 1) * BLK)
                if tb == 0:
                    dve.wait_ge(tab_in, 48)
                if tb >= 1:
                    dve.wait_ge(rot_ready, 3 * tb)
                dve.wait_ge(q_ps, tb + 1)
                nc.vector.tensor_tensor(prod[:, 0, :], bank[4][:], cos[:, pos], ALU.mult).then_inc(prod_q, 1)
                nc.vector.tensor_tensor(prod[:, 1, :], bank[5][:], sin[:, pos], ALU.mult).then_inc(prod_q, 1)
                nc.vector.tensor_tensor(prod[:, 2, :], bank[5][:], cos[:, pos], ALU.mult).then_inc(prod_q, 1)
                nc.vector.tensor_tensor(prod[:, 3, :], bank[4][:], sin[:, pos], ALU.mult).then_inc(prod_q, 1)
                dve.wait_ge(k_ps, tb + 1)
                nc.vector.tensor_tensor(prod[:, 4, :], bank[6][:], cos[:, pos], ALU.mult).then_inc(prod_k, 1)
                nc.vector.tensor_tensor(prod[:, 5, :], bank[7][:], sink[:, pos], ALU.mult).then_inc(prod_k, 1)
                if tb >= 1:
                    dve.wait_ge(part1, 3 * tb)
                    dve.wait_ge(resid, 3 * tb)
                dve.wait_ge(prod_q, 4 * tb + 4)
                nc.vector.tensor_tensor(rot[:, 0, :], prod[:, 0, :], prod[:, 1, :], ALU.subtract).then_inc(rot_ready, 1)
                nc.vector.tensor_tensor(rot[:, 1, :], prod[:, 2, :], prod[:, 3, :], ALU.add).then_inc(rot_ready, 1)
                dve.wait_ge(prod_k, 2 * tb + 2)
                nc.vector.tensor_tensor(rot[:, 2, :], prod[:, 4, :], prod[:, 5, :], ALU.add).then_inc(rot_ready, 1)
                for u in range(3):
                    dve.wait_ge(part1, 3 * tb + u + 1)
                    if tb >= 1:
                        dve.wait_ge(part3, 3 * (tb - 1) + u + 1)
                    nc.vector.tensor_tensor(res[:, u, :], rot[:, u, :], part[:, tb % 2, u, 0, :],
                                            ALU.subtract).then_inc(resid, 1)

            norm(0)
            norm(1)
            low(0)
            for g in range(NB):
                if g + 1 < NB:
                    low(g + 1)
                if g + 2 < NB:
                    norm(g + 2)
                rope(g)

        @block.tensor
        def _(pe):
            pe.wait_ge(id_in, 16)

            def turn(g):
                pe.wait_ge(xn_ready, TPB * (g + 1))
                for kc in range(KC):
                    if g >= 1:
                        pe.wait_ge(xt_lo, (g - 1) * KC + kc + 1)
                    for i in range(TPB):
                        mm = nc.tensor.transpose(bank[kc][:, i * P:(i + 1) * P], xn[:, g % 2, i, kc * P:(kc + 1) * P],
                                                 m.ident[:])
                    mm.then_inc(xt_ps, 1)

            def project(tb):
                cols = slice(tb * BLK, (tb + 1) * BLK)
                pe.wait_ge(xt_lo, KC * (tb + 1))
                if tb == 0:
                    pe.wait_ge(w_ready, 1)
                for j in range(4):
                    if tb >= 1 and j == 0:
                        pe.wait_ge(prod_q, 4 * tb)
                    if tb >= 1 and j == 2:
                        pe.wait_ge(prod_k, 2 * tb)
                    mm = three(nc, bank[4 + j][:], [(wh[:, kc, j * P:(j + 1) * P], wl[:, kc, j * P:(j + 1) * P],
                                                     m.xTh[:, kc, cols], m.xTl[:, kc, cols]) for kc in range(KC)])
                    if j == 1:
                        mm.then_inc(q_ps, 1)
                    if j == 3:
                        mm.then_inc(k_ps, 1)
                if tb >= 2:
                    pe.wait_ge(v_out, TPB * (tb - 1))
                for i in range(TPB):
                    tok = slice(tb * BLK + i * P, tb * BLK + (i + 1) * P)
                    mm = three(nc, bank[2 + tb % 2][:, i * P:(i + 1) * P],
                               [(m.xTh[:, kc, tok], m.xTl[:, kc, tok], wh[:, kc, 4 * P:], wl[:, kc, 4 * P:])
                                for kc in range(KC)])
                mm.then_inc(v_ps, 1)

            turn(0)
            for g in range(NB):
                if g + 1 < NB:
                    turn(g + 1)
                project(g)


def three(nc, out, operands, start=True, stop=True):
    n = len(operands)
    for i, (lh, ll, rh, rl) in enumerate(operands):
        nc.tensor.matmul(out, ll, rh, start=start and i == 0, stop=False)
        nc.tensor.matmul(out, lh, rl, start=False, stop=False)
        mm = nc.tensor.matmul(out, lh, rh, start=False, stop=stop and i == n - 1)
    return mm


def attention_stage(nc, m, a):
    at, sem, bank = m.at, m.sem, m.bank
    NG = B * KV
    NTT = S // P
    NJ = G * S // BLK
    NST = G * S // P
    b = m.p0
    QS, KS, qk_in, load_qk = m.QS, m.KS, m.qk_in, m.load_qk
    wtmp = at("lut_tmp", [P, 3, m.PIECE], F32, b); b += 3 * m.PIECE * 4
    b = max(b, m.p0 + 18432)
    NPT = 2 * NJ
    pt = at("probs_t", [P, NPT, BLK], F32, b); b += NPT * BLK * 4
    osb = at("o_sb", [P, 2, BLK], F32, b); b += 2 * BLK * 4
    m.ctxT = at("ctxT", [P, KC, T], F32, b); b += KC * T * 4
    m.after_ctx = b
    rec = at("rec_b", [P, 2, S], F32, b); b += 2 * S * 4
    mx = at("row_max", [P, 2, 32], F32, b); b += 2 * 32 * 4
    mT = at("row_max_t", [P, 32], F32, b); b += 32 * 4
    mres = at("max_res", [P, 2, 32], F32, b); b += 2 * 32 * 4
    mpt = at("max_parts", [P, 3, 32], BF16, b); b += 3 * 32 * 2
    den = at("den", [P, NST], F32, b); b += NST * 4
    rden = at("rden", [P, NST], F32, b); b += NST * 4
    m.p1 = b
    NLUT, NPIECE, PIECE = m.NLUT, m.NPIECE, m.PIECE
    idx = at("lut_idx", [P, NLUT], I32, b)
    m.fl = at("ffn_l", [P, NLUT], F32R, b); b += NLUT * 4
    m.fh = at("ffn_h", [P, NLUT], F32R, b); b += NLUT * 4
    m.woh = at("wo_h", [P, KC, E], F32R, b); b += KC * E * 4
    m.wol = at("wo_l", [P, KC, E], F32R, b); b += KC * E * 4
    m.w1 = b
    wsum = at("lut_sum", [P, NLUT], F32, b); b += NLUT * 4
    lut = at("lut", [P, LUT], F32, b); b += LUT * 4
    assert b <= m.qk_at, b
    lut_in, idx_in, lut_prod, lut_add, f_hi, f_lo = (
        sem(n) for n in ("lut_in", "idx_in", "lut_prod", "lut_add", "f_hi", "f_lo"))

    ones_ready, mx_zero = sem("ones_ready"), sem("mx_zero")
    max_ps, max_done, mt_done, mp_done, mp_out, m_in = (
        sem(n) for n in ("max_ps", "max_done", "mt_done", "mp_done", "mp_out", "m_in"))
    m.s_ps = sem("s_ps")
    s_ps, p_ready, pv_done, o_done = m.s_ps, sem("p_ready"), sem("pv_done"), sem("o_done")
    o_out, den_out, den_in, rden_ready, rden_out, rec_in, norm_done = (
        sem(n) for n in ("o_out", "den_out", "den_in", "rden_ready", "rden_out", "rec_in", "norm_done"))
    mres_done = sem("mres_done")
    AHEAD = NST // 2
    MX = [bank[0:2], bank[2:4]]
    SP = bank[4:7]
    OB = bank[7]
    def ring(i):
        return SP[i % 3]

    def leave(sp, n):
        bb, kv = divmod(n, KV)
        sp.wait_ge(o_done, n + 1)
        ct, r = kv // 4, kv % 4 * G * HD
        sp.dma_start(m.den_rows[n].rearrange("(j s) -> j s", j=NJ),
                     osb[HD:P:32, n % 2, :]).then_inc(den_out, 16)
        for j in range(NJ):
            g, half = divmod(j, NJ // G)
            sp.dma_start(m.ctxT[r + g * HD:r + (g + 1) * HD, ct,
                                bb * S + half * BLK:bb * S + (half + 1) * BLK],
                         osb[32 * j:32 * j + HD, n % 2, :]).then_inc(o_out, 16)
        sp.wait_ge(den_out, 16 * (n + 1))
        if n >= 1:
            sp.wait_ge(rden_ready, n)
        sp.dma_start(den[:], m.den_rows[n].rearrange("(p c) -> p c", p=P)).then_inc(den_in, 16)

    def spread(sp, n):
        bb, kv = divmod(n, KV)
        r = kv % 4 * G * HD
        sp.wait_ge(rden_ready, n + 1)
        if n >= 1:
            sp.wait_ge(rec_in, 16 * G * n)
        sp.dma_start(m.rec_rows[n].rearrange("(p c) -> p c", p=P), rden[:]).then_inc(rden_out, 16)
        sp.wait_ge(rden_out, 16 * (n + 1))
        if n >= 8:
            sp.wait_ge(norm_done, n // 4 - 1)
        for g in range(G):
            sp.dma_start(rec[r + g * HD:r + (g + 1) * HD, (n // 4) % 2, :],
                         m.rec_rows[n, g * S:(g + 1) * S].rearrange("(o s) -> o s", o=1)
                         .broadcast_to([HD, S])).then_inc(rec_in, 16)

    def normalize(pool, c):
        bb, ct = divmod(c, KC)
        pool.wait_ge(o_out, 16 * NJ * 4 * (c + 1))
        pool.wait_ge(rec_in, 16 * G * 4 * (c + 1))
        v = m.ctxT[:, ct, bb * S:(bb + 1) * S]
        nc.gpsimd.tensor_tensor(v, v, rec[:, c % 2, :], ALU.mult).then_inc(norm_done, 1)

    def take_o(dve, n):
        dve.wait_ge(pv_done, NTT * NJ * (n + 1))
        if n >= 2:
            dve.wait_ge(o_out, 16 * NJ * (n - 1))
            dve.wait_ge(den_out, 16 * (n - 1))
        nc.vector.tensor_copy(osb[:, n % 2, :], OB[:]).then_inc(o_done, 1)

    def invert(dve, n):
        dve.wait_ge(den_in, 16 * (n + 1))
        if n >= 1:
            dve.wait_ge(rden_out, 16 * n)
        nc.vector.reciprocal(rden[:], den[:]).then_inc(rden_ready, 1)

    m.leave, m.spread, m.normalize, m.invert, m.NG = leave, spread, normalize, invert, NG
    m.norm_done, m.all_normed = norm_done, NG // 4
    m.f_hi, m.f_lo, m.lut_add, m.wsum = f_hi, f_lo, lut_add, wsum

    with nc.Block() as block:
        @block.sync
        def _(sp):
            def place_max(n):
                sp.wait_ge(mp_done, 3 * (n + 1))
                for q in range(4):
                    sp.dma_start(m.m_rows[n].rearrange("i (c q s) -> q c i s", q=4, s=32)[q],
                                 mpt[32 * q:32 * q + NST, :, :]).then_inc(mp_out, 16)
                sp.wait_ge(mp_out, 64 * (n + 1))
                sp.dma_start(QS[n % 3][NROW:NAUG, :], m.m_rows[n]).then_inc(m_in, 16)

            for i in range(2):
                sp.wait_ge(m.part_out[i], 16 * 9 * NB // 2)
            sp.dma_start(lut[:], a["lut"].rearrange("(o s) -> o s", o=1).broadcast_to([P, LUT])).then_inc(lut_in, 16)
            sp.dma_start(idx[:, 0:KC * 2 * INTER].rearrange("p (c n) -> p c n", c=KC),
                         a["gu_idx"].rearrange("(c p) n -> p c n", p=P)).then_inc(idx_in, 16)
            sp.dma_start(idx[:, KC * 2 * INTER:].rearrange("p (c n) -> p c n", c=NI),
                         a["down_idx"].rearrange("(c p) n -> p c n", p=P)).then_inc(idx_in, 16)
            place_max(0)
            for n in range(NG):
                if n >= 1:
                    if n + 2 < NG:
                        load_qk(sp, n + 2)
                    leave(sp, n - 1)
                    spread(sp, n - 1)
                if n + 1 < NG:
                    place_max(n + 1)

        def low_part(pool, c):
            cols = slice(c * PIECE, (c + 1) * PIECE)
            if c == 0:
                pool.wait_ge(f_hi, 1)
                nc.gpsimd.tensor_tensor(m.wol[:], m.wo[:], m.woh[:], ALU.subtract).then_inc(f_lo, 1)
            pool.wait_ge(f_hi, c + 2)
            nc.gpsimd.tensor_tensor(m.fl[:, cols], wsum[:, cols], m.fh[:, cols], ALU.subtract).then_inc(f_lo, 1)

        @block.gpsimd
        def _(pool):
            nc.gpsimd.memset(KS[0][NROW:NAUG, :], 1.0).then_inc(ones_ready, 1)
            nc.gpsimd.memset(KS[1][NROW:NAUG, :], 1.0).then_inc(ones_ready, 1)
            nc.gpsimd.memset(KS[2][NROW:NAUG, :], 1.0).then_inc(ones_ready, 1)
            for c in range(NG // 4):
                cols = slice(c * PIECE, (c + 1) * PIECE)
                for v in range(1, LUT):
                    k = c * (LUT - 1) + v - 1
                    pool.wait_ge(lut_prod, c * LUT + v + 1)
                    if k >= 1:
                        pool.wait_ge(lut_add, k)
                    nc.gpsimd.tensor_tensor(wsum[:, cols], wsum[:, cols], wtmp[:, k % 3, :],
                                            ALU.add).then_inc(lut_add, 1)
                if c >= 1:
                    low_part(pool, c - 1)
                    normalize(pool, c - 1)

        def take_high(act, c):
            cols = slice(c * PIECE, (c + 1) * PIECE)
            act.wait_ge(lut_add, (c + 1) * (LUT - 1))
            nc.scalar.activation(m.fh[:, cols], wsum[:, cols], ACT.Copy).then_inc(f_hi, 1)

        @block.scalar
        def _(act):
            for n in range(NG):
                if n == 2 or n >= 5 and n % 4 == 1:
                    if n == 2:
                        nc.scalar.activation(m.woh[:], m.wo[:], ACT.Copy).then_inc(f_hi, 1)
                    else:
                        take_high(act, n // 4 - 1)
                for i in range(NTT * NJ):
                    k = n * NTT * NJ + i
                    act.wait_ge(s_ps, k + 1)
                    if k >= NPT:
                        act.wait_ge(pv_done, k - NPT + 1)
                    nc.scalar.activation(pt[:, k % NPT, :], ring(k)[:], ACT.Exp,
                                         scale=float(E) ** -0.5).then_inc(p_ready, 1)

        @block.vector
        def _(dve):
            nc.vector.memset(mx[:], 0.0).then_inc(mx_zero, 1)
            dve.wait_ge(mx_zero, 1)

            def row_max(n, i):
                k = n * NST + i
                dve.wait_ge(max_ps, k + 1)
                if i == 0 and n >= 2:
                    dve.wait_ge(mt_done, n - 1)
                nc.vector.tensor_reduce(mx[:, n % 2, i:i + 1], m.psum[:, 2 * (k % 2):2 * (k % 2) + 2, :], AX_XY, ALU.max).then_inc(max_done, 1)

            def max_parts(n):
                dve.wait_ge(max_done, NST * (n + 1))
                if n >= 1:
                    dve.wait_ge(mp_done, 3 * n)
                nc.vector.transpose(mT[:], mx[:, n % 2, :]).then_inc(mt_done, 1)
                dve.wait_ge(mt_done, n + 1)
                if n >= 1:
                    dve.wait_ge(mp_out, 64 * n)
                nc.vector.tensor_scalar(mpt[:, 0, :], mT[:], -1.0, None, ALU.mult).then_inc(mp_done, 1)
                dve.wait_ge(mp_done, 3 * n + 1)
                nc.vector.scalar_tensor_tensor(mres[:, 0, :], mT[:], -1.0, mpt[:, 0, :], ALU.mult,
                                               ALU.subtract).then_inc(mres_done, 1)
                dve.wait_ge(mres_done, n + 1)
                nc.vector.tensor_copy(mpt[:, 1, :], mres[:, 0, :]).then_inc(mp_done, 1)
                dve.wait_ge(mp_done, 3 * n + 2)
                nc.vector.tensor_tensor(mpt[:, 2, :], mres[:, 0, :], mpt[:, 1, :], ALU.subtract).then_inc(mp_done, 1)

            def look_up(k):
                c, v = divmod(k, LUT)
                cols = slice(c * PIECE, (c + 1) * PIECE)
                if k == 0:
                    dve.wait_ge(lut_in, 16)
                    dve.wait_ge(idx_in, 32)
                slot = c * (LUT - 1) + v - 1
                if v >= 1 and slot >= 3:
                    dve.wait_ge(lut_add, slot - 2)
                nc.vector.tensor_scalar(wsum[:, cols] if v == 0 else wtmp[:, slot % 3, :], idx[:, cols], float(v),
                                        lut[:, v:v + 1], ALU.is_equal, ALU.mult).then_inc(lut_prod, 1)

            for i in range(NST + AHEAD):
                row_max(i // NST, i % NST)
                if i == NST - 1:
                    max_parts(0)
            for n in range(NG):
                for i in range(NST):
                    if i == 2 and n >= 1:
                        take_o(dve, n - 1)
                    k = (n + 1) * NST + AHEAD + i
                    if k < NG * NST:
                        row_max(k // NST, k % NST)
                        if k % NST == NST - 1:
                            max_parts(k // NST)
                    if i == 6 and n >= 1:
                        invert(dve, n - 1)
                    if n < NG - 2 and i % 4 == 0:
                        look_up(4 * n + i // 4)
                    elif n == NG - 2 and i % 2 == 1:
                        look_up(4 * n + i // 2)
            take_o(dve, NG - 1)

        @block.tensor
        def _(pe):
            pe.wait_ge(ones_ready, 3)

            def maxima(n, i):
                k = n * NST + i
                if i == 0:
                    pe.wait_ge(qk_in[n % 3], 16 * (1 + G) * (n // 3 + 1))
                if k >= 2:
                    pe.wait_ge(max_done, k - 1)
                for h in range(2):
                    mm = nc.tensor.matmul(MX[k % 2][h][:], QS[n % 3][0:NROW, i * P:(i + 1) * P],
                                          KS[n % 3][0:NROW, h * BLK:(h + 1) * BLK], start=True, stop=True)
                mm.then_inc(max_ps, 1)

            def scores(n, t, j):
                k = (n * NTT + t) * NJ + j
                if t == 0 and j == 0:
                    pe.wait_ge(m_in, 16 * (n + 1))
                if k >= 3:
                    pe.wait_ge(p_ready, k - 2)
                nc.tensor.matmul(ring(k)[:], KS[n % 3][:, t * P:(t + 1) * P], QS[n % 3][:, j * BLK:(j + 1) * BLK],
                                 start=True, stop=True).then_inc(s_ps, 1)

            def weigh(n, t):
                bb, kv = divmod(n, KV)
                for j in range(NJ):
                    k = (n * NTT + t) * NJ + j
                    pe.wait_ge(p_ready, k + 1)
                    if t == 0 and j == 0 and n >= 1:
                        pe.wait_ge(o_done, n)
                    nc.tensor.matmul(OB[32 * j:32 * (j + 1), :], m.VS[:, bb * NTT + t, kv, :], pt[:, k % NPT, :],
                                     start=(t == 0), stop=(t == NTT - 1)).then_inc(pv_done, 1)

            def maxima_ahead(k):
                if k < NG * NST:
                    maxima(k // NST, k % NST)

            for k in range(NST + AHEAD):
                maxima_ahead(k)
            for n in range(NG):
                for t in range(NTT):
                    k = (n + 1) * NST + AHEAD + 2 * t
                    maxima_ahead(k)
                    scores(n, t, 0)
                    if t >= 1:
                        weigh(n, t - 1)
                    elif n >= 1:
                        weigh(n - 1, NTT - 1)
                    maxima_ahead(k + 1)
                    for j in range(1, NJ):
                        scores(n, t, j)
            weigh(NG - 1, NTT - 1)




def ffn_stage(nc, m, a):
    at, sem, bank = m.at, m.sem, m.bank
    b = m.l0
    ch = at("ctx_h", [P, KC, T], F32R, b); b += KC * T * 4
    cl = at("ctx_l", [P, KC, T], F32R, b); b += KC * T * 4
    m.woh1 = at("wout_h", [P, KC, E], F32R, b); b += KC * E * 4
    m.wol1 = at("wout_l", [P, KC, E], F32R, b); b += KC * E * 4
    m.ident1 = at("ident1", [P, P], F32, b); b += P * 4
    m.mv1 = at("mv1", [P, NT, 2], F32, b); b += NT * 8
    m.rstd1 = at("rstd1", [P, NT], F32, b); b += NT * 4
    m.p3 = b
    sg = at("f_silu", [P, 2, BLK], F32, b); b += 2 * BLK * 4
    hf = at("f_h", [P, 2, BLK], F32, b); b += 2 * BLK * 4
    hh = at("f_hh", [P, 3, BLK], F32R, b); b += 3 * BLK * 4
    m.xb = at("x_norm2", [P, NT, E], F32, m.after_ctx - KC * T * 4)
    assert b <= m.after_ctx - KC * T * 4
    b = m.after_ctx
    gs = at("f_gs", [P, TPB, E], F32, b); b += TPB * E * 4
    m.xa = at("f_xa", [P, TPB, E], F32, b); b += TPB * E * 4
    assert b <= m.p1
    b = m.w1
    m.raw1 = raw = at("w1_raw", [P, 6, KC, E], F32, b); b += 6 * KC * E * 4
    m.wh1 = wh = at("w1_h", [P, 4, KC, E], F32R, b); b += 4 * KC * E * 4
    m.wl1 = wl = at("w1_l", [P, 4, KC, E], F32R, b); b += 4 * KC * E * 4
    m.cols3 = at("cols3", [P, 3, KC], F32, b); b += 32
    m.gw = at("gate_w", [P, KC, NE], F32, b); b += KC * NE * 4
    m.st = at("bn_st1", [P, 2, TPB, 6], F32, b); b += 2 * TPB * 24
    m.ve = at("var_eps1", [P, 2, TPB], F32, b); b += 2 * TPB * 4
    m.mv2 = at("mv2", [P, TPB, 2], F32, b); b += TPB * 8
    m.rstd2 = at("rstd2", [P, TPB], F32, b); b += 32
    m.mhalf = at("minus_half1", [P, TPB], F32, b); b += 32
    gate = at("f_gate", [P, TPB, E], F32, b); b += TPB * E * 4
    hl = at("f_hl", [P, 3, BLK], F32R, b); b += 3 * BLK * 4
    assert b <= nc.sbuf_usable_end, b
    w_in, c_in, const, wc_ps, wh_ready, wl_ready = (
        sem(n) for n in ("t_w_in", "t_c_in", "t_const", "wc_ps", "t_wh", "t_wl"))
    m.stats, m.var, m.rstd, m.xa_ready, m.xb_ready = (sem(n) for n in ("t_stats", "t_var", "t_rstd", "t_xa", "t_xb"))
    ctx_hi, ctx_lo, gu_ps, silu_done, h_done, hi_done, lo_done, down_done, s_done = (
        sem(n) for n in ("ctx_hi", "ctx_lo", "gu_ps", "f_silu_done", "h_done", "hi_done", "lo_done", "down_done", "s_done"))
    gate_done, gs_done, x_done = sem("gate_done"), sem("gs_done"), sem("x_done")
    NQ = NI + 1
    fh = m.fh[:, 0:KC * 2 * INTER].rearrange("p (c n) -> p c n", c=KC)
    fl = m.fl[:, 0:KC * 2 * INTER].rearrange("p (c n) -> p c n", c=KC)
    dh = m.fh[:, KC * 2 * INTER:].rearrange("p (c n) -> p c n", c=NI)
    dl = m.fl[:, KC * 2 * INTER:].rearrange("p (c n) -> p c n", c=NI)
    pieces = parts(INTER, P)

    def wc_banks():
        s = NB * NQ % 2 * 2
        return m.psum[:, s:s + 2, :]

    with nc.Block() as block:
        @block.sync
        def _(sp):
            m.leave(sp, m.NG - 1)
            m.spread(sp, m.NG - 1)
            for j, n in enumerate(("wx_t", "ww", "wk", "wr", "wv", "wout")):
                sp.dma_start(raw[:, j, :, :], a[n].rearrange("(c p) n -> p c n", p=P)).then_inc(w_in, 16)
            sp.dma_start(m.ident1[:], a["ident"]).then_inc(c_in, 16)
            for j, n in enumerate(("gamma", "beta", "bw")):
                sp.dma_start(m.cols3[:, j, :], a[n]).then_inc(c_in, 16)
            sp.dma_start(m.gw[:], a["gate_w_t"].rearrange("(c p) n -> p c n", p=P)).then_inc(c_in, 16)
            sp.wait_ge(c_in, 80)

        @block.gpsimd
        def _(pool):
            nc.gpsimd.memset(m.mhalf[:], -0.5).then_inc(const, 1)
            m.normalize(pool, m.NG // 4 - 1)
            pool.wait_ge(wh_ready, 2)
            nc.gpsimd.tensor_tensor(wl[:, 1:4, :, :], raw[:, 2:5, :, :], wh[:, 1:4, :, :], ALU.subtract).then_inc(wl_ready, 1)
            nc.gpsimd.tensor_tensor(m.wol1[:], raw[:, 5, :, :], m.woh1[:], ALU.subtract).then_inc(wl_ready, 1)
            pool.wait_ge(const, 1)
            for g in range(NB - 1):
                for i in range(2):
                    inverse_deviation(pool, m, g, i)

        @block.scalar
        def _(act):
            last = slice((m.NPIECE - 1) * m.PIECE, m.NLUT)
            nc.scalar.activation(m.fh[:, last], m.wsum[:, last], ACT.Copy).then_inc(m.f_hi, 1)

            def cut_ctx(tb):
                act.wait_ge(m.norm_done, m.all_normed)
                cols = slice(tb * BLK, (tb + 1) * BLK)
                nc.scalar.activation(ch[:, :, cols], m.ctxT[:, :, cols], ACT.Copy).then_inc(ctx_hi, 1)
            for tb in range(NB):
                for c, (i0, n) in enumerate(pieces):
                    k = tb * NI + c
                    act.wait_ge(gu_ps, k + 1)
                    if k >= 2:
                        act.wait_ge(h_done, k - 1)
                    nc.scalar.activation(sg[0:n, k % 2, :], bank[(tb * NQ + c) % 2 * 2][0:n, :],
                                         ACT.Silu).then_inc(silu_done, 1)
                    act.wait_ge(h_done, k + 1)
                    if k >= 3:
                        act.wait_ge(down_done, k - 2)
                    nc.scalar.activation(hh[0:n, k % 3, :], hf[0:n, k % 2, :], ACT.Copy).then_inc(hi_done, 1)
                    if tb == 0 and c == NI - 1:
                        for i in range(NB):
                            cut_ctx(i)
                    if tb == 1 and c == 0:
                        act.wait_ge(w_in, 16 * 6)
                        act.wait_ge(m.f_lo, m.NPIECE + 1)
                        nc.scalar.activation(wh[:, 1:4, :, :], raw[:, 2:5, :, :], ACT.Copy).then_inc(wh_ready, 1)
                        nc.scalar.activation(m.woh1[:], raw[:, 5, :, :], ACT.Copy).then_inc(wh_ready, 1)
                if tb == NB - 1:
                    act.wait_ge(wc_ps, 1)
                    nc.scalar.activation(wh[:, 0, :, :], wc_banks()[:, :, 0:E], ACT.Copy).then_inc(wh_ready, 1)
                act.wait_ge(down_done, (tb + 1) * NI)
                if tb >= 1:
                    act.wait_ge(gs_done, tb)
                nc.scalar.activation(gate[:], m.psum[:, 4:8, 0:E], ACT.Silu).then_inc(gate_done, 1)

        @block.vector
        def _(dve):
            last = slice((m.NPIECE - 1) * m.PIECE, m.NLUT)
            dve.wait_ge(m.f_hi, m.NPIECE + 1)
            nc.vector.tensor_tensor(m.fl[:, last], m.wsum[:, last], m.fh[:, last], ALU.subtract).then_inc(m.f_lo, 1)

            def low_ctx(tb):
                cols = slice(tb * BLK, (tb + 1) * BLK)
                dve.wait_ge(ctx_hi, tb + 1)
                nc.vector.tensor_tensor(cl[:, :, cols], m.ctxT[:, :, cols], ch[:, :, cols],
                                        ALU.subtract).then_inc(ctx_lo, 1)

            for tb in range(NB):
                for c, (i0, n) in enumerate(pieces):
                    k = tb * NI + c
                    if k == 2:
                        m.invert(dve, m.NG - 1)
                    dve.wait_ge(silu_done, k + 1)
                    if k >= 2:
                        dve.wait_ge(lo_done, k - 1)
                        dve.wait_ge(hi_done, k - 1)
                    nc.vector.tensor_tensor(hf[0:n, k % 2, :], bank[(tb * NQ + c) % 2 * 2 + 1][0:n, :],
                                            sg[0:n, k % 2, :], ALU.mult).then_inc(h_done, 1)
                    dve.wait_ge(hi_done, k + 1)
                    if k >= 3:
                        dve.wait_ge(down_done, k - 2)
                    nc.vector.tensor_tensor(hl[0:n, k % 3, :], hf[0:n, k % 2, :], hh[0:n, k % 3, :],
                                            ALU.subtract).then_inc(lo_done, 1)
                    if tb == 0 and c == NI - 1:
                        for i in range(NB):
                            low_ctx(i)
                    if tb >= 1 and c < 4:
                        if c == 0:
                            dve.wait_ge(x_done, tb)
                        if tb == 1 and c == 3:
                            dve.wait_ge(ctx_lo, NB)
                        (statistics if c % 2 == 0 else norm)(nc, dve, m, tb - 1, c // 2)
                if tb == NB - 1:
                    dve.wait_ge(wh_ready, 3)
                    nc.vector.tensor_tensor(wl[:, 0, :, :], wc_banks()[:, :, 0:E], wh[:, 0, :, :],
                                            ALU.subtract).then_inc(wl_ready, 1)
                dve.wait_ge(gate_done, tb + 1)
                dve.wait_ge(s_done, tb + 1)
                if tb >= 1:
                    dve.wait_ge(x_done, tb)
                slot = (tb * NQ + NI) % 2 * 2
                nc.vector.tensor_tensor(gs[:], m.psum[:, slot:slot + 2, :].rearrange("p b (n e) -> p (b n) e", e=E),
                                        gate[:], ALU.mult).then_inc(gs_done, 1)
                xt = m.x[:, tb * TPB:(tb + 1) * TPB, :]
                dve.wait_ge(gs_done, tb + 1)
                nc.vector.tensor_tensor(xt, xt, gs[:], ALU.add).then_inc(x_done, 1)
        @block.tensor
        def _(pe):
            def slot_free(tb, c):
                q = tb * NQ + c - 2
                if q >= 0:
                    t0, c0 = divmod(q, NQ)
                    if c0 < NI:
                        pe.wait_ge(h_done, t0 * NI + c0 + 1)
                    else:
                        pe.wait_ge(gs_done, t0 + 1)
                return (q + 2) % 2 * 2

            def join_weights():
                pe.wait_ge(w_in, 16 * 6)
                s = slot_free(NB, 0)
                for i in range(KC):
                    for mc in range(KC):
                        mm = nc.tensor.matmul(bank[s + i][:, 0:E], raw[:, 0, mc, i * P:(i + 1) * P], raw[:, 1, mc, :],
                                              start=(mc == 0), stop=(mc == KC - 1))
                mm.then_inc(wc_ps, 1)

            def up(tb, c):
                i0, n = pieces[c]
                cols = slice(tb * BLK, (tb + 1) * BLK)
                s = slot_free(tb, c)
                for w in range(2):
                    i = w * INTER + i0
                    mm = three(nc, bank[s + w][0:n, :], [(fh[:, kc, i:i + n], fl[:, kc, i:i + n],
                                                          m.xTh[:, kc, cols], m.xTl[:, kc, cols]) for kc in range(KC)])
                mm.then_inc(gu_ps, 1)

            def down(tb, c):
                i0, n = pieces[c]
                k = tb * NI + c
                pe.wait_ge(lo_done, k + 1)
                if c == 0 and tb >= 1:
                    pe.wait_ge(gate_done, tb)
                if c == 0 and tb == 0:
                    pe.wait_ge(m.f_lo, m.NPIECE + 1)
                for i in range(TPB):
                    tok = slice(i * P, (i + 1) * P)
                    mm = three(nc, bank[4 + i][:, 0:E], [(hh[0:n, k % 3, tok], hl[0:n, k % 3, tok],
                                                          dh[0:n, c, :], dl[0:n, c, :])],
                               start=(c == 0), stop=(c == NI - 1))
                mm.then_inc(down_done, 1)

            def attn_out(tb):
                pe.wait_ge(ctx_lo, tb + 1)
                s = slot_free(tb, NI)
                for i in range(TPB):
                    tok = slice(tb * BLK + i * P, tb * BLK + (i + 1) * P)
                    mm = three(nc, bank[s + i // 2][:, i % 2 * E:(i % 2 + 1) * E],
                               [(ch[:, kc, tok], cl[:, kc, tok], m.woh[:, kc, :], m.wol[:, kc, :])
                                for kc in range(KC)])
                mm.then_inc(s_done, 1)

            for tb in range(NB):
                for c in range(NI):
                    up(tb, c)
                    if c >= 1:
                        down(tb, c - 1)
                attn_out(tb)
                if tb == NB - 1:
                    join_weights()
                down(tb, NI - 1)


def statistics(nc, dve, m, g, i):
    ts = slice(g * TPB, (g + 1) * TPB)
    src, mv = (m.x[:, ts, :], m.mv1[:, ts, :]) if i == 0 else (m.xa, m.mv2)
    done = (2 * g + i) * 2 * TPB
    if i == 1:
        dve.wait_ge(m.xa_ready, TPB * (g + 1))
    if g >= 1:
        dve.wait_ge(m.xb_ready, TPB * g)
    for j in range(TPB):
        nc.vector.bn_stats(m.st[:, i, j, :], src[:, j, :]).then_inc(m.stats, 1)
    dve.wait_ge(m.stats, done + TPB)
    for j in range(TPB):
        nc.vector.bn_aggr(mv[:, j, :], m.st[:, i, j, :]).then_inc(m.stats, 1)
    dve.wait_ge(m.stats, done + 2 * TPB)
    nc.vector.tensor_scalar(m.ve[:, i, :], mv[:, :, 1], EPS, None, ALU.add).then_inc(m.var, 1)


def inverse_deviation(pool, m, g, i):
    pool.wait_ge(m.var, 2 * g + i + 1)
    pool.tensor_tensor(m.rstd1[:, g * TPB:(g + 1) * TPB] if i == 0 else m.rstd2[:], m.ve[:, i, :], m.mhalf[:],
                       ALU.pow).then_inc(m.rstd, 1)


def norm(nc, dve, m, g, i):
    dve.wait_ge(m.rstd, 2 * g + i + 1)
    for j in range(TPB):
        n = g * TPB + j
        if i == 0:
            nc.vector.tensor_scalar(m.xa[:, j, :], m.x[:, n, :], m.mv1[:, n, 0:1], m.rstd1[:, n:n + 1],
                                    ALU.subtract, ALU.mult).then_inc(m.xa_ready, 1)
        else:
            nc.vector.tensor_scalar(m.xb[:, n, :], m.xa[:, j, :], m.mv2[:, j, 0:1], m.rstd2[:, j:j + 1],
                                    ALU.subtract, ALU.mult).then_inc(m.xb_ready, 1)


LH, LD = 4, 64
NCH = 2 * B
CH = 128
NC = S // CH
SMALL = 5
QB = 32


def time_mix_in_stage(nc, m, a):
    at, sem, bank = m.at, m.sem, m.bank
    b = m.base
    m.D = at("decay", [P, KC, T], F32, b); b += KC * T * 4
    m.K = at("key", [P, KC, T], F32, b); b += KC * T * 4
    m.R = at("recept", [P, KC, T], F32, b); b += KC * T * 4
    m.V = at("value", [P, NT, E], F32, b); b += NT * E * 4
    assert b <= m.l0 + 2 * KC * T * 4
    b = m.p3
    yh = at("y_h", [P, KC, T], F32R, b); b += KC * T * 4
    assert b <= m.after_ctx - KC * T * 4
    b = m.after_ctx
    b = m.after_ctx + 2 * TPB * E * 4
    yl = at("y_l", [P, KC, T], F32R, b); b += KC * T * 4
    yf = at("y_f", [P, 2, KC, BLK], F32, b); b += 2 * KC * BLK * 4
    xa = at("x_norm", [P, TPB, E], F32, b); b += TPB * E * 4
    xt = at("x_norm_t", [P, KC, BLK], F32, b); b += KC * BLK * 4
    nbw = at("nbw", [P, KC], F32, b); b += 32
    assert b <= m.w1
    raw, wh, wl, cols3 = m.raw1, m.wh1, m.wl1, m.cols3
    m.rt_at = nc.sbuf_usable_end // 32 * 32 - NMC * WP * 4 - 9 * NT * NE * 4
    m.lt = at("logits_t", [P, NT, NE], F32, m.rt_at)
    names = ("t2_xa", "t_ps", "t_yf", "t_yh", "t_xt", "t_yl", "t_nbw", "pr_ps", "act_out", "dve_out", "lt_ps", "lt_out")
    (xa_ready, t_ps, yf_ready, yh_ready, xt_ready, yl_ready, nbw_ready, pr_ps, act_out, dve_out, lt_ps, lt_out) = (
        sem(n) for n in names)

    ITEMS = [("w", 0), ("k", 0), ("r", 0), ("w", 1), ("k", 1), ("r", 1), ("v", 0), ("v", 1)]
    NIT = len(ITEMS)
    RING = 5

    def taken_by(kind):
        return "act" if kind in "wr" else "dve"

    def order(k):
        who = taken_by(ITEMS[k % NIT][0])
        per = sum(taken_by(x[0]) == who for x in ITEMS)
        return k // NIT * per + sum(taken_by(x[0]) == who for x in ITEMS[:k % NIT + 1])

    def rbank(k):
        return bank[2 + k % RING]

    def take(eng, k, tb):
        kind, i = ITEMS[k % NIT]
        cols = slice(tb * BLK, (tb + 1) * BLK)
        eng.wait_ge(pr_ps, k + 1)
        if kind == "w":
            nc.scalar.activation(m.D[:, i, cols], rbank(k), ACT.Sigmoid, bias=nbw[:, i:i + 1],
                                 scale=-1.0).then_inc(act_out, 1)
        elif kind == "r":
            nc.scalar.activation(m.R[:, i, cols], rbank(k), ACT.Sigmoid).then_inc(act_out, 1)
        elif kind == "k":
            nc.vector.tensor_copy(m.K[:, i, cols], rbank(k)).then_inc(dve_out, 1)
        else:
            n = tb * TPB + 2 * i
            nc.vector.tensor_copy(m.V[:, n:n + 2, :], rbank(k).rearrange("p (n e) -> p n e", n=2)).then_inc(dve_out, 1)

    with nc.Block() as block:
        @block.gpsimd
        def _(pool):
            for i in range(2):
                inverse_deviation(pool, m, NB - 1, i)

        @block.scalar
        def _(act):
            def out_b(g):
                for kc in range(KC):
                    act.wait_ge(t_ps, 2 * g * KC + kc + 1)
                    if g >= 2:
                        act.wait_ge(yl_ready, g - 1)
                    nc.scalar.activation(yf[:, g % 2, kc, :], bank[kc], ACT.Identity, bias=cols3[:, 1, kc:kc + 1],
                                         scale=cols3[:, 0, kc:kc + 1]).then_inc(yf_ready, 1)
                act.wait_ge(yf_ready, KC * (g + 1))
                nc.scalar.activation(yh[:, :, g * BLK:(g + 1) * BLK], yf[:, g % 2, :, :], ACT.Copy).then_inc(yh_ready, 1)

            def out_a(g):
                for kc in range(KC):
                    act.wait_ge(t_ps, (2 * g + 1) * KC + kc + 1)
                    if g >= 1:
                        act.wait_ge(lt_ps, g)
                    nc.scalar.activation(xt[:, kc, :], bank[kc], ACT.Copy).then_inc(xt_ready, 1)

            out_b(0)
            out_a(0)
            out_b(1)
            act.wait_ge(nbw_ready, 1)
            for g in range(NB):
                for i in range(NIT):
                    if taken_by(ITEMS[i][0]) == "act":
                        take(act, g * NIT + i, g)
                if g + 1 < NB:
                    out_a(g + 1)
                if g + 2 < NB:
                    out_b(g + 2)

        @block.vector
        def _(dve):
            def once_normed(g):
                if g >= 1:
                    dve.wait_ge(t_ps, 2 * g * KC)
                for j in range(TPB):
                    n = g * TPB + j
                    nc.vector.tensor_scalar(xa[:, j, :], m.x[:, n, :], m.mv1[:, n, 0:1], m.rstd1[:, n:n + 1],
                                            ALU.subtract, ALU.mult).then_inc(xa_ready, 1)

            def low(g):
                dve.wait_ge(yh_ready, g + 1)
                cols = slice(g * BLK, (g + 1) * BLK)
                nc.vector.tensor_tensor(yl[:, :, cols], yf[:, g % 2, :, :], yh[:, :, cols],
                                        ALU.subtract).then_inc(yl_ready, 1)
            nc.vector.tensor_scalar(nbw[:], cols3[:, 2, :], -1.0, None, ALU.mult).then_inc(nbw_ready, 1)
            once_normed(0)
            low(0)
            for g in range(NB):
                if g == 0:
                    for i in range(2):
                        statistics(nc, dve, m, NB - 1, i)
                        norm(nc, dve, m, NB - 1, i)
                if g + 1 < NB:
                    once_normed(g + 1)
                    low(g + 1)
                for i in range(NIT):
                    if taken_by(ITEMS[i][0]) == "dve":
                        take(dve, g * NIT + i, g)
            dve.wait_ge(lt_ps, NB)
            nc.vector.tensor_copy(m.lt[:], bank[7][:, 0:NT * NE].rearrange("p (n e) -> p n e", e=NE)).then_inc(lt_out, 1)

        @block.tensor
        def _(pe):
            def turn(g, which):
                k = 2 * g + which
                if which:
                    pe.wait_ge(xa_ready, TPB * (g + 1))
                elif g == NB - 1:
                    pe.wait_ge(m.xb_ready, NT)
                for kc in range(KC):
                    if k >= 1:
                        if which:
                            pe.wait_ge(yf_ready, g * KC + kc + 1)
                        else:
                            pe.wait_ge(xt_ready, (g - 1) * KC + kc + 1)
                    for i in range(TPB):
                        src = xa[:, i, kc * P:(kc + 1) * P] if which else m.xb[:, g * TPB + i, kc * P:(kc + 1) * P]
                        mm = nc.tensor.transpose(bank[kc][:, i * P:(i + 1) * P], src, m.ident1[:])
                    mm.then_inc(t_ps, 1)

            def logits(g):
                pe.wait_ge(xt_ready, KC * (g + 1))
                for j in range(TPB):
                    n = g * TPB + j
                    for kc in range(KC):
                        mm = nc.tensor.matmul(bank[7][:, n * NE:(n + 1) * NE], xt[:, kc, j * P:(j + 1) * P],
                                              m.gw[:, kc, :], start=(kc == 0), stop=(kc == KC - 1))
                mm.then_inc(lt_ps, 1)

            def project(g):
                cols = slice(g * BLK, (g + 1) * BLK)
                pe.wait_ge(yl_ready, g + 1)
                for i, (kind, c) in enumerate(ITEMS):
                    k = g * NIT + i
                    if k >= RING:
                        pe.wait_ge(act_out if taken_by(ITEMS[(k - RING) % NIT][0]) == "act" else dve_out, order(k - RING))
                    if kind == "v":
                        for j in range(2):
                            tok = slice(g * BLK + (2 * c + j) * P, g * BLK + (2 * c + j + 1) * P)
                            mm = three(nc, rbank(k)[:, j * E:(j + 1) * E],
                                       [(yh[:, kc, tok], yl[:, kc, tok], wh[:, 3, kc, :], wl[:, 3, kc, :])
                                        for kc in range(KC)])
                    else:
                        w = "wkr".index(kind)
                        ch = slice(c * P, (c + 1) * P)
                        mm = three(nc, rbank(k), [(wh[:, w, kc, ch], wl[:, w, kc, ch], yh[:, kc, cols], yl[:, kc, cols])
                                                  for kc in range(KC)])
                    mm.then_inc(pr_ps, 1)

            turn(0, 0)
            turn(0, 1)
            turn(1, 0)
            for g in range(NB):
                project(g)
                logits(g)
                if g + 1 < NB:
                    turn(g + 1, 1)
                if g + 2 < NB:
                    turn(g + 2, 0)


def time_mix_stage(nc, m, a):
    at, sem, bank = m.at, m.sem, m.bank
    NH = 2
    NS = NC * NH
    b = m.p3
    A = [at(f"A{g}", [P, NS, CH], F32, b + g * NS * CH * 4) for g in range(NCH)]; b += NCH * NS * CH * 4
    AD = [at(f"AD{g}", [P, NS, QB], F32, b + g * NS * QB * 4) for g in range(NCH)]; b += NCH * NS * QB * 4
    combT = at("comb_t", [NE, T], F32, b)
    TOT = {1: None}
    for s in (2, 4, 8, 16, 32, 64, 128):
        TOT[s] = at(f"tot{s}", [P, NCH, S // s], F32, b); b += NCH * (S // s) * 4
    kT = [at(f"kT{i}", [P, NC, P], F32, b + i * NC * P * 4) for i in range(2)]; b += 2 * NC * P * 4
    ST = [at(f"state{i}", [P, NC, LD], F32, b + i * NC * LD * 4) for i in range(2)]; b += 2 * NC * LD * 4
    yl = at("ty_l", [P, KC, T], F32R, m.p3)
    masks = at("masks", [P, SMALL + 1, QB], I32, b); b += (SMALL + 1) * QB * 4
    diag = at("diag", [P, QB], F32, b); b += QB * 4
    rank = at("rank", [P, NE], F32, b); b += NE * 4
    assert b <= m.rt_at, b
    b = m.rt_at + NT * NE * 4
    rt = {}
    for n in ("e", "p", "q1", "s1", "q2", "s2", "sel"):
        rt[n] = at("rt_" + n, [P, NT, NE], F32, b); b += NT * NE * 4
    r1 = at("rt_r", [P, 8, NT], F32, b); b += 8 * NT * 4
    rt["l"] = m.lt
    m.raw = at("m_raw", [P, NMC, WP], F32, b); b += NMC * WP * 4
    assert b <= nc.sbuf_usable_end, b
    m.comb_rows = nc.dram_tensor("comb_rows", (NE, T), F32, kind="Internal").ap()
    rt_done, exp_done, ct_ps, ct_ready, crow_out, raw_in = (
        sem(n) for n in ("e_rt", "e_exp", "e_ct_ps", "e_ct", "e_crow", "e_w_in"))
    NSTEP = 22
    yh = at("ty_h", [P, KC, T], F32R, m.base)
    m.s = at("s_tok", [P, NT, E], F32, m.base + KC * T * 4)
    names = ("mask_in", "a_zero", "tot_done", "lev_ps", "lev_take", "r_done", "k_done", "ad_put", "kt_ps", "kt_done",
             "u_ps", "st_done", "ty_ps", "tyh_done", "tyl_done", "so_ps", "so_done")
    (mask_in, a_zero, tot_done, lev_ps, lev_take, r_done, k_done, ad_put, kt_ps, kt_done, u_ps, st_done, ty_ps,
     tyh_done, tyl_done, so_ps, so_done) = (sem(n) for n in names)
    HALVES = [1, 2, 4, 8, 16, 32, 64]
    NL = 1 + len(HALVES)

    def group(t, g):
        ct, bb = divmod(g, B)
        return t[:, ct, bb * S:(bb + 1) * S]

    def tot(s, g):
        return group(m.D, g) if s == 1 else TOT[s][:, g, :]

    def lbanks(l, g):
        j = (l * NCH + g) % 4 * 2
        return m.psum[:, j:j + 2, :].rearrange("p b (n q) -> p (b n) q", q=2 * QB)

    with nc.Block() as block:
        @block.sync
        def _(sp):
            sp.dma_start(masks[:], a["masks"]).then_inc(mask_in, 16)
            sp.dma_start(diag[:], a["diag"]).then_inc(mask_in, 16)
            sp.dma_start(rank[:], a["rank"]).then_inc(mask_in, 16)
            for i in range(2):
                c = slice(i * NMC // 2, (i + 1) * NMC // 2)
                sp.dma_start(m.raw[:, c, :], a["experts_w"].rearrange("p (c n) -> p c n", c=NMC)[:, c, :]
                             ).then_inc(raw_in, 16)
            sp.wait_ge(ct_ready, 1)
            sp.dma_start(m.comb_rows, combT[:]).then_inc(crow_out, 16)
            sp.wait_ge(crow_out, 16)
            sp.wait_ge(raw_in, 32)

        @block.gpsimd
        def _(pool):
            n = 0
            for s in (1, 2, 4, 8, 16, 32, 64):
                for g in range(NCH):
                    v = tot(s, g).rearrange("p (n two) -> p n two", two=2)
                    if s > 1:
                        pool.wait_ge(tot_done, n - NCH + 1)
                    nc.gpsimd.tensor_tensor(TOT[2 * s][:, g, :], v[:, :, 0], v[:, :, 1], ALU.mult).then_inc(tot_done, 1)
                    n += 1
                if s == 1:
                    for g in range(NCH):
                        nc.gpsimd.memset(A[g][:], 0.0).then_inc(a_zero, 1)
                for g in range(NCH):
                    k = group(m.K, g).rearrange("p (n two s) -> p n two s", two=2, s=s)
                    t = tot(s, g).rearrange("p (n two) -> p n two", two=2)
                    l = HALVES.index(s) + 1
                    pool.wait_ge(lev_ps, l * NCH + g + 1)
                    if l >= 2:
                        pool.wait_ge(k_done, (l - 2) * NCH + g + 1)
                    nc.gpsimd.tensor_tensor(k[:, :, 0, :], k[:, :, 0, :],
                                            t[:, :, 1].unsqueeze(2).broadcast_to([P, S // (2 * s), s]),
                                            ALU.mult).then_inc(k_done, 1)

        def take_y(act, g):
            act.wait_ge(ty_ps, g + 1)
            ct, bb = divmod(g, B)
            nc.scalar.activation(yh[:, ct, bb * S:(bb + 1) * S], m.psum[:, 2 * (g % 2):2 * (g % 2) + 2, :]
                                 .rearrange("p b c -> p (b c)"), ACT.Copy).then_inc(tyh_done, 1)



        @block.scalar
        def _(act):
            act.wait_ge(rt_done, 2)
            nc.scalar.activation(rt["e"][:], rt["l"][:], ACT.Exp).then_inc(exp_done, 1)
            for g in range(NCH):
                act.wait_ge(a_zero, g + 1)
                act.wait_ge(lev_take, SMALL * NCH + g + 1)
                for q in range(4):
                    r = slice(QB * q, QB * (q + 1))
                    nc.scalar.activation(A[g][r, :, r], AD[g][r, :, :], ACT.Copy).then_inc(ad_put, 1)
            act.wait_ge(ct_ps, 1)
            act.wait_ge(r_done, NL * NCH)
            act.wait_ge(k_done, (NL - 1) * NCH)
            nc.scalar.activation(combT[:], m.psum[0:NE, 0:4, :].rearrange("p b c -> p (b c)"), ACT.Copy
                                 ).then_inc(ct_ready, 1)
            for g in range(NCH):
                act.wait_ge(kt_ps, g + 1)
                if g >= 2:
                    act.wait_ge(u_ps, g - 1)
                nc.scalar.activation(kT[g % 2][:], m.psum[:, 4:6, :].rearrange("p b (n c) -> p (b n) c", c=P),
                                     ACT.Copy).then_inc(kt_done, 1)
                if g >= 1:
                    take_y(act, g - 1)
            take_y(act, NCH - 1)

        def low_y(dve, g):
            dve.wait_ge(tyh_done, g + 1)
            ct, bb = divmod(g, B)
            v = slice(bb * S, (bb + 1) * S)
            nc.vector.tensor_tensor(yl[:, ct, v], m.psum[:, 2 * (g % 2):2 * (g % 2) + 2, :].rearrange("p b c -> p (b c)"),
                                    yh[:, ct, v], ALU.subtract).then_inc(tyl_done, 1)


        @block.vector
        def _(dve):
            dve.wait_ge(mask_in, 48)

            def take_level(l, g):
                k = l * NCH + g
                dve.wait_ge(lev_ps, k + 1)
                ps = lbanks(l, g)
                if l == 0:
                    nc.vector.tensor_tensor(AD[g][:], ps[:, :, 0:QB], diag[:].unsqueeze(1).broadcast_to([P, NS, QB]),
                                            ALU.mult).then_inc(lev_take, 1)
                elif l <= SMALL:
                    dve.wait_ge(lev_take, k - NCH + 1)
                    nc.vector.copy_predicated(AD[g][:], masks[:, l, :].unsqueeze(1).broadcast_to([P, NS, QB]),
                                              ps[:, :, 0:QB]).then_inc(lev_take, 1)
                elif l == SMALL + 1:
                    dve.wait_ge(a_zero, g + 1)
                    nc.vector.tensor_copy(A[g][0:QB, :, QB:2 * QB], ps[0:QB, :, 0:QB])
                    nc.vector.tensor_copy(A[g][2 * QB:3 * QB, :, 3 * QB:], ps[2 * QB:3 * QB, :, 0:QB]
                                          ).then_inc(lev_take, 1)
                else:
                    nc.vector.tensor_copy(A[g][0:2 * QB, :, 2 * QB:], ps[0:2 * QB]).then_inc(lev_take, 1)

            def scale_r(l, g):
                dve.wait_ge(lev_ps, l * NCH + g + 1)
                if l >= 1:
                    dve.wait_ge(r_done, (l - 1) * NCH + g + 1)
                r = group(m.R, g)
                if l == 0:
                    nc.vector.tensor_tensor(r, r, group(m.D, g), ALU.mult).then_inc(r_done, 1)
                    return
                s = HALVES[l - 1]
                if s > 1:
                    dve.wait_ge(tot_done, (l - 2) * NCH + g + 1)
                v = r.rearrange("p (n two s) -> p n two s", two=2, s=s)
                t = tot(s, g).rearrange("p (n two) -> p n two", two=2)
                nc.vector.tensor_tensor(v[:, :, 1, :], v[:, :, 1, :],
                                        t[:, :, 0].unsqueeze(2).broadcast_to([P, S // (2 * s), s]),
                                        ALU.mult).then_inc(r_done, 1)

            def wide(v):
                return v.unsqueeze(2).broadcast_to([P, NT, NE])

            def route(step):
                if step >= 1:
                    dve.wait_ge(rt_done, step)
                if step == 2:
                    dve.wait_ge(exp_done, 1)
                tt, red = nc.vector.tensor_tensor, nc.vector.tensor_reduce
                second = step >= 11
                q, v = (rt["q2"], rt["s2"]) if second else (rt["q1"], rt["s1"])
                left, i = (rt["sel"], 2) if second else (rt["p"], 0)
                if step == 0:
                    ins = red(r1[:, 0, :], rt["l"][:], AX_X, ALU.max)
                elif step == 1:
                    ins = tt(rt["l"][:], rt["l"][:], wide(r1[:, 0, :]), ALU.subtract)
                elif step == 2:
                    ins = red(r1[:, 1, :], rt["e"][:], AX_X, ALU.add)
                elif step == 3:
                    ins = nc.vector.reciprocal(r1[:, 2, :], r1[:, 1, :])
                elif step == 4:
                    ins = tt(rt["p"][:], rt["e"][:], wide(r1[:, 2, :]), ALU.mult)
                elif step in (5, 11):
                    ins = red(r1[:, 3 + i, :], left[:], AX_X, ALU.max)
                elif step in (6, 12):
                    ins = tt(q[:], left[:], wide(r1[:, 3 + i, :]), ALU.is_equal)
                elif step in (7, 13):
                    ins = tt(v[:], q[:], rank[:].unsqueeze(1).broadcast_to([P, NT, NE]), ALU.mult)
                elif step in (8, 14):
                    ins = red(r1[:, 4 + i, :], v[:], AX_X, ALU.max)
                elif step in (9, 15):
                    ins = tt(q[:], v[:], wide(r1[:, 4 + i, :]), ALU.is_equal)
                elif step == 10:
                    ins = nc.vector.scalar_tensor_tensor(rt["sel"][:], q[:], -2.0, rt["p"][:], ALU.mult, ALU.add)
                elif step == 16:
                    ins = tt(rt["e"][:], rt["q1"][:], rt["q2"][:], ALU.add)
                elif step == 17:
                    ins = tt(r1[:, 0, :], r1[:, 3, :], r1[:, 5, :], ALU.add)
                elif step == 18:
                    ins = nc.vector.tensor_scalar(r1[:, 1, :], r1[:, 0, :], 1e-20, None, ALU.add)
                elif step == 19:
                    ins = nc.vector.reciprocal(r1[:, 2, :], r1[:, 1, :])
                elif step == 20:
                    ins = tt(rt["s1"][:], rt["p"][:], rt["e"][:], ALU.mult)
                else:
                    ins = tt(rt["l"][:], rt["s1"][:], wide(r1[:, 2, :]), ALU.mult)
                ins.then_inc(rt_done, 1)

            for l in range(NL):
                for g in range(NCH):
                    scale_r(l, g)
                    take_level(l, g)
                    if l * NCH + g < NSTEP:
                        route(l * NCH + g)
            for g in range(NCH):
                dve.wait_ge(u_ps, g + 1)
                u = bank[6 + g % 2]
                if g >= 2:
                    dve.wait_ge(ty_ps, g - 1)
                if g == 0:
                    dve.wait_ge(tot_done, NCH * len(HALVES))
                nc.vector.tensor_copy(ST[g % 2][:, 1, :], u[:, 0:LD]).then_inc(st_done, 1)
                for c in range(1, NC - 1):
                    dve.wait_ge(st_done, g * (NC - 1) + c)
                    nc.vector.scalar_tensor_tensor(ST[g % 2][:, c + 1, :], ST[g % 2][:, c, :], TOT[128][:, g, c:c + 1],
                                                   u[:, c * LD:(c + 1) * LD], ALU.mult, ALU.add).then_inc(st_done, 1)
                if g >= 1:
                    low_y(dve, g - 1)
            low_y(dve, NCH - 1)
            for n in range(0, NT, 2):
                dve.wait_ge(so_ps, n // 2 + 1)
                nc.vector.tensor_copy(m.s[:, n:n + 2, :], bank[4 + n // 2 % 4].rearrange("p (n e) -> p n e", n=2)
                                      ).then_inc(so_done, 1)

        @block.tensor
        def _(pe):
            def level(l, g):
                k = l * NCH + g
                if k >= 4:
                    pe.wait_ge(lev_take, k - 3)
                if l >= 1:
                    pe.wait_ge(r_done, (l - 1) * NCH + g + 1)
                if l >= 2:
                    pe.wait_ge(k_done, (l - 2) * NCH + g + 1)
                kk, rr, ps = group(m.K, g), group(m.R, g), lbanks(l, g)
                for n in range(NS):
                    h, c = divmod(n, NC)
                    ch = slice(h * LD, (h + 1) * LD)
                    if l <= SMALL:
                        for q in range(4):
                            t = c * CH + q * QB
                            mm = nc.tensor.matmul(ps[QB * q:QB * (q + 1), n, 0:QB], kk[ch, t:t + QB],
                                                  rr[ch, t:t + QB], start=True, stop=True)
                    elif l == SMALL + 1:
                        for q in (0, 2):
                            t = c * CH + q * QB
                            mm = nc.tensor.matmul(ps[QB * q:QB * (q + 1), n, 0:QB], kk[ch, t:t + QB],
                                                  rr[ch, t + QB:t + 2 * QB], start=True, stop=True)
                    else:
                        t = c * CH
                        mm = nc.tensor.matmul(ps[0:2 * QB, n, :],
                                              kk[ch, t:t + 2 * QB], rr[ch, t + 2 * QB:t + CH], start=True, stop=True)
                mm.then_inc(lev_ps, 1)

            def turn_k(g):
                pe.wait_ge(k_done, (NL - 2) * NCH + g + 1)
                if g >= 1:
                    pe.wait_ge(kt_done, g)
                for c in range(NC):
                    mm = nc.tensor.transpose(bank[4 + c // 4][:, c % 4 * P:(c % 4 + 1) * P],
                                             group(m.K, g)[:, c * CH:(c + 1) * CH], m.ident1[:])
                mm.then_inc(kt_ps, 1)

            def update(g):
                ct, bb = divmod(g, B)
                pe.wait_ge(kt_done, g + 1)
                if g >= 2:
                    pe.wait_ge(st_done, (g - 1) * (NC - 1))
                for c in range(NC - 1):
                    for h in range(NH):
                        ch = slice(h * LD, (h + 1) * LD)
                        mm = nc.tensor.matmul(bank[6 + g % 2][ch, c * LD:(c + 1) * LD], kT[g % 2][:, c, ch],
                                              m.V[:, bb * NC + c, ct * P + h * LD:ct * P + (h + 1) * LD],
                                              start=True, stop=True)
                mm.then_inc(u_ps, 1)

            def output(g):
                ct, bb = divmod(g, B)
                pe.wait_ge(st_done, (g + 1) * (NC - 1))
                pe.wait_ge(ad_put, 4 * (g + 1))
                pe.wait_ge(r_done, (NL - 1) * NCH + g + 1)
                if g >= 2:
                    pe.wait_ge(tyl_done, g - 1)
                else:
                    pe.wait_ge(ct_ready, 1)
                for c in range(NC):
                    for h in range(NH):
                        ch = slice(h * LD, (h + 1) * LD)
                        out = m.psum[ch, 2 * (g % 2) + c // 4, c % 4 * CH:(c % 4 + 1) * CH]
                        mm = nc.tensor.matmul(out, m.V[:, bb * NC + c, ct * P + h * LD:ct * P + (h + 1) * LD],
                                              A[g][:, h * NC + c, :], start=True, stop=(c == 0))
                        if c:
                            mm = nc.tensor.matmul(out, ST[g % 2][ch, c, :], group(m.R, g)[ch, c * CH:(c + 1) * CH],
                                                  start=False, stop=True)
                mm.then_inc(ty_ps, 1)

            for l in range(NL):
                for g in range(NCH):
                    level(l, g)
            pe.wait_ge(lev_take, NL * NCH)
            pe.wait_ge(rt_done, NSTEP)
            for n in range(NT):
                mm = nc.tensor.transpose(bank[n // 4][0:NE, n % 4 * P:(n % 4 + 1) * P], rt["l"][:, n, :], m.ident1[:])
            mm.then_inc(ct_ps, 1)
            turn_k(0)
            for g in range(NCH):
                update(g)
                if g + 1 < NCH:
                    turn_k(g + 1)
                output(g)
            pe.wait_ge(tyl_done, NCH)
            for n in range(NT):
                if n >= 8 and n % 2 == 0:
                    pe.wait_ge(so_done, n // 2 - 3)
                tok = slice(n * P, (n + 1) * P)
                mm = three(nc, bank[4 + n // 2 % 4][:, n % 2 * E:(n % 2 + 1) * E],
                           [(yh[:, kc, tok], yl[:, kc, tok], m.woh1[:, kc, :], m.wol1[:, kc, :]) for kc in range(KC)])
                if n % 2:
                    mm.then_inc(so_ps, 1)


def experts_stage(nc, m, a):
    at, sem, bank = m.at, m.sem, m.bank
    b = m.base
    xl = at("x1_l", [P, KC, T], F32R, b); b += KC * T * 4
    b += NT * E * 4
    xh = at("x1_h", [P, KC, T], F32R, b); b += KC * T * 4
    xa = at("m_xa", [P, TPB, E], F32, b); b += TPB * E * 4
    comb = at("comb_b", [P, 4, BLK], F32, b); b += 4 * BLK * 4
    gate = at("m_gate", [P, TPB, E], F32, b); b += TPB * E * 4
    assert b <= m.p3
    b = m.p3
    raw = m.raw
    wl = at("m_l", [P, NMC, WP], F32R, m.rt_at + 9 * NT * NE * 4)
    wh = at("m_h", [P, NMC, WP], F32R, b); b += NMC * WP * 4
    hh = at("m_hh", [P, 3, BLK], F32R, b); b += 3 * BLK * 4
    hl = at("m_hl", [P, 3, BLK], F32R, b); b += 3 * BLK * 4
    sg = at("m_silu", [P, 2, BLK], F32, b); b += 2 * BLK * 4
    hf = at("m_h_f", [P, 3, BLK], F32, b); b += 3 * BLK * 4
    assert b <= m.rt_at + 9 * NT * NE * 4, b
    gs = gate

    names = ("e_xa", "e_t_ps", "e_xh", "e_xl", "e_wh", "e_wl", "e_gu_ps", "e_silu", "e_h", "e_hc", "e_hi", "e_lo",
             "e_down", "e_gate", "e_gs", "e_x", "e_out")
    (xa_ready, t_ps, xh_ready, xl_ready, wh_ready, wl_ready, gu_ps, silu_done, h_done, hc_done, hi_done, lo_done,
     down_done, gate_done, gs_done, x_done, x_out) = (sem(n) for n in names)
    comb_in = [sem(f"comb_in{i}") for i in range(4)]

    ORDER = list(range(NEC, NMC)) + list(range(NEC))
    NX = sum(c < NEC for c in ORDER)
    TURN_AT = 6

    def ncomb(k):
        return k // NMC * NX + sum(c < NEC for c in ORDER[:k % NMC + 1])

    def slot(tb, i):
        return place(tb, i) % 2 * 2

    def place(tb, i):
        return 1 + tb * (NMC + 1) + i + (i >= TURN_AT and tb < NB - 1)

    def turn_place(g):
        return 0 if g == 0 else 1 + (g - 1) * (NMC + 1) + TURN_AT

    WHAT = {}
    for tb in range(NB):
        WHAT[turn_place(tb)] = ("x", tb)
        for i in range(NMC):
            WHAT[place(tb, i)] = ("h", tb * NMC + i)

    def wgu(t, w, kc, c):
        i = (2 * w + kc) * P
        return t[:, c, i:i + P]

    with nc.Block() as block:
        def store(sp, tb):
            sp.wait_ge(x_done, tb + 1)
            ts = slice(tb * TPB, (tb + 1) * TPB)
            sp.dma_start(a["out"].rearrange("(n p) f -> p n f", p=P)[:, ts, :], m.x[:, ts, :]).then_inc(x_out, 16)

        @block.sync
        def _(sp):
            for tb in range(NB):
                for c in range(NEC):
                    j = tb * NEC + c
                    if j >= 4:
                        sp.wait_ge(hc_done, j - 3)
                    lo = c * P
                    while lo < (c + 1) * P:
                        e = lo // EI
                        hi = min((c + 1) * P, (e + 1) * EI)
                        sp.dma_start(comb[lo - c * P:hi - c * P, j % 4, :],
                                     m.comb_rows[e:e + 1, tb * BLK:(tb + 1) * BLK].broadcast_to([hi - lo, BLK])
                                     ).then_inc(comb_in[j % 4], 16)
                        lo = hi
                if tb >= 1:
                    store(sp, tb - 1)
            store(sp, NB - 1)
            sp.wait_ge(x_out, 16 * NB)

        def pieces_in(j):
            def count(i):
                c = i % NEC
                return (c * P + P - 1) // EI - c * P // EI + 1
            return sum(count(i) for i in range(j % 4, j + 1, 4))

        @block.gpsimd
        def _(pool):
            for tb in range(NB):
                for c in ORDER:
                    if c >= NEC:
                        continue
                    j = tb * NEC + c
                    k = tb * NMC + ORDER.index(c)
                    pool.wait_ge(comb_in[j % 4], 16 * pieces_in(j))
                    pool.wait_ge(h_done, k + 1)
                    nc.gpsimd.tensor_tensor(hf[:, k % 3, :], hf[:, k % 3, :], comb[:, j % 4, :],
                                            ALU.mult).then_inc(hc_done, 1)

        @block.scalar
        def _(act):
            def high(k):
                act.wait_ge(h_done, k + 1)
                if ORDER[k % NMC] < NEC:
                    act.wait_ge(hc_done, ncomb(k))
                if k >= 3:
                    act.wait_ge(down_done, k - 2)
                nc.scalar.activation(hh[:, k % 3, :], hf[:, k % 3, :], ACT.Copy).then_inc(hi_done, 1)

            def high_x(g):
                s = turn_place(g) % 2 * 2
                for kc in range(KC):
                    act.wait_ge(t_ps, g * KC + kc + 1)
                    nc.scalar.activation(xh[:, kc, g * BLK:(g + 1) * BLK], bank[s + kc], ACT.Copy).then_inc(xh_ready, 1)

            def high_w(i):
                nc.scalar.activation(wh[:, ORDER[i], :], raw[:, ORDER[i], :], ACT.Copy).then_inc(wh_ready, 1)

            high_w(0)
            high_x(0)
            high_w(1)
            for tb in range(NB):
                for i in range(NMC):
                    k = tb * NMC + i
                    if i == TURN_AT and tb + 1 < NB:
                        high_x(tb + 1)
                    act.wait_ge(gu_ps, k + 1)
                    if k >= 2:
                        act.wait_ge(h_done, k - 1)
                    nc.scalar.activation(sg[:, k % 2, :], bank[slot(tb, i)], ACT.Silu).then_inc(silu_done, 1)
                    if i >= 1:
                        high(k - 1)
                    if tb == 0 and i + 2 < NMC:
                        high_w(i + 2)
                high(tb * NMC + NMC - 1)
                act.wait_ge(down_done, (tb + 1) * NMC)
                if tb >= 1:
                    act.wait_ge(x_done, tb)
                nc.scalar.activation(gate[:], m.psum[:, 4:8, 0:E], ACT.Silu).then_inc(gate_done, 1)

        @block.vector
        def _(dve):
            def norm(g):
                if g >= 1:
                    dve.wait_ge(t_ps, KC * g)
                for j in range(TPB):
                    n = g * TPB + j
                    nc.vector.tensor_scalar(xa[:, j, :], m.x[:, n, :], m.mv1[:, n, 0:1], m.rstd1[:, n:n + 1],
                                            ALU.subtract, ALU.mult).then_inc(xa_ready, 1)

            def low_x(g):
                cols = slice(g * BLK, (g + 1) * BLK)
                s = turn_place(g) % 2 * 2
                for kc in range(KC):
                    dve.wait_ge(xh_ready, g * KC + kc + 1)
                    nc.vector.tensor_tensor(xl[:, kc, cols], bank[s + kc], xh[:, kc, cols],
                                            ALU.subtract).then_inc(xl_ready, 1)

            def low_w(i):
                dve.wait_ge(wh_ready, i + 1)
                c = ORDER[i]
                nc.vector.tensor_tensor(wl[:, c, :], raw[:, c, :], wh[:, c, :], ALU.subtract).then_inc(wl_ready, 1)

            def low_h(k):
                dve.wait_ge(hi_done, k + 1)
                if k >= 3:
                    dve.wait_ge(down_done, k - 2)
                nc.vector.tensor_tensor(hl[:, k % 3, :], hf[:, k % 3, :], hh[:, k % 3, :],
                                        ALU.subtract).then_inc(lo_done, 1)

            norm(0)
            low_w(0)
            low_x(0)
            low_w(1)
            for tb in range(NB):
                for i in range(NMC):
                    k = tb * NMC + i
                    if i == TURN_AT and tb + 1 < NB:
                        low_x(tb + 1)
                    dve.wait_ge(silu_done, k + 1)
                    if k >= 3:
                        dve.wait_ge(lo_done, k - 2)
                    nc.vector.tensor_tensor(hf[:, k % 3, :], bank[slot(tb, i) + 1], sg[:, k % 2, :],
                                            ALU.mult).then_inc(h_done, 1)
                    if k >= 1 and i >= 1:
                        low_h(k - 1)
                    if tb == 0 and i + 2 < NMC:
                        low_w(i + 2)
                    if i == TURN_AT - 3 and tb + 1 < NB:
                        norm(tb + 1)
                low_h(tb * NMC + NMC - 1)
                ts = slice(tb * TPB, (tb + 1) * TPB)
                dve.wait_ge(gate_done, tb + 1)
                nc.vector.tensor_tensor(gs[:], gate[:], m.s[:, ts, :], ALU.mult).then_inc(gs_done, 1)
                dve.wait_ge(gs_done, tb + 1)
                nc.vector.tensor_tensor(m.x[:, ts, :], m.x[:, ts, :], gs[:], ALU.add).then_inc(x_done, 1)

        @block.tensor
        def _(pe):
            def slot_free(q):
                if q >= 2:
                    what, k = WHAT[q - 2]
                    if what == "x":
                        pe.wait_ge(xl_ready, KC * (k + 1))
                    else:
                        pe.wait_ge(h_done, k + 1)
                return q % 2 * 2

            def turn(g):
                s = slot_free(turn_place(g))
                pe.wait_ge(xa_ready, TPB * (g + 1))
                for kc in range(KC):
                    for i in range(TPB):
                        mm = nc.tensor.transpose(bank[s + kc][:, i * P:(i + 1) * P], xa[:, i, kc * P:(kc + 1) * P],
                                                 m.ident1[:])
                    mm.then_inc(t_ps, 1)

            def up(tb, i):
                c = ORDER[i]
                cols = slice(tb * BLK, (tb + 1) * BLK)
                s = slot_free(place(tb, i))
                if tb == 0:
                    pe.wait_ge(wl_ready, i + 1)
                if i == 0:
                    pe.wait_ge(xl_ready, KC * (tb + 1))
                for w in range(2):
                    mm = three(nc, bank[s + w], [(wgu(wh, w, kc, c), wgu(wl, w, kc, c), xh[:, kc, cols], xl[:, kc, cols])
                                                 for kc in range(KC)])
                mm.then_inc(gu_ps, 1)

            def down(tb, i):
                c = ORDER[i]
                k = tb * NMC + i
                pe.wait_ge(lo_done, k + 1)
                if i == 0 and tb >= 1:
                    pe.wait_ge(gate_done, tb)
                for j in range(TPB):
                    tok = slice(j * P, (j + 1) * P)
                    mm = three(nc, bank[4 + j][:, 0:E], [(hh[:, k % 3, tok], hl[:, k % 3, tok],
                                                          wh[:, c, 4 * P:], wl[:, c, 4 * P:])],
                               start=(i == 0), stop=(i == NMC - 1))
                mm.then_inc(down_done, 1)

            turn(0)
            for tb in range(NB):
                for i in range(NMC):
                    if i == TURN_AT and tb + 1 < NB:
                        turn(tb + 1)
                    up(tb, i)
                    if i >= 2:
                        down(tb, i - 2)
                down(tb, NMC - 2)
                down(tb, NMC - 1)


def kernel(**inputs):
    import numpy as np
    import concourse.bacc as bacc
    from concourse.bass_utils import run_bass_kernel_spmd

    i = {n: np.asarray(v) for n, v in inputs.items()}

    def rows(*arrays):
        return np.concatenate(arrays, 0)

    def columns(v):
        return v.reshape(KC, P).T

    q_rows = [(u * HALF + d) * HEADS + h for u in range(2) for h in range(HEADS) for d in range(HALF)]
    k_rows, k_rows_turned = ([((u + turn) % 2 * HALF + d) * KV + kv for u in range(2) for kv in range(KV)
                              for d in range(HALF)] for turn in range(2))
    v_rows = [d * KV + kv for kv in range(KV) for d in range(HD)]

    freq = np.float32(1.0) / np.float32(10000.0) ** (np.arange(HALF, dtype=np.float32) * np.float32(2.0) / np.float32(HD))
    angle = np.arange(S, dtype=np.float32)[:, None] * freq[None, :]
    cos = np.tile(np.cos(angle).T, (P // HALF, 1))
    sin = np.tile(np.sin(angle).T, (P // HALF, 1))
    sin_k = sin.copy()
    sin_k[:P // 2] *= -1
    masks = np.zeros((P, SMALL + 1, QB), np.int32)
    u, t = (np.arange(P) % QB)[:, None], np.arange(QB)[None, :]
    for level in range(SMALL):
        h = 1 << level
        masks[:, level + 1, :] = (u // (2 * h) == t // (2 * h)) & (u % (2 * h) < h) & (t % (2 * h) >= h)

    def gap(v, n):
        return np.zeros((n, v.shape[1]), v.dtype)

    down_idx = i["L0_ffn_down_idx"].T
    pad = NMC * P - MI
    pieces = []
    for name in ("gate", "up"):
        w = rows(i[f"L1_ffn_expert_{name}"].reshape(NE * EI, E), i[f"L1_ffn_shared_{name}"])
        w = rows(w, gap(w, pad)).T.reshape(KC, P, NMC, P)
        pieces += [w[kc] for kc in range(KC)]
    w = rows(i["L1_ffn_expert_down"].transpose(0, 2, 1).reshape(NE * EI, E), i["L1_ffn_shared_down"].T)
    pieces.append(rows(w, gap(w, pad)).reshape(NMC, P, E).transpose(1, 0, 2))
    experts_w = np.concatenate(pieces, 2).reshape(P, NMC * WP)
    arrays = dict(
        x=i["L0_attn_x"].reshape(T, E), ident=np.eye(P, dtype=np.float32),
        wqkv=rows(i["L0_attn_W_Q"][q_rows], i["L0_attn_W_K"][k_rows], i["L0_attn_W_K"][k_rows_turned],
                  i["L0_attn_W_V"][v_rows]).T,
        cos=cos, sin=sin, sink=sin_k, wo=i["L0_attn_W_O"].T, lut=i["L0_ffn_lut"],
        gu_idx=rows(i["L0_ffn_gate_idx"], i["L0_ffn_up_idx"]).T,
        down_idx=rows(down_idx, gap(down_idx, NI * P - INTER)),
        wx_t=i["L1_attn_Wx"].T, ww=i["L1_attn_Ww"], wk=i["L1_attn_Wk"], wr=i["L1_attn_Wr"], wv=i["L1_attn_Wv"],
        wout=i["L1_attn_Wout"], gamma=columns(i["L1_attn_gamma"]), beta=columns(i["L1_attn_beta"]),
        bw=columns(i["L1_attn_bw"]), masks=masks, diag=(u == t).astype(np.float32),
        gate_w_t=i["L1_ffn_gate_w"].T, rank=np.tile(np.arange(NE, 0, -1, dtype=np.float32), (P, 1)), experts_w=experts_w)
    arrays = {n: np.ascontiguousarray(v) for n, v in arrays.items()}

    nc = bacc.Bacc("TRN2", target_bir_lowering=False, num_devices=1)
    a = {n: nc.dram_tensor(n, v.shape, mybir.dt.from_np(v.dtype), kind="ExternalInput").ap()
         for n, v in arrays.items()}
    a["out"] = nc.dram_tensor("out", (T, E), F32, kind="ExternalOutput").ap()
    program(nc, a)
    result = run_bass_kernel_spmd(nc, [arrays], core_ids=[0])
    return result.results[0]["out"].reshape(B, S, E)
```

```python
from contextlib import ExitStack

import concourse.bass as bass
from concourse import mybir

F32 = mybir.dt.float32
F32R = mybir.dt.float32r
BF16 = mybir.dt.bfloat16
I32 = mybir.dt.int32
ALU = mybir.AluOpType
ACT = mybir.ActivationFunctionType
AX_X = mybir.AxisListType.X
AX_XY = mybir.AxisListType.XY

P = 128
B, S, E = 2, 1024, 256
T = B * S
NT = T // P
KC = E // P
BLK = 512
NB = T // BLK
TPB = BLK // P

HEADS, G, HD = 16, 2, 16
KV = HEADS // G
HALF = HD // 2
SLOTS = ((0, 1), (0, 2), (0, 0), (1, 0), (2, 0), (1, 1))
Q_SLOTS = (slice(0, 3), slice(3, 6, 2), slice(4, 5))
K_SLOTS = (slice(2, 5), slice(0, 6, 5), slice(1, 2))
NROW = HD * len(SLOTS)
NAUG = NROW + 3
VW = 32

INTER = 688
LUT = 16
NI = (INTER + P - 1) // P

EPS = 1e-5

NE, EI, SI = 8, 176, 352
MI = NE * EI + SI
NEC = NE * EI // P
NMC = (MI + P - 1) // P
ORDER = list(range(NEC, NMC)) + list(range(NEC))
WP = 4 * P + E



class Mem:
    pass


def parts(n, size):
    return [(i, min(size, n - i)) for i in range(0, n, size)]


def program(nc, a):
    with ExitStack() as ctx:
        m = Mem()
        off = [16512]

        def at(name, shape, dt, offset):
            return nc.alloc_sbuf_tensor_at(name, shape, dt, offset=offset)

        def sem(name):
            return ctx.enter_context(nc.semaphore(name))

        m.at, m.sem = at, sem
        m.psum = ctx.enter_context(nc.psum_tensor("psum", [P, 8, BLK], F32))
        m.bank = [m.psum[:, i, :] for i in range(8)]
        base = 16512
        m.x = at("x_tok", [P, NT, E], F32, base)
        m.base = base + NT * E * 4
        b = m.base
        m.xTh = at("xTh", [P, KC, T], F32R, b)
        m.xTl = at("xTl", [P, KC, T], F32R, b + KC * T * 4)
        b += 2 * KC * T * 4
        m.ident = at("ident", [P, P], F32, b)
        m.rstd = at("rstd", [P, NT], F32, b + 512)
        m.mv = at("mv", [P, NT, 2], F32, b + 640)
        b += 1024
        m.l0 = b
        m.q_rows = nc.dram_tensor("q_rows", (len(SLOTS), 2, HEADS, HALF, T), BF16, kind="Internal").ap()
        m.k_rows = nc.dram_tensor("k_rows", (len(SLOTS), 2, KV, HALF, T), BF16, kind="Internal").ap()
        m.m_rows = nc.dram_tensor("m_rows", (B * KV, 3, G * S), BF16, kind="Internal").ap()
        m.den_rows = nc.dram_tensor("den_rows", (B * KV, G * S), F32, kind="Internal").ap()
        m.rec_rows = nc.dram_tensor("rec_rows", (B * KV, G * S), F32, kind="Internal").ap()
        qkv_stage(nc, m, a)
        attention_stage(nc, m, a)
        ffn_stage(nc, m, a)
        time_mix_in_stage(nc, m, a)
        time_mix_stage(nc, m, a)
        experts_stage(nc, m, a)


def qkv_stage(nc, m, a):
    at, sem, bank = m.at, m.sem, m.bank
    b = m.l0
    m.VS = at("VS", [P, NT, KV, VW], F32, b); b += NT * KV * VW * 4
    m.wo = at("wo_raw", [P, KC, E], F32, b); b += KC * E * 4
    m.p0 = b
    NQ = E + 2 * P + P
    wraw = at("wqkv_raw", [P, KC, NQ], F32, b); b += KC * NQ * 4
    wh = at("wqkv_h", [P, KC, NQ], F32R, b); b += KC * NQ * 4
    wl = at("wqkv_l", [P, KC, NQ], F32R, b); b += KC * NQ * 4
    cos = at("cos", [P, S], F32, b); b += S * 4
    sin = at("sin", [P, S], F32, b); b += S * 4
    sink = at("sink", [P, S], F32, b); b += S * 4
    xn = at("xn", [P, 2, TPB, E], F32, b); b += 2 * TPB * E * 4
    prod = at("rope_prod", [P, 6, BLK], F32, b); b += 6 * BLK * 4
    rot = at("rotated", [P, 3, BLK], F32, b); b += 3 * BLK * 4
    res = at("residue", [P, 3, BLK], F32, b); b += 3 * BLK * 4
    st = at("bn_st", [P, NT, 6], F32, b); b += NT * 6 * 4
    ve = at("var_eps", [P, NT], F32, b); b += NT * 4
    mhalf = at("minus_half", [P, TPB], F32, b); b += 32
    assert b <= nc.sbuf_usable_end, b

    x_in = [sem(f"x_in{g}") for g in range(NB)]
    w_in, tab_in, id_in, wo_in = sem("w_in"), sem("tab_in"), sem("id_in"), sem("wo_in")
    w_ready, stats, var_ready, rstd_ready = sem("w_ready"), sem("stats"), sem("var_ready"), sem("rstd_ready")
    const_ready, xn_ready, xt_ps, xt_hi, xt_lo = sem("const_ready"), sem("xn_ready"), sem("xt_ps"), sem("xt_hi"), sem("xt_lo")
    q_ps, k_ps, v_ps, v_out = sem("q_ps"), sem("k_ps"), sem("v_ps"), sem("v_out")
    prod_q, prod_k, rot_ready, part1, resid, part2, part3 = (
        sem(n) for n in ("prod_q", "prod_k", "rot_ready", "part1", "resid", "part2", "part3"))
    part_out = m.part_out = [sem("part_out0"), sem("part_out1")]
    m.qk_in = [sem(f"qk_in{i}") for i in range(3)]
    m.NLUT = KC * 2 * INTER + NI * E
    m.NPIECE = 4
    m.PIECE = m.NLUT // m.NPIECE
    m.qk_at = nc.sbuf_usable_end // 32 * 32 - 3 * (G + 1) * S * 2
    m.QS = [at(f"QS{i}", [NAUG, G * S], BF16, m.qk_at + i * G * S * 2) for i in range(3)]
    m.KS = [at(f"KS{i}", [NAUG, S], BF16, m.qk_at + 3 * G * S * 2 + i * S * 2) for i in range(3)]
    part_at = m.qk_at - 18 * BLK * 2
    assert b <= part_at, b
    part = at("part", [P, 2, 3, 3, BLK], BF16, part_at)

    def load_qk(sp, n):
        bb, kv = divmod(n, KV)
        if n >= 3:
            sp.wait_ge(m.s_ps, (n - 2) * (S // P) * (G * S // BLK))
        seq = slice(bb * S, (bb + 1) * S)
        sp.dma_start(m.KS[n % 3][0:NROW, :],
                     m.k_rows[:, :, kv, :, seq].rearrange("s u d t -> (s u) d t")).then_inc(m.qk_in[n % 3], 16)
        for g in range(G):
            sp.dma_start(m.QS[n % 3][0:NROW, g * S:(g + 1) * S],
                         m.q_rows[:, :, kv * G + g, :, seq].rearrange("s u d t -> (s u) d t")
                         ).then_inc(m.qk_in[n % 3], 16)

    m.load_qk = load_qk
    wh_ready = sem("wh_ready")

    def block_out(sp, tb):
        cols = slice(tb * BLK, (tb + 1) * BLK)
        for i in range(3):
            for u in range(3):
                if i == 0:
                    sp.wait_ge(part1, 3 * tb + u + 1)
                elif i == 1:
                    sp.wait_ge(part2, 3 * tb + u + 1)
                else:
                    sp.wait_ge(part3, 3 * tb + u + 1)
                if u < 2:
                    dst = m.q_rows[Q_SLOTS[i], u, :, :, cols].rearrange("s h d t -> (h d) s t")
                else:
                    dst = m.k_rows[K_SLOTS[i], :, :, :, cols].rearrange("s u h d t -> (u h d) s t")
                src = part[:, tb % 2, u, i, :].unsqueeze(1).broadcast_to([P, dst.shape[1], BLK])
                sp.dma_start(dst, src).then_inc(part_out[tb % 2], 16)

    def cut(act, tb):
        for u in range(3):
            act.wait_ge(rot_ready, 3 * tb + u + 1)
            if tb >= 2:
                act.wait_ge(part_out[tb % 2], 16 * 9 * (tb // 2))
            nc.scalar.activation(part[:, tb % 2, u, 0, :], rot[:, u, :], ACT.Copy).then_inc(part1, 1)
        for u in range(3):
            act.wait_ge(resid, 3 * tb + u + 1)
            nc.scalar.activation(part[:, tb % 2, u, 1, :], res[:, u, :], ACT.Copy).then_inc(part2, 1)

    def take_v(act, tb):
        act.wait_ge(v_ps, tb + 1)
        act.wait_ge(const_ready, 2)
        for i in range(TPB):
            nc.scalar.activation(m.VS[:, tb * TPB + i, :, 0:HD],
                                 bank[2 + tb % 2][:, i * P:(i + 1) * P].rearrange("p (k d) -> p k d", k=KV),
                                 ACT.Copy).then_inc(v_out, 1)

    def third_parts(pool, tb):
        for u in range(3):
            pool.wait_ge(part2, 3 * tb + u + 1)
            nc.gpsimd.tensor_tensor(part[:, tb % 2, u, 2, :], res[:, u, :], part[:, tb % 2, u, 1, :],
                                    ALU.subtract).then_inc(part3, 1)

    def rope(dve, tb):
        pos = slice((tb % (S // BLK)) * BLK, (tb % (S // BLK) + 1) * BLK)
        if tb == 0:
            dve.wait_ge(tab_in, 48)
        if tb >= 1:
            dve.wait_ge(rot_ready, 3 * tb)
        dve.wait_ge(q_ps, tb + 1)
        nc.vector.tensor_tensor(prod[:, 0, :], bank[4][:], cos[:, pos], ALU.mult).then_inc(prod_q, 1)
        nc.vector.tensor_tensor(prod[:, 1, :], bank[5][:], sin[:, pos], ALU.mult).then_inc(prod_q, 1)
        nc.vector.tensor_tensor(prod[:, 2, :], bank[5][:], cos[:, pos], ALU.mult).then_inc(prod_q, 1)
        nc.vector.tensor_tensor(prod[:, 3, :], bank[4][:], sin[:, pos], ALU.mult).then_inc(prod_q, 1)
        dve.wait_ge(k_ps, tb + 1)
        nc.vector.tensor_tensor(prod[:, 4, :], bank[6][:], cos[:, pos], ALU.mult).then_inc(prod_k, 1)
        nc.vector.tensor_tensor(prod[:, 5, :], bank[7][:], sink[:, pos], ALU.mult).then_inc(prod_k, 1)
        if tb >= 1:
            dve.wait_ge(part1, 3 * tb)
            dve.wait_ge(resid, 3 * tb)
        dve.wait_ge(prod_q, 4 * tb + 4)
        nc.vector.tensor_tensor(rot[:, 0, :], prod[:, 0, :], prod[:, 1, :], ALU.subtract).then_inc(rot_ready, 1)
        nc.vector.tensor_tensor(rot[:, 1, :], prod[:, 2, :], prod[:, 3, :], ALU.add).then_inc(rot_ready, 1)
        dve.wait_ge(prod_k, 2 * tb + 2)
        nc.vector.tensor_tensor(rot[:, 2, :], prod[:, 4, :], prod[:, 5, :], ALU.add).then_inc(rot_ready, 1)
        for u in range(3):
            dve.wait_ge(part1, 3 * tb + u + 1)
            if tb >= 1:
                dve.wait_ge(part3, 3 * (tb - 1) + u + 1)
            nc.vector.tensor_tensor(res[:, u, :], rot[:, u, :], part[:, tb % 2, u, 0, :],
                                    ALU.subtract).then_inc(resid, 1)

    m.block_out, m.cut, m.take_v, m.third_parts, m.rope = block_out, cut, take_v, third_parts, rope
    m.v_out, m.prod_q, m.prod_k = v_out, prod_q, prod_k

    with nc.Block() as block:
        @block.sync
        def _(sp):
            for g in range(NB):
                sp.dma_start(m.x[:, g * TPB:(g + 1) * TPB, :],
                             a["x"].rearrange("(n p) f -> p n f", p=P)[:, g * TPB:(g + 1) * TPB, :]).then_inc(x_in[g], 16)
            sp.dma_start(cos[:], a["cos"]).then_inc(tab_in, 16)
            sp.dma_start(sin[:], a["sin"]).then_inc(tab_in, 16)
            sp.dma_start(sink[:], a["sink"]).then_inc(tab_in, 16)
            sp.dma_start(m.wo[:], a["wo"].rearrange("(c p) n -> p c n", p=P)).then_inc(wo_in, 16)
            for tb in range(NB - 2):
                block_out(sp, tb)
                if tb == S // BLK - 1:
                    for i in range(2):
                        sp.wait_ge(part_out[i], 16 * 9 * (tb + 1) // 2)
                    for n in range(3):
                        load_qk(sp, n)
            sp.wait_ge(wo_in, 16)

        @block.scalar
        def _(act):
            act.dma_start(m.ident[:], a["ident"]).then_inc(id_in, 16)
            act.dma_start(wraw[:], a["wqkv"].rearrange("(c p) n -> p c n", p=P)).then_inc(w_in, 16)
            act.wait_ge(w_in, 16)
            nc.scalar.activation(wh[:], wraw[:], ACT.Copy).then_inc(wh_ready, 1)

            def take_xt(g):
                for kc in range(KC):
                    act.wait_ge(xt_ps, g * KC + kc + 1)
                    nc.scalar.activation(m.xTh[:, kc, g * BLK:(g + 1) * BLK], bank[kc][:], ACT.Copy).then_inc(xt_hi, 1)

            for g in range(NB):
                take_xt(g)
                if g >= 1:
                    take_v(act, g - 1)
                    cut(act, g - 1)

        @block.gpsimd
        def _(pool):
            nc.gpsimd.memset(mhalf[:], -0.5).then_inc(const_ready, 1)
            nc.gpsimd.memset(m.VS[:], 1.0).then_inc(const_ready, 1)
            for g in range(NB):
                pool.wait_ge(const_ready, 1)
                pool.wait_ge(var_ready, g + 1)
                nc.gpsimd.tensor_tensor(m.rstd[:, g * TPB:(g + 1) * TPB], ve[:, g * TPB:(g + 1) * TPB], mhalf[:],
                                        ALU.pow).then_inc(rstd_ready, 1)
                if g == 1:
                    pool.wait_ge(wh_ready, 1)
                    nc.gpsimd.tensor_tensor(wl[:], wraw[:], wh[:], ALU.subtract).then_inc(w_ready, 1)
                if g >= 2:
                    third_parts(pool, g - 2)

        @block.vector
        def _(dve):
            def norm(g):
                dve.wait_ge(x_in[g], 16)
                for i in range(g * TPB, (g + 1) * TPB):
                    nc.vector.bn_stats(st[:, i, :], m.x[:, i, :]).then_inc(stats, 1)
                dve.wait_ge(stats, (2 * g + 1) * TPB)
                for i in range(g * TPB, (g + 1) * TPB):
                    nc.vector.bn_aggr(m.mv[:, i, :], st[:, i, :]).then_inc(stats, 1)
                dve.wait_ge(stats, (2 * g + 2) * TPB)
                nc.vector.tensor_scalar(ve[:, g * TPB:(g + 1) * TPB], m.mv[:, g * TPB:(g + 1) * TPB, 1], EPS, None,
                                        ALU.add).then_inc(var_ready, 1)
                dve.wait_ge(rstd_ready, g + 1)
                if g >= 2:
                    dve.wait_ge(xt_ps, KC * (g - 1))
                for i in range(TPB):
                    n = g * TPB + i
                    nc.vector.tensor_scalar(xn[:, g % 2, i, :], m.x[:, n, :], m.mv[:, n, 0:1], m.rstd[:, n:n + 1],
                                            ALU.subtract, ALU.mult).then_inc(xn_ready, 1)

            def low(g):
                for kc in range(KC):
                    dve.wait_ge(xt_hi, g * KC + kc + 1)
                    cols = slice(g * BLK, (g + 1) * BLK)
                    nc.vector.tensor_tensor(m.xTl[:, kc, cols], bank[kc][:], m.xTh[:, kc, cols],
                                            ALU.subtract).then_inc(xt_lo, 1)

            norm(0)
            norm(1)
            low(0)
            for g in range(NB):
                if g + 1 < NB:
                    low(g + 1)
                if g + 2 < NB:
                    norm(g + 2)
                if g + 1 < NB:
                    rope(dve, g)

        @block.tensor
        def _(pe):
            pe.wait_ge(id_in, 16)

            def turn(g):
                pe.wait_ge(xn_ready, TPB * (g + 1))
                for kc in range(KC):
                    if g >= 1:
                        pe.wait_ge(xt_lo, (g - 1) * KC + kc + 1)
                    for i in range(TPB):
                        mm = nc.tensor.transpose(bank[kc][:, i * P:(i + 1) * P], xn[:, g % 2, i, kc * P:(kc + 1) * P],
                                                 m.ident[:])
                    mm.then_inc(xt_ps, 1)

            def project(tb):
                cols = slice(tb * BLK, (tb + 1) * BLK)
                pe.wait_ge(xt_lo, KC * (tb + 1))
                if tb == 0:
                    pe.wait_ge(w_ready, 1)
                for j in range(4):
                    if tb >= 1 and j == 0:
                        pe.wait_ge(prod_q, 4 * tb)
                    if tb >= 1 and j == 2:
                        pe.wait_ge(prod_k, 2 * tb)
                    mm = three(nc, bank[4 + j][:], [(wh[:, kc, j * P:(j + 1) * P], wl[:, kc, j * P:(j + 1) * P],
                                                     m.xTh[:, kc, cols], m.xTl[:, kc, cols]) for kc in range(KC)])
                    if j == 1:
                        mm.then_inc(q_ps, 1)
                    if j == 3:
                        mm.then_inc(k_ps, 1)
                if tb >= 2:
                    pe.wait_ge(v_out, TPB * (tb - 1))
                for i in range(TPB):
                    tok = slice(tb * BLK + i * P, tb * BLK + (i + 1) * P)
                    mm = three(nc, bank[2 + tb % 2][:, i * P:(i + 1) * P],
                               [(m.xTh[:, kc, tok], m.xTl[:, kc, tok], wh[:, kc, 4 * P:], wl[:, kc, 4 * P:])
                                for kc in range(KC)])
                mm.then_inc(v_ps, 1)

            turn(0)
            for g in range(NB):
                if g + 1 < NB:
                    turn(g + 1)
                project(g)


def three(nc, out, operands, start=True, stop=True):
    n = len(operands)
    for i, (lh, ll, rh, rl) in enumerate(operands):
        nc.tensor.matmul(out, ll, rh, start=start and i == 0, stop=False)
        nc.tensor.matmul(out, lh, rl, start=False, stop=False)
        mm = nc.tensor.matmul(out, lh, rh, start=False, stop=stop and i == n - 1)
    return mm


def attention_stage(nc, m, a):
    at, sem, bank = m.at, m.sem, m.bank
    NG = B * KV
    NTT = S // P
    NJ = G * S // BLK
    NST = G * S // P
    b = m.p0
    QS, KS, qk_in, load_qk = m.QS, m.KS, m.qk_in, m.load_qk
    wtmp = at("lut_tmp", [P, 3, m.PIECE], F32, b); b += 3 * m.PIECE * 4
    b = max(b, m.p0 + 18432)
    NPT = 2 * NJ
    pt = at("probs_t", [P, NPT, BLK], F32, b); b += NPT * BLK * 4
    osb = at("o_sb", [P, 2, BLK], F32, b); b += 2 * BLK * 4
    m.ctxT = at("ctxT", [P, KC, T], F32, b); b += KC * T * 4
    m.after_ctx = b
    rec = at("rec_b", [P, 2, S], F32, b); b += 2 * S * 4
    mx = at("row_max", [P, 2, 32], F32, b); b += 2 * 32 * 4
    mT = at("row_max_t", [P, 32], F32, b); b += 32 * 4
    mres = at("max_res", [P, 2, 32], F32, b); b += 2 * 32 * 4
    mpt = at("max_parts", [P, 3, 32], BF16, b); b += 3 * 32 * 2
    den = at("den", [P, NST], F32, b); b += NST * 4
    rden = at("rden", [P, NST], F32, b); b += NST * 4
    m.p1 = b
    NLUT, NPIECE, PIECE = m.NLUT, m.NPIECE, m.PIECE
    idx = at("lut_idx", [P, NLUT], I32, b)
    m.fl = at("ffn_l", [P, NLUT], F32R, b); b += NLUT * 4
    m.fh = at("ffn_h", [P, NLUT], F32R, b); b += NLUT * 4
    m.woh = at("wo_h", [P, KC, E], F32R, b); b += KC * E * 4
    m.wol = at("wo_l", [P, KC, E], F32R, b); b += KC * E * 4
    m.w1 = b
    wsum = at("lut_sum", [P, NLUT], F32, b); b += NLUT * 4
    lut = at("lut", [P, LUT], F32, b); b += LUT * 4
    assert b <= m.qk_at, b
    lut_in, idx_in, lut_prod, lut_add, f_hi, f_lo = (
        sem(n) for n in ("lut_in", "idx_in", "lut_prod", "lut_add", "f_hi", "f_lo"))

    ones_ready, mx_zero = sem("ones_ready"), sem("mx_zero")
    max_ps, max_done, mt_done, mp_done, mp_out, m_in = (
        sem(n) for n in ("max_ps", "max_done", "mt_done", "mp_done", "mp_out", "m_in"))
    m.s_ps = sem("s_ps")
    s_ps, p_ready, pv_done, o_done = m.s_ps, sem("p_ready"), sem("pv_done"), sem("o_done")
    o_out, den_out, den_in, rden_ready, rden_out, rec_in, norm_done = (
        sem(n) for n in ("o_out", "den_out", "den_in", "rden_ready", "rden_out", "rec_in", "norm_done"))
    mres_done = sem("mres_done")
    AHEAD = NST // 2
    MX = [bank[0:2], bank[2:4]]
    SP = bank[4:7]
    OB = bank[7]
    def ring(i):
        return SP[i % 3]

    def leave(sp, n):
        bb, kv = divmod(n, KV)
        sp.wait_ge(o_done, n + 1)
        ct, r = kv // 4, kv % 4 * G * HD
        sp.dma_start(m.den_rows[n].rearrange("(j s) -> j s", j=NJ),
                     osb[HD:P:32, n % 2, :]).then_inc(den_out, 16)
        for j in range(NJ):
            g, half = divmod(j, NJ // G)
            sp.dma_start(m.ctxT[r + g * HD:r + (g + 1) * HD, ct,
                                bb * S + half * BLK:bb * S + (half + 1) * BLK],
                         osb[32 * j:32 * j + HD, n % 2, :]).then_inc(o_out, 16)
        sp.wait_ge(den_out, 16 * (n + 1))
        if n >= 1:
            sp.wait_ge(rden_ready, n)
        sp.dma_start(den[:], m.den_rows[n].rearrange("(p c) -> p c", p=P)).then_inc(den_in, 16)

    def spread(sp, n):
        bb, kv = divmod(n, KV)
        r = kv % 4 * G * HD
        sp.wait_ge(rden_ready, n + 1)
        if n >= 1:
            sp.wait_ge(rec_in, 16 * G * n)
        sp.dma_start(m.rec_rows[n].rearrange("(p c) -> p c", p=P), rden[:]).then_inc(rden_out, 16)
        sp.wait_ge(rden_out, 16 * (n + 1))
        if n >= 8:
            sp.wait_ge(norm_done, n // 4 - 1)
        for g in range(G):
            sp.dma_start(rec[r + g * HD:r + (g + 1) * HD, (n // 4) % 2, :],
                         m.rec_rows[n, g * S:(g + 1) * S].rearrange("(o s) -> o s", o=1)
                         .broadcast_to([HD, S])).then_inc(rec_in, 16)

    def normalize(pool, c):
        bb, ct = divmod(c, KC)
        pool.wait_ge(o_out, 16 * NJ * 4 * (c + 1))
        pool.wait_ge(rec_in, 16 * G * 4 * (c + 1))
        v = m.ctxT[:, ct, bb * S:(bb + 1) * S]
        nc.gpsimd.tensor_tensor(v, v, rec[:, c % 2, :], ALU.mult).then_inc(norm_done, 1)

    def take_o(act, n):
        act.wait_ge(pv_done, NTT * NJ * (n + 1))
        if n >= 2:
            act.wait_ge(o_out, 16 * NJ * (n - 1))
            act.wait_ge(den_out, 16 * (n - 1))
        nc.scalar.activation(osb[:, n % 2, :], OB[:], ACT.Copy).then_inc(o_done, 1)

    def invert(dve, n):
        dve.wait_ge(den_in, 16 * (n + 1))
        if n >= 1:
            dve.wait_ge(rden_out, 16 * n)
        nc.vector.reciprocal(rden[:], den[:]).then_inc(rden_ready, 1)

    m.leave, m.spread, m.normalize, m.invert, m.NG = leave, spread, normalize, invert, NG
    m.norm_done = norm_done
    m.f_hi, m.f_lo, m.lut_add, m.wsum = f_hi, f_lo, lut_add, wsum

    with nc.Block() as block:
        @block.sync
        def _(sp):
            def place_max(n):
                sp.wait_ge(mp_done, 3 * (n + 1))
                for q in range(4):
                    sp.dma_start(m.m_rows[n].rearrange("i (c q s) -> q c i s", q=4, s=32)[q],
                                 mpt[32 * q:32 * q + NST, :, :]).then_inc(mp_out, 16)
                sp.wait_ge(mp_out, 64 * (n + 1))
                sp.dma_start(QS[n % 3][NROW:NAUG, :], m.m_rows[n]).then_inc(m_in, 16)

            for tb in (NB - 2, NB - 1):
                m.block_out(sp, tb)
            for i in range(2):
                sp.wait_ge(m.part_out[i], 16 * 9 * NB // 2)
            sp.dma_start(lut[:], a["lut"].rearrange("(o s) -> o s", o=1).broadcast_to([P, LUT])).then_inc(lut_in, 16)
            sp.dma_start(idx[:, 0:KC * 2 * INTER].rearrange("p (c n) -> p c n", c=KC),
                         a["gu_idx"].rearrange("(c p) n -> p c n", p=P)).then_inc(idx_in, 16)
            sp.dma_start(idx[:, KC * 2 * INTER:].rearrange("p (c n) -> p c n", c=NI),
                         a["down_idx"].rearrange("(c p) n -> p c n", p=P)).then_inc(idx_in, 16)
            place_max(0)
            for n in range(NG):
                if n >= 1:
                    if n + 2 < NG:
                        load_qk(sp, n + 2)
                    leave(sp, n - 1)
                    spread(sp, n - 1)
                if n + 1 < NG:
                    place_max(n + 1)

        def low_part(pool, c):
            cols = slice(c * PIECE, (c + 1) * PIECE)
            if c == 0:
                pool.wait_ge(f_hi, 1)
                nc.gpsimd.tensor_tensor(m.wol[:], m.wo[:], m.woh[:], ALU.subtract).then_inc(f_lo, 1)
            pool.wait_ge(f_hi, c + 2)
            nc.gpsimd.tensor_tensor(m.fl[:, cols], wsum[:, cols], m.fh[:, cols], ALU.subtract).then_inc(f_lo, 1)

        def max_parts(pool, n):
            pool.wait_ge(mt_done, n + 1)
            nc.gpsimd.tensor_scalar(mres[:, 0, :], mT[:], -1.0, None, ALU.mult).then_inc(mres_done, 1)
            pool.wait_ge(mres_done, 2 * n + 1)
            if n >= 1:
                pool.wait_ge(mp_out, 64 * n)
            nc.gpsimd.tensor_copy(mpt[:, 0, :], mres[:, 0, :]).then_inc(mp_done, 1)
            pool.wait_ge(mp_done, 3 * n + 1)
            nc.gpsimd.tensor_tensor(mres[:, 1, :], mres[:, 0, :], mpt[:, 0, :], ALU.subtract).then_inc(mres_done, 1)
            pool.wait_ge(mres_done, 2 * n + 2)
            nc.gpsimd.tensor_copy(mpt[:, 1, :], mres[:, 1, :]).then_inc(mp_done, 1)
            pool.wait_ge(mp_done, 3 * n + 2)
            nc.gpsimd.tensor_tensor(mpt[:, 2, :], mres[:, 1, :], mpt[:, 1, :], ALU.subtract).then_inc(mp_done, 1)

        @block.gpsimd
        def _(pool):
            nc.gpsimd.memset(KS[0][NROW:NAUG, :], 1.0).then_inc(ones_ready, 1)
            nc.gpsimd.memset(KS[1][NROW:NAUG, :], 1.0).then_inc(ones_ready, 1)
            nc.gpsimd.memset(KS[2][NROW:NAUG, :], 1.0).then_inc(ones_ready, 1)
            pool.wait_ge(ones_ready, 3)
            for tb in (NB - 2, NB - 1):
                m.third_parts(pool, tb)
            max_parts(pool, 0)
            for n in range(NG):
                for k in range(4 * n, 4 * n + 4 if n < NG - 2 else LUT * NPIECE if n == NG - 2 else 0):
                    c, v = divmod(k, LUT)
                    cols = slice(c * PIECE, (c + 1) * PIECE)
                    if v >= 1:
                        slot = c * (LUT - 1) + v - 1
                        pool.wait_ge(lut_prod, k + 1)
                        if slot >= 1:
                            pool.wait_ge(lut_add, slot)
                        nc.gpsimd.tensor_tensor(wsum[:, cols], wsum[:, cols], wtmp[:, slot % 3, :],
                                                ALU.add).then_inc(lut_add, 1)
                    if n + 1 < NG and k == 4 * n + 1:
                        max_parts(pool, n + 1)
                if n % 4 == 1 and n > 4:
                    low_part(pool, n // 4 - 1)
                    normalize(pool, n // 4 - 1)
        def take_high(act, c):
            cols = slice(c * PIECE, (c + 1) * PIECE)
            act.wait_ge(lut_add, (c + 1) * (LUT - 1))
            nc.scalar.activation(m.fh[:, cols], wsum[:, cols], ACT.Copy).then_inc(f_hi, 1)

        @block.scalar
        def _(act):
            m.take_v(act, NB - 1)
            m.cut(act, NB - 1)
            for n in range(NG):
                if n == 2 or n >= 5 and n % 4 == 1:
                    if n == 2:
                        nc.scalar.activation(m.woh[:], m.wo[:], ACT.Copy).then_inc(f_hi, 1)
                    else:
                        take_high(act, n // 4 - 1)
                for i in range(NTT * NJ):
                    k = n * NTT * NJ + i
                    if i == 4 and n >= 1:
                        take_o(act, n - 1)
                    act.wait_ge(s_ps, k + 1)
                    if k >= NPT:
                        act.wait_ge(pv_done, k - NPT + 1)
                    nc.scalar.activation(pt[:, k % NPT, :], ring(k)[:], ACT.Exp,
                                         scale=float(E) ** -0.5).then_inc(p_ready, 1)
            take_o(act, NG - 1)

        @block.vector
        def _(dve):
            nc.vector.memset(mx[:], 0.0).then_inc(mx_zero, 1)
            m.rope(dve, NB - 1)
            dve.wait_ge(mx_zero, 1)

            def row_max(n, i):
                k = n * NST + i
                dve.wait_ge(max_ps, k + 1)
                if i == 0 and n >= 2:
                    dve.wait_ge(mt_done, n - 1)
                nc.vector.tensor_reduce(mx[:, n % 2, i:i + 1], m.psum[:, 2 * (k % 2):2 * (k % 2) + 2, :], AX_XY, ALU.max).then_inc(max_done, 1)

            def turn_max(n):
                dve.wait_ge(max_done, NST * (n + 1))
                if n >= 1:
                    dve.wait_ge(mres_done, 2 * n - 1)
                nc.vector.transpose(mT[:], mx[:, n % 2, :]).then_inc(mt_done, 1)

            def look_up(k):
                c, v = divmod(k, LUT)
                cols = slice(c * PIECE, (c + 1) * PIECE)
                if k == 0:
                    dve.wait_ge(lut_in, 16)
                    dve.wait_ge(idx_in, 32)
                slot = c * (LUT - 1) + v - 1
                if v >= 1 and slot >= 3:
                    dve.wait_ge(lut_add, slot - 2)
                nc.vector.tensor_scalar(wsum[:, cols] if v == 0 else wtmp[:, slot % 3, :], idx[:, cols], float(v),
                                        lut[:, v:v + 1], ALU.is_equal, ALU.mult).then_inc(lut_prod, 1)

            for i in range(NST + AHEAD):
                row_max(i // NST, i % NST)
                if i == NST - 1:
                    turn_max(0)
            for n in range(NG):
                for i in range(NST):
                    k = (n + 1) * NST + AHEAD + i
                    if k < NG * NST:
                        row_max(k // NST, k % NST)
                        if k % NST == NST - 1:
                            turn_max(k // NST)
                    if i == 6 and n >= 1:
                        invert(dve, n - 1)
                    if n < NG - 2 and i % 4 == 0:
                        look_up(4 * n + i // 4)
                    elif n == NG - 2 and i % 2 == 1:
                        look_up(4 * n + i // 2)

        @block.tensor
        def _(pe):
            pe.wait_ge(ones_ready, 3)

            def maxima(n, i):
                k = n * NST + i
                if i == 0:
                    pe.wait_ge(qk_in[n % 3], 16 * (1 + G) * (n // 3 + 1))
                if k >= 2:
                    pe.wait_ge(max_done, k - 1)
                if k == 1:
                    pe.wait_ge(m.v_out, NT)
                for h in range(2):
                    mm = nc.tensor.matmul(MX[k % 2][h][:], QS[n % 3][0:NROW, i * P:(i + 1) * P],
                                          KS[n % 3][0:NROW, h * BLK:(h + 1) * BLK], start=True, stop=True)
                mm.then_inc(max_ps, 1)

            def scores(n, t, j):
                k = (n * NTT + t) * NJ + j
                if t == 0 and j == 0:
                    pe.wait_ge(m_in, 16 * (n + 1))
                if n == 0 and t == 0 and j == 0:
                    pe.wait_ge(m.prod_q, 4 * NB)
                    pe.wait_ge(m.prod_k, 2 * NB)
                if k >= 3:
                    pe.wait_ge(p_ready, k - 2)
                nc.tensor.matmul(ring(k)[:], KS[n % 3][:, t * P:(t + 1) * P], QS[n % 3][:, j * BLK:(j + 1) * BLK],
                                 start=True, stop=True).then_inc(s_ps, 1)

            def weigh(n, t):
                bb, kv = divmod(n, KV)
                for j in range(NJ):
                    k = (n * NTT + t) * NJ + j
                    pe.wait_ge(p_ready, k + 1)
                    if t == 0 and j == 0 and n >= 1:
                        pe.wait_ge(o_done, n)
                    nc.tensor.matmul(OB[32 * j:32 * (j + 1), :], m.VS[:, bb * NTT + t, kv, :], pt[:, k % NPT, :],
                                     start=(t == 0), stop=(t == NTT - 1)).then_inc(pv_done, 1)

            def maxima_ahead(k):
                if k < NG * NST:
                    maxima(k // NST, k % NST)

            for k in range(NST + AHEAD):
                maxima_ahead(k)
            for n in range(NG):
                for t in range(NTT):
                    k = (n + 1) * NST + AHEAD + 2 * t
                    maxima_ahead(k)
                    scores(n, t, 0)
                    if t >= 1:
                        weigh(n, t - 1)
                    elif n >= 1:
                        weigh(n - 1, NTT - 1)
                    maxima_ahead(k + 1)
                    for j in range(1, NJ):
                        scores(n, t, j)
            weigh(NG - 1, NTT - 1)




def ffn_stage(nc, m, a):
    at, sem, bank = m.at, m.sem, m.bank
    b = m.l0
    ch = at("ctx_h", [P, KC, T], F32R, b); b += KC * T * 4
    cl = at("ctx_l", [P, KC, T], F32R, b); b += KC * T * 4
    m.woh1 = at("wout_h", [P, KC, E], F32R, b); b += KC * E * 4
    m.wol1 = at("wout_l", [P, KC, E], F32R, b); b += KC * E * 4
    m.ident1 = at("ident1", [P, P], F32, b); b += P * 4
    m.mv1 = at("mv1", [P, NT, 2], F32, b); b += NT * 8
    m.rstd1 = at("rstd1", [P, NT], F32, b); b += NT * 4
    m.p3 = b
    sg = at("f_silu", [P, 2, BLK], F32, b); b += 2 * BLK * 4
    hf = at("f_h", [P, 2, BLK], F32, b); b += 2 * BLK * 4
    hh = at("f_hh", [P, 3, BLK], F32R, b); b += 3 * BLK * 4
    m.xb = at("x_norm2", [P, NT, E], F32, m.after_ctx - KC * T * 4)
    assert b <= m.after_ctx - KC * T * 4
    b = m.after_ctx
    gs = at("f_gs", [P, TPB, E], F32, b); b += TPB * E * 4
    m.xa = at("f_xa", [P, TPB, E], F32, b); b += TPB * E * 4
    assert b <= m.p1
    b = m.w1
    m.raw1 = raw = at("w1_raw", [P, 6, KC, E], F32, b); b += 6 * KC * E * 4
    m.wh1 = wh = at("w1_h", [P, 4, KC, E], F32R, b); b += 4 * KC * E * 4
    m.wl1 = wl = at("w1_l", [P, 4, KC, E], F32R, b); b += 4 * KC * E * 4
    m.cols3 = at("cols3", [P, 3, KC], F32, b); b += 32
    m.gw = at("gate_w", [P, KC, NE], F32, b); b += KC * NE * 4
    m.st = at("bn_st1", [P, 2, TPB, 6], F32, b); b += 2 * TPB * 24
    m.ve = at("var_eps1", [P, 2, TPB], F32, b); b += 2 * TPB * 4
    m.mv2 = at("mv2", [P, TPB, 2], F32, b); b += TPB * 8
    m.rstd2 = at("rstd2", [P, TPB], F32, b); b += 32
    m.mhalf = at("minus_half1", [P, TPB], F32, b); b += 32
    gate = at("f_gate", [P, TPB, E], F32, b); b += TPB * E * 4
    hl = at("f_hl", [P, 3, BLK], F32R, b); b += 3 * BLK * 4
    assert b <= nc.sbuf_usable_end, b
    w_in, c_in, const, wc_ps, wh_ready, wl_ready = (
        sem(n) for n in ("t_w_in", "t_c_in", "t_const", "wc_ps", "t_wh", "t_wl"))
    m.stats, m.var, m.rstd, m.xa_ready, m.xb_ready = (sem(n) for n in ("t_stats", "t_var", "t_rstd", "t_xa", "t_xb"))
    ctx_hi, ctx_lo, gu_ps, silu_done, h_done, hi_done, lo_done, down_done, s_done = (
        sem(n) for n in ("ctx_hi", "ctx_lo", "gu_ps", "f_silu_done", "h_done", "hi_done", "lo_done", "down_done", "s_done"))
    gate_done, gs_done, x_done = sem("gate_done"), sem("gs_done"), sem("x_done")
    NQ = NI + 1
    fh = m.fh[:, 0:KC * 2 * INTER].rearrange("p (c n) -> p c n", c=KC)
    fl = m.fl[:, 0:KC * 2 * INTER].rearrange("p (c n) -> p c n", c=KC)
    dh = m.fh[:, KC * 2 * INTER:].rearrange("p (c n) -> p c n", c=NI)
    dl = m.fl[:, KC * 2 * INTER:].rearrange("p (c n) -> p c n", c=NI)
    pieces = parts(INTER, P)

    def gate_out(act, tb):
        act.wait_ge(down_done, (tb + 1) * NI)
        if tb >= 1:
            act.wait_ge(gs_done, tb)
        nc.scalar.activation(gate[:], m.psum[:, 4:8, 0:E], ACT.Silu).then_inc(gate_done, 1)

    def add_gated(dve, tb):
        dve.wait_ge(gate_done, tb + 1)
        dve.wait_ge(s_done, tb + 1)
        if tb >= 1:
            dve.wait_ge(x_done, tb)
        slot = (tb * NQ + NI) % 2 * 2
        nc.vector.tensor_tensor(gs[:], m.psum[:, slot:slot + 2, :].rearrange("p b (n e) -> p (b n) e", e=E),
                                gate[:], ALU.mult).then_inc(gs_done, 1)
        xt = m.x[:, tb * TPB:(tb + 1) * TPB, :]
        dve.wait_ge(gs_done, tb + 1)
        nc.vector.tensor_tensor(xt, xt, gs[:], ALU.add).then_inc(x_done, 1)

    m.gate_out, m.add_gated, m.gs_done, m.x_done = gate_out, add_gated, gs_done, x_done

    def wc_banks():
        s = NB * NQ % 2 * 2
        return m.psum[:, s:s + 2, :]

    with nc.Block() as block:
        @block.sync
        def _(sp):
            m.leave(sp, m.NG - 1)
            m.spread(sp, m.NG - 1)
            for j, n in enumerate(("wx_t", "ww", "wk", "wr", "wv", "wout")):
                sp.dma_start(raw[:, j, :, :], a[n].rearrange("(c p) n -> p c n", p=P)).then_inc(w_in, 16)
            sp.dma_start(m.ident1[:], a["ident"]).then_inc(c_in, 16)
            for j, n in enumerate(("gamma", "beta", "bw")):
                sp.dma_start(m.cols3[:, j, :], a[n]).then_inc(c_in, 16)
            sp.dma_start(m.gw[:], a["gate_w_t"].rearrange("(c p) n -> p c n", p=P)).then_inc(c_in, 16)
            sp.wait_ge(c_in, 80)

        @block.gpsimd
        def _(pool):
            nc.gpsimd.memset(m.mhalf[:], -0.5).then_inc(const, 1)
            m.normalize(pool, m.NG // 4 - 1)
            pool.wait_ge(const, 1)
            for g in range(NB - 1):
                for i in range(2):
                    inverse_deviation(pool, m, g, i)
                if g == 0:
                    pool.wait_ge(wh_ready, 4)
                    nc.gpsimd.tensor_tensor(wl[:, 1:4, :, :], raw[:, 2:5, :, :], wh[:, 1:4, :, :], ALU.subtract).then_inc(wl_ready, 1)
                    nc.gpsimd.tensor_tensor(m.wol1[:], raw[:, 5, :, :], m.woh1[:], ALU.subtract).then_inc(wl_ready, 1)

        @block.scalar
        def _(act):
            last = slice((m.NPIECE - 1) * m.PIECE, m.NLUT)
            nc.scalar.activation(m.fh[:, last], m.wsum[:, last], ACT.Copy).then_inc(m.f_hi, 1)

            def cut_ctx(tb):
                act.wait_ge(m.norm_done, KC * (tb * BLK // S + 1))
                cols = slice(tb * BLK, (tb + 1) * BLK)
                nc.scalar.activation(ch[:, :, cols], m.ctxT[:, :, cols], ACT.Copy).then_inc(ctx_hi, 1)
            for tb in range(NB):
                for c, (i0, n) in enumerate(pieces):
                    k = tb * NI + c
                    act.wait_ge(gu_ps, k + 1)
                    if k >= 2:
                        act.wait_ge(h_done, k - 1)
                    nc.scalar.activation(sg[0:n, k % 2, :], bank[(tb * NQ + c) % 2 * 2][0:n, :],
                                         ACT.Silu).then_inc(silu_done, 1)
                    act.wait_ge(h_done, k + 1)
                    if k >= 3:
                        act.wait_ge(down_done, k - 2)
                    nc.scalar.activation(hh[0:n, k % 3, :], hf[0:n, k % 2, :], ACT.Copy).then_inc(hi_done, 1)
                    if tb == 0 and c >= NI - NB:
                        cut_ctx(c - NI + NB)
                    if tb == 1 and c < 4:
                        if c == 0:
                            act.wait_ge(w_in, 16 * 6)
                            act.wait_ge(m.f_lo, m.NPIECE + 1)
                        nc.scalar.activation(wh[:, 1 + c, :, :] if c < 3 else m.woh1[:], raw[:, 2 + c, :, :],
                                             ACT.Copy).then_inc(wh_ready, 1)
                if tb == NB - 1:
                    act.wait_ge(wc_ps, 1)
                    nc.scalar.activation(wh[:, 0, :, :], wc_banks()[:, :, 0:E], ACT.Copy).then_inc(wh_ready, 1)
                if tb < NB - 1:
                    gate_out(act, tb)

        @block.vector
        def _(dve):
            last = slice((m.NPIECE - 1) * m.PIECE, m.NLUT)
            dve.wait_ge(m.f_hi, m.NPIECE + 1)
            nc.vector.tensor_tensor(m.fl[:, last], m.wsum[:, last], m.fh[:, last], ALU.subtract).then_inc(m.f_lo, 1)

            def low_ctx(tb):
                cols = slice(tb * BLK, (tb + 1) * BLK)
                dve.wait_ge(ctx_hi, tb + 1)
                nc.vector.tensor_tensor(cl[:, :, cols], m.ctxT[:, :, cols], ch[:, :, cols],
                                        ALU.subtract).then_inc(ctx_lo, 1)

            for tb in range(NB):
                for c, (i0, n) in enumerate(pieces):
                    k = tb * NI + c
                    if k == 2:
                        m.invert(dve, m.NG - 1)
                    dve.wait_ge(silu_done, k + 1)
                    if k >= 2:
                        dve.wait_ge(lo_done, k - 1)
                        dve.wait_ge(hi_done, k - 1)
                    nc.vector.tensor_tensor(hf[0:n, k % 2, :], bank[(tb * NQ + c) % 2 * 2 + 1][0:n, :],
                                            sg[0:n, k % 2, :], ALU.mult).then_inc(h_done, 1)
                    dve.wait_ge(hi_done, k + 1)
                    if k >= 3:
                        dve.wait_ge(down_done, k - 2)
                    nc.vector.tensor_tensor(hl[0:n, k % 3, :], hf[0:n, k % 2, :], hh[0:n, k % 3, :],
                                            ALU.subtract).then_inc(lo_done, 1)
                    if tb == 0 and c >= NI - NB:
                        low_ctx(c - NI + NB)
                    if tb >= 1 and c < 4:
                        if c == 0:
                            dve.wait_ge(x_done, tb)
                        if tb == 1 and c == 3:
                            dve.wait_ge(ctx_lo, NB)
                        (statistics if c % 2 == 0 else norm)(nc, dve, m, tb - 1, c // 2)
                if tb == NB - 1:
                    dve.wait_ge(wh_ready, 5)
                    nc.vector.tensor_tensor(wl[:, 0, :, :], wc_banks()[:, :, 0:E], wh[:, 0, :, :],
                                            ALU.subtract).then_inc(wl_ready, 1)
                if tb < NB - 1:
                    add_gated(dve, tb)
        @block.tensor
        def _(pe):
            def slot_free(tb, c):
                q = tb * NQ + c - 2
                if q >= 0:
                    t0, c0 = divmod(q, NQ)
                    if c0 < NI:
                        pe.wait_ge(h_done, t0 * NI + c0 + 1)
                    else:
                        pe.wait_ge(gs_done, t0 + 1)
                return (q + 2) % 2 * 2

            def join_weights():
                pe.wait_ge(w_in, 16 * 6)
                s = slot_free(NB, 0)
                for i in range(KC):
                    for mc in range(KC):
                        mm = nc.tensor.matmul(bank[s + i][:, 0:E], raw[:, 0, mc, i * P:(i + 1) * P], raw[:, 1, mc, :],
                                              start=(mc == 0), stop=(mc == KC - 1))
                mm.then_inc(wc_ps, 1)

            def up(tb, c):
                i0, n = pieces[c]
                cols = slice(tb * BLK, (tb + 1) * BLK)
                s = slot_free(tb, c)
                for w in range(2):
                    i = w * INTER + i0
                    mm = three(nc, bank[s + w][0:n, :], [(fh[:, kc, i:i + n], fl[:, kc, i:i + n],
                                                          m.xTh[:, kc, cols], m.xTl[:, kc, cols]) for kc in range(KC)])
                mm.then_inc(gu_ps, 1)

            def down(tb, c):
                i0, n = pieces[c]
                k = tb * NI + c
                pe.wait_ge(lo_done, k + 1)
                if c == 0 and tb >= 1:
                    pe.wait_ge(gate_done, tb)
                if c == 0 and tb == 0:
                    pe.wait_ge(m.f_lo, m.NPIECE + 1)
                for i in range(TPB):
                    tok = slice(i * P, (i + 1) * P)
                    mm = three(nc, bank[4 + i][:, 0:E], [(hh[0:n, k % 3, tok], hl[0:n, k % 3, tok],
                                                          dh[0:n, c, :], dl[0:n, c, :])],
                               start=(c == 0), stop=(c == NI - 1))
                mm.then_inc(down_done, 1)

            def attn_out(tb):
                pe.wait_ge(ctx_lo, tb + 1)
                s = slot_free(tb, NI)
                for i in range(TPB):
                    tok = slice(tb * BLK + i * P, tb * BLK + (i + 1) * P)
                    mm = three(nc, bank[s + i // 2][:, i % 2 * E:(i % 2 + 1) * E],
                               [(ch[:, kc, tok], cl[:, kc, tok], m.woh[:, kc, :], m.wol[:, kc, :])
                                for kc in range(KC)])
                mm.then_inc(s_done, 1)

            for tb in range(NB):
                for c in range(NI):
                    up(tb, c)
                    if c >= 1:
                        down(tb, c - 1)
                attn_out(tb)
                if tb == NB - 1:
                    join_weights()
                down(tb, NI - 1)


def statistics(nc, dve, m, g, i):
    ts = slice(g * TPB, (g + 1) * TPB)
    src, mv = (m.x[:, ts, :], m.mv1[:, ts, :]) if i == 0 else (m.xa, m.mv2)
    done = (2 * g + i) * 2 * TPB
    if i == 1:
        dve.wait_ge(m.xa_ready, TPB * (g + 1))
    if g >= 1:
        dve.wait_ge(m.xb_ready, TPB * g)
    for j in range(TPB):
        nc.vector.bn_stats(m.st[:, i, j, :], src[:, j, :]).then_inc(m.stats, 1)
    dve.wait_ge(m.stats, done + TPB)
    for j in range(TPB):
        nc.vector.bn_aggr(mv[:, j, :], m.st[:, i, j, :]).then_inc(m.stats, 1)
    dve.wait_ge(m.stats, done + 2 * TPB)
    nc.vector.tensor_scalar(m.ve[:, i, :], mv[:, :, 1], EPS, None, ALU.add).then_inc(m.var, 1)


def inverse_deviation(pool, m, g, i):
    pool.wait_ge(m.var, 2 * g + i + 1)
    pool.tensor_tensor(m.rstd1[:, g * TPB:(g + 1) * TPB] if i == 0 else m.rstd2[:], m.ve[:, i, :], m.mhalf[:],
                       ALU.pow).then_inc(m.rstd, 1)


def norm(nc, dve, m, g, i):
    dve.wait_ge(m.rstd, 2 * g + i + 1)
    for j in range(TPB):
        n = g * TPB + j
        if i == 0:
            nc.vector.tensor_scalar(m.xa[:, j, :], m.x[:, n, :], m.mv1[:, n, 0:1], m.rstd1[:, n:n + 1],
                                    ALU.subtract, ALU.mult).then_inc(m.xa_ready, 1)
        else:
            nc.vector.tensor_scalar(m.xb[:, n, :], m.xa[:, j, :], m.mv2[:, j, 0:1], m.rstd2[:, j:j + 1],
                                    ALU.subtract, ALU.mult).then_inc(m.xb_ready, 1)


LH, LD = 4, 64
NCH = 2 * B
CH = 128
NC = S // CH
SMALL = 5
QB = 32


def time_mix_in_stage(nc, m, a):
    at, sem, bank = m.at, m.sem, m.bank
    b = m.base
    m.D = at("decay", [P, KC, T], F32, b); b += KC * T * 4
    m.K = at("key", [P, KC, T], F32, b); b += KC * T * 4
    m.R = at("recept", [P, KC, T], F32, b); b += KC * T * 4
    m.V = at("value", [P, NT, E], F32, b); b += NT * E * 4
    assert b <= m.l0 + 2 * KC * T * 4
    b = m.p3
    yh = at("y_h", [P, KC, T], F32R, b); b += KC * T * 4
    assert b <= m.after_ctx - KC * T * 4
    b = m.after_ctx
    b = m.after_ctx + 2 * TPB * E * 4
    yl = at("y_l", [P, KC, T], F32R, b); b += KC * T * 4
    yf = at("y_f", [P, 2, KC, BLK], F32, b); b += 2 * KC * BLK * 4
    xa = at("x_norm", [P, TPB, E], F32, b); b += TPB * E * 4
    xt = at("x_norm_t", [P, KC, BLK], F32, b); b += KC * BLK * 4
    nbw = at("nbw", [P, KC], F32, b); b += 32
    assert b <= m.w1
    raw, wh, wl, cols3 = m.raw1, m.wh1, m.wl1, m.cols3
    m.rt_at = nc.sbuf_usable_end // 32 * 32 - NMC * WP * 4 - 9 * NT * NE * 4
    m.lt = at("logits_t", [P, NT, NE], F32, m.rt_at)
    names = ("t2_xa", "t_ps", "t_yf", "t_yh", "t_xt", "t_yl", "t_nbw", "pr_ps", "act_out", "dve_out", "lt_ps", "lt_out")
    (xa_ready, t_ps, yf_ready, yh_ready, xt_ready, yl_ready, nbw_ready, pr_ps, act_out, dve_out, lt_ps, lt_out) = (
        sem(n) for n in names)

    ITEMS = [("w", 0), ("k", 0), ("r", 0), ("w", 1), ("k", 1), ("r", 1), ("v", 0), ("v", 1)]
    NIT = len(ITEMS)
    RING = 5

    def taken_by(kind):
        return "act" if kind in "wr" else "dve"

    def order(k):
        who = taken_by(ITEMS[k % NIT][0])
        per = sum(taken_by(x[0]) == who for x in ITEMS)
        return k // NIT * per + sum(taken_by(x[0]) == who for x in ITEMS[:k % NIT + 1])

    def rbank(k):
        return bank[2 + k % RING]

    def take(eng, k, tb):
        kind, i = ITEMS[k % NIT]
        cols = slice(tb * BLK, (tb + 1) * BLK)
        eng.wait_ge(pr_ps, k + 1)
        if kind == "w":
            nc.scalar.activation(m.D[:, i, cols], rbank(k), ACT.Sigmoid, bias=nbw[:, i:i + 1],
                                 scale=-1.0).then_inc(act_out, 1)
        elif kind == "r":
            nc.scalar.activation(m.R[:, i, cols], rbank(k), ACT.Sigmoid).then_inc(act_out, 1)
        elif kind == "k":
            nc.vector.tensor_copy(m.K[:, i, cols], rbank(k)).then_inc(dve_out, 1)
        else:
            n = tb * TPB + 2 * i
            nc.vector.tensor_copy(m.V[:, n:n + 2, :], rbank(k).rearrange("p (n e) -> p n e", n=2)).then_inc(dve_out, 1)

    with nc.Block() as block:
        @block.gpsimd
        def _(pool):
            for i in range(2):
                inverse_deviation(pool, m, NB - 1, i)

        @block.scalar
        def _(act):
            def out_b(g):
                for kc in range(KC):
                    act.wait_ge(t_ps, 2 * g * KC + kc + 1)
                    if g >= 2:
                        act.wait_ge(yl_ready, g - 1)
                    nc.scalar.activation(yf[:, g % 2, kc, :], bank[kc], ACT.Identity, bias=cols3[:, 1, kc:kc + 1],
                                         scale=cols3[:, 0, kc:kc + 1]).then_inc(yf_ready, 1)
                act.wait_ge(yf_ready, KC * (g + 1))
                nc.scalar.activation(yh[:, :, g * BLK:(g + 1) * BLK], yf[:, g % 2, :, :], ACT.Copy).then_inc(yh_ready, 1)

            def out_a(g):
                for kc in range(KC):
                    act.wait_ge(t_ps, (2 * g + 1) * KC + kc + 1)
                    if g >= 1:
                        act.wait_ge(lt_ps, g)
                    nc.scalar.activation(xt[:, kc, :], bank[kc], ACT.Copy).then_inc(xt_ready, 1)

            m.gate_out(act, NB - 1)
            out_b(0)
            out_a(0)
            out_b(1)
            act.wait_ge(nbw_ready, 1)
            for g in range(NB):
                for i in range(NIT):
                    if taken_by(ITEMS[i][0]) == "act":
                        take(act, g * NIT + i, g)
                if g + 1 < NB:
                    out_a(g + 1)
                if g + 2 < NB:
                    out_b(g + 2)

        @block.vector
        def _(dve):
            def once_normed(g):
                if g >= 1:
                    dve.wait_ge(t_ps, 2 * g * KC)
                for j in range(TPB):
                    n = g * TPB + j
                    nc.vector.tensor_scalar(xa[:, j, :], m.x[:, n, :], m.mv1[:, n, 0:1], m.rstd1[:, n:n + 1],
                                            ALU.subtract, ALU.mult).then_inc(xa_ready, 1)

            def low(g):
                dve.wait_ge(yh_ready, g + 1)
                cols = slice(g * BLK, (g + 1) * BLK)
                nc.vector.tensor_tensor(yl[:, :, cols], yf[:, g % 2, :, :], yh[:, :, cols],
                                        ALU.subtract).then_inc(yl_ready, 1)
            nc.vector.tensor_scalar(nbw[:], cols3[:, 2, :], -1.0, None, ALU.mult).then_inc(nbw_ready, 1)
            once_normed(0)
            m.add_gated(dve, NB - 1)
            low(0)
            for g in range(NB):
                if g + 1 < NB:
                    once_normed(g + 1)
                    low(g + 1)
                for j, i in enumerate(i for i in range(NIT) if taken_by(ITEMS[i][0]) == "dve"):
                    take(dve, g * NIT + i, g)
                    if g == 0 and j == 0:
                        dve.wait_ge(m.x_done, NB)
                    if g == 0:
                        (statistics if j % 2 == 0 else norm)(nc, dve, m, NB - 1, j // 2)
            dve.wait_ge(lt_ps, NB)
            nc.vector.tensor_copy(m.lt[:], bank[7][:, 0:NT * NE].rearrange("p (n e) -> p n e", e=NE)).then_inc(lt_out, 1)

        @block.tensor
        def _(pe):
            def turn(g, which):
                k = 2 * g + which
                if which:
                    pe.wait_ge(xa_ready, TPB * (g + 1))
                elif g == NB - 1:
                    pe.wait_ge(m.xb_ready, NT)
                for kc in range(KC):
                    if k >= 1:
                        if which:
                            pe.wait_ge(yf_ready, g * KC + kc + 1)
                        else:
                            pe.wait_ge(xt_ready, (g - 1) * KC + kc + 1)
                    for i in range(TPB):
                        src = xa[:, i, kc * P:(kc + 1) * P] if which else m.xb[:, g * TPB + i, kc * P:(kc + 1) * P]
                        mm = nc.tensor.transpose(bank[kc][:, i * P:(i + 1) * P], src, m.ident1[:])
                    mm.then_inc(t_ps, 1)

            def logits(g):
                pe.wait_ge(xt_ready, KC * (g + 1))
                if g == 0:
                    pe.wait_ge(m.gs_done, NB)
                for j in range(TPB):
                    n = g * TPB + j
                    for kc in range(KC):
                        mm = nc.tensor.matmul(bank[7][:, n * NE:(n + 1) * NE], xt[:, kc, j * P:(j + 1) * P],
                                              m.gw[:, kc, :], start=(kc == 0), stop=(kc == KC - 1))
                mm.then_inc(lt_ps, 1)

            def project(g):
                cols = slice(g * BLK, (g + 1) * BLK)
                pe.wait_ge(yl_ready, g + 1)
                if g == 0:
                    pe.wait_ge(m.gs_done, NB)
                for i, (kind, c) in enumerate(ITEMS):
                    k = g * NIT + i
                    if k >= RING:
                        pe.wait_ge(act_out if taken_by(ITEMS[(k - RING) % NIT][0]) == "act" else dve_out, order(k - RING))
                    if kind == "v":
                        for j in range(2):
                            tok = slice(g * BLK + (2 * c + j) * P, g * BLK + (2 * c + j + 1) * P)
                            mm = three(nc, rbank(k)[:, j * E:(j + 1) * E],
                                       [(yh[:, kc, tok], yl[:, kc, tok], wh[:, 3, kc, :], wl[:, 3, kc, :])
                                        for kc in range(KC)])
                    else:
                        w = "wkr".index(kind)
                        ch = slice(c * P, (c + 1) * P)
                        mm = three(nc, rbank(k), [(wh[:, w, kc, ch], wl[:, w, kc, ch], yh[:, kc, cols], yl[:, kc, cols])
                                                  for kc in range(KC)])
                    mm.then_inc(pr_ps, 1)

            turn(0, 0)
            turn(0, 1)
            turn(1, 0)
            for g in range(NB):
                project(g)
                logits(g)
                if g + 1 < NB:
                    turn(g + 1, 1)
                if g + 2 < NB:
                    turn(g + 2, 0)


def time_mix_stage(nc, m, a):
    at, sem, bank = m.at, m.sem, m.bank
    NH = 2
    NS = NC * NH
    b = m.p3
    A = [at(f"A{g}", [P, NS, CH], F32, b + g * NS * CH * 4) for g in range(NCH)]; b += NCH * NS * CH * 4
    Q = [at(f"prod{g}", [P, 2, S], F32, m.p3 + g * NS * CH * 4) for g in range(NCH)]
    R2 = [at(f"recept2_{g}", [P, NH, S], F32, m.p3 + g * NS * CH * 4) for g in range(NCH)]
    AD = [at(f"AD{g}", [P, NS, QB], F32, b + g * NS * QB * 4) for g in range(NCH)]; b += NCH * NS * QB * 4
    combT = at("comb_t", [NE, T], F32, b)
    TOT = {1: None}
    for s in (2, 4, 8, 16, 32, 64, 128):
        TOT[s] = at(f"tot{s}", [P, NCH, S // s], F32, b); b += NCH * (S // s) * 4
    kT = [at(f"kT{i}", [P, NC, P], F32, b + i * NC * P * 4) for i in range(2)]; b += 2 * NC * P * 4
    ST = [at(f"state{i}", [P, NC, LD], F32, b + i * NC * LD * 4) for i in range(2)]; b += 2 * NC * LD * 4
    yl = at("ty_l", [P, KC, T], F32R, m.p3)
    masks = at("masks", [P, SMALL + 1, QB], I32, b); b += (SMALL + 1) * QB * 4
    diag = at("diag", [P, QB], F32, b); b += QB * 4
    rank = at("rank", [P, NE], F32, b); b += NE * 4
    heads = at("heads", [P, NH], F32, b); b += NH * 4
    assert b <= m.rt_at, b
    b = m.rt_at + NT * NE * 4
    rt = {}
    for n in ("e", "p", "q1", "s1", "q2", "s2", "sel"):
        rt[n] = at("rt_" + n, [P, NT, NE], F32, b); b += NT * NE * 4
    r1 = at("rt_r", [P, 8, NT], F32, b); b += 8 * NT * 4
    rt["l"] = m.lt
    m.raw = at("m_raw", [P, NMC, WP], F32, b); b += NMC * WP * 4
    assert b <= nc.sbuf_usable_end, b
    m.comb_rows = nc.dram_tensor("comb_rows", (NE, T), F32, kind="Internal").ap()
    rt_done, exp_done, ct_ps, ct_ready, crow_out, raw_in = (
        sem(n) for n in ("e_rt", "e_exp", "e_ct_ps", "e_ct", "e_crow", "e_w_in"))
    q_done, odd_zero, heads_ready = sem("q_done"), sem("odd_zero"), sem("heads_ready")
    r2_zero, r2_in, r_back = sem("r2_zero"), sem("r2_in"), sem("r_back")
    NSTEP = 22
    yh = at("ty_h", [P, KC, T], F32R, m.base)
    m.s = at("s_tok", [P, NT, E], F32, m.base + KC * T * 4)
    names = ("mask_in", "a_zero", "tot_done", "lev_ps", "lev_take", "r_done", "k_done", "ad_put", "kt_ps", "kt_done",
             "u_ps", "st_done", "ty_ps", "tyh_done", "tyl_done", "so_ps", "so_done")
    (mask_in, a_zero, tot_done, lev_ps, lev_take, r_done, k_done, ad_put, kt_ps, kt_done, u_ps, st_done, ty_ps,
     tyh_done, tyl_done, so_ps, so_done) = (sem(n) for n in names)
    m.xa1 = at("m_xa", [P, TPB, E], F32, m.base + 3 * KC * T * 4)
    m.wl = at("m_l", [P, NMC, WP], F32R, m.rt_at + 9 * NT * NE * 4)
    m.wh = at("m_h", [P, NMC, WP], F32R, m.p3)
    m.e_xa, m.e_wh, m.e_wl = sem("e_xa"), sem("e_wh"), sem("e_wl")

    def once_normed(dve, g):
        for j in range(TPB):
            n = g * TPB + j
            nc.vector.tensor_scalar(m.xa1[:, j, :], m.x[:, n, :], m.mv1[:, n, 0:1], m.rstd1[:, n:n + 1],
                                    ALU.subtract, ALU.mult).then_inc(m.e_xa, 1)

    def high_w(i):
        c = ORDER[i]
        nc.scalar.activation(m.wh[:, c, :], m.raw[:, c, :], ACT.Copy).then_inc(m.e_wh, 1)

    def low_w(dve, i):
        c = ORDER[i]
        dve.wait_ge(m.e_wh, i + 1)
        nc.vector.tensor_tensor(m.wl[:, c, :], m.raw[:, c, :], m.wh[:, c, :], ALU.subtract).then_inc(m.e_wl, 1)

    m.once_normed, m.high_w, m.low_w = once_normed, high_w, low_w
    HALVES = [1, 2, 4, 8, 16, 32, 64]
    NL = 1 + len(HALVES)

    def group(t, g):
        ct, bb = divmod(g, B)
        return t[:, ct, bb * S:(bb + 1) * S]

    def tot(s, g):
        return group(m.D, g) if s == 1 else TOT[s][:, g, :]

    def lbanks(l, g):
        j = (l * NCH + g) % 4 * 2
        return m.psum[:, j:j + 2, :].rearrange("p b (n q) -> p (b n) q", q=2 * QB)

    def both_heads(l, g):
        return bank[(l * NCH + g) % 4 * 2].rearrange("p (c h q) -> p c h q", h=NH, q=QB)

    with nc.Block() as block:
        @block.sync
        def _(sp):
            sp.dma_start(masks[:], a["masks"]).then_inc(mask_in, 16)
            sp.dma_start(diag[:], a["diag"]).then_inc(mask_in, 16)
            sp.dma_start(rank[:], a["rank"]).then_inc(mask_in, 16)
            for i in range(2):
                c = slice(i * NMC // 2, (i + 1) * NMC // 2)
                sp.dma_start(m.raw[:, c, :], a["experts_w"].rearrange("p (c n) -> p c n", c=NMC)[:, c, :]
                             ).then_inc(raw_in, 16)
            sp.wait_ge(ct_ready, 1)
            sp.dma_start(m.comb_rows, combT[:]).then_inc(crow_out, 16)
            sp.wait_ge(crow_out, 16)
            sp.wait_ge(raw_in, 32)

        @block.gpsimd
        def _(pool):
            nc.gpsimd.memset(heads[:], 0.0).then_inc(heads_ready, 1)
            pool.wait_ge(heads_ready, 1)
            for h in range(NH):
                nc.gpsimd.memset(heads[h * LD:(h + 1) * LD, h:h + 1], 1.0).then_inc(heads_ready, 1)
                pool.wait_ge(heads_ready, 2 + h)
            for g in range(NCH):
                nc.gpsimd.memset(Q[g][:, 1, :].rearrange("p (n two) -> p n two", two=2)[:, :, 1], 0.0
                                 ).then_inc(odd_zero, 1)
            def pair_decays(s, g):
                v = tot(s, g).rearrange("p (n two) -> p n two", two=2)
                if s > 1:
                    pool.wait_ge(tot_done, (HALVES.index(s) - 1) * NCH + g + 1)
                nc.gpsimd.tensor_tensor(TOT[2 * s][:, g, :], v[:, :, 0], v[:, :, 1], ALU.mult).then_inc(tot_done, 1)

            def scale_k(s, g):
                k = group(m.K, g).rearrange("p (n two s) -> p n two s", two=2, s=s)
                t = tot(s, g).rearrange("p (n two) -> p n two", two=2)
                l = HALVES.index(s) + 1
                if l == 1:
                    pool.wait_ge(q_done, 2 * (g + 1))
                else:
                    pool.wait_ge(lev_ps, l * NCH + g + 1)
                if l >= 2:
                    pool.wait_ge(k_done, (l - 2) * NCH + g + 1)
                nc.gpsimd.tensor_tensor(k[:, :, 0, :], k[:, :, 0, :],
                                        t[:, :, 1].unsqueeze(2).broadcast_to([P, S // (2 * s), s]),
                                        ALU.mult).then_inc(k_done, 1)

            def zero_r2(g):
                pool.wait_ge(lev_ps, 2 * (g + 1))
                pool.wait_ge(tot_done, min(g + 2, NCH))
                pool.wait_ge(k_done, g + 1 if g < 2 else NCH)
                for h in range(NH):
                    other = slice((1 - h) * LD, (2 - h) * LD)
                    nc.gpsimd.memset(R2[g][other, h, :], 0.0).then_inc(r2_zero, 1)
                    pool.wait_ge(r2_zero, NH * g + h + 1)

            pair_decays(1, 0)
            scale_k(1, 0)
            pair_decays(1, 1)
            zero_r2(0)
            scale_k(1, 1)
            pair_decays(1, 2)
            zero_r2(1)
            scale_k(1, 2)
            pair_decays(1, 3)
            scale_k(1, 3)
            zero_r2(2)
            zero_r2(3)
            for s in HALVES[1:]:
                for g in range(NCH):
                    pair_decays(s, g)
                for g in range(NCH):
                    scale_k(s, g)
                if s == QB // 2:
                    for g in range(NCH):
                        pool.wait_ge(r_back, NH * (g + 1))
                        nc.gpsimd.memset(A[g][:], 0.0).then_inc(a_zero, 1)

        def take_y(act, g):
            act.wait_ge(ty_ps, g + 1)
            ct, bb = divmod(g, B)
            nc.scalar.activation(yh[:, ct, bb * S:(bb + 1) * S], m.psum[:, 2 * (g % 2):2 * (g % 2) + 2, :]
                                 .rearrange("p b c -> p (b c)"), ACT.Copy).then_inc(tyh_done, 1)



        @block.scalar
        def _(act):
            for g in range(NCH):
                act.wait_ge(lev_ps, 2 * (g + 1))
                act.wait_ge(r_done, NCH + g + 1)
                for h in range(NH):
                    rows = slice(h * LD, (h + 1) * LD)
                    nc.scalar.activation(R2[g][rows, h, :], group(m.R, g)[rows, :], ACT.Copy).then_inc(r2_in, 1)
            act.wait_ge(rt_done, 2)
            nc.scalar.activation(rt["e"][:], rt["l"][:], ACT.Exp).then_inc(exp_done, 1)
            for g in range(NCH):
                act.wait_ge(r_done, SMALL * NCH + g + 1)
                for h in range(NH):
                    rows = slice(h * LD, (h + 1) * LD)
                    nc.scalar.activation(group(m.R, g)[rows, :], R2[g][rows, h, :], ACT.Copy).then_inc(r_back, 1)
            for g in range(NCH):
                act.wait_ge(a_zero, g + 1)
                act.wait_ge(lev_take, SMALL * NCH + g + 1)
                for q in range(4):
                    r = slice(QB * q, QB * (q + 1))
                    nc.scalar.activation(A[g][r, :, r], AD[g][r, :, :], ACT.Copy).then_inc(ad_put, 1)
            act.wait_ge(ct_ps, 1)
            act.wait_ge(r_done, NL * NCH)
            act.wait_ge(k_done, (NL - 1) * NCH)
            nc.scalar.activation(combT[:], m.psum[0:NE, 0:4, :].rearrange("p b c -> p (b c)"), ACT.Copy
                                 ).then_inc(ct_ready, 1)
            for g in range(NCH):
                act.wait_ge(kt_ps, g + 1)
                if g >= 2:
                    act.wait_ge(u_ps, g - 1)
                nc.scalar.activation(kT[g % 2][:], m.psum[:, 4:6, :].rearrange("p b (n c) -> p (b n) c", c=P),
                                     ACT.Copy).then_inc(kt_done, 1)
                if g >= 2:
                    take_y(act, g - 2)
            take_y(act, NCH - 2)
            take_y(act, NCH - 1)
            act.wait_ge(raw_in, 32)
            act.wait_ge(ad_put, 4 * NCH)
            for i in range(2):
                m.high_w(i)

        def low_y(dve, g):
            dve.wait_ge(tyh_done, g + 1)
            ct, bb = divmod(g, B)
            v = slice(bb * S, (bb + 1) * S)
            nc.vector.tensor_tensor(yl[:, ct, v], m.psum[:, 2 * (g % 2):2 * (g % 2) + 2, :].rearrange("p b c -> p (b c)"),
                                    yh[:, ct, v], ALU.subtract).then_inc(tyl_done, 1)


        @block.vector
        def _(dve):

            def take_level(l, g):
                k = l * NCH + g
                if l <= 1:
                    dve.wait_ge(lev_ps, 2 * g + l + 1)
                    w = bank[2 * g + l][:, 0:NS].unsqueeze(2).broadcast_to([P, NS, QB])
                    if l == 0:
                        nc.vector.tensor_tensor(AD[g][:], w, diag[:].unsqueeze(1).broadcast_to([P, NS, QB]),
                                                ALU.mult).then_inc(lev_take, 1)
                    else:
                        dve.wait_ge(lev_take, 2 * g + 1)
                        nc.vector.copy_predicated(AD[g][:], masks[:, 1, :].unsqueeze(1).broadcast_to([P, NS, QB]),
                                                  w).then_inc(lev_take, 1)
                    return
                dve.wait_ge(lev_ps, k + 1)
                ps = lbanks(l, g)
                if l <= SMALL:
                    dve.wait_ge(lev_take, k - NCH + 1)
                    for h in range(NH):
                        mm = nc.vector.copy_predicated(AD[g][:, h * NC:(h + 1) * NC, :],
                                                       masks[:, l, :].unsqueeze(1).broadcast_to([P, NC, QB]),
                                                       both_heads(l, g)[:, :, h, :])
                    mm.then_inc(lev_take, 1)
                elif l == SMALL + 1:
                    dve.wait_ge(a_zero, g + 1)
                    nc.vector.tensor_copy(A[g][0:QB, :, QB:2 * QB], ps[0:QB, :, 0:QB])
                    nc.vector.tensor_copy(A[g][2 * QB:3 * QB, :, 3 * QB:], ps[2 * QB:3 * QB, :, 0:QB]
                                          ).then_inc(lev_take, 1)
                else:
                    nc.vector.tensor_copy(A[g][0:2 * QB, :, 2 * QB:], ps[0:2 * QB]).then_inc(lev_take, 1)

            def scale_r(l, g):
                if l <= 1:
                    dve.wait_ge(q_done, 2 * g + l + 1)
                else:
                    dve.wait_ge(lev_ps, l * NCH + g + 1)
                if l >= 1:
                    dve.wait_ge(r_done, (l - 1) * NCH + g + 1)
                r = group(m.R, g)
                if l == 0:
                    nc.vector.tensor_tensor(r, r, group(m.D, g), ALU.mult).then_inc(r_done, 1)
                    return
                s = HALVES[l - 1]
                if s > 1:
                    dve.wait_ge(tot_done, (l - 2) * NCH + g + 1)
                if 2 <= l <= SMALL:
                    for h in range(NH):
                        rows = slice(h * LD, (h + 1) * LD)
                        v = R2[g][rows, h, :].rearrange("p (n two s) -> p n two s", two=2, s=s)
                        t = tot(s, g)[rows, :].rearrange("p (n two) -> p n two", two=2)
                        mm = nc.vector.tensor_tensor(v[:, :, 1, :], v[:, :, 1, :],
                                                     t[:, :, 0].unsqueeze(2).broadcast_to([LD, S // (2 * s), s]),
                                                     ALU.mult)
                    mm.then_inc(r_done, 1)
                    return
                if l == SMALL + 1:
                    dve.wait_ge(r_back, NH * (g + 1))
                v = r.rearrange("p (n two s) -> p n two s", two=2, s=s)
                t = tot(s, g).rearrange("p (n two) -> p n two", two=2)
                nc.vector.tensor_tensor(v[:, :, 1, :], v[:, :, 1, :],
                                        t[:, :, 0].unsqueeze(2).broadcast_to([P, S // (2 * s), s]),
                                        ALU.mult).then_inc(r_done, 1)

            def wide(v):
                return v.unsqueeze(2).broadcast_to([P, NT, NE])

            def route(step):
                if step >= 1:
                    dve.wait_ge(rt_done, step)
                if step == 2:
                    dve.wait_ge(exp_done, 1)
                tt, red = nc.vector.tensor_tensor, nc.vector.tensor_reduce
                second = step >= 11
                q, v = (rt["q2"], rt["s2"]) if second else (rt["q1"], rt["s1"])
                left, i = (rt["sel"], 2) if second else (rt["p"], 0)
                if step == 0:
                    ins = red(r1[:, 0, :], rt["l"][:], AX_X, ALU.max)
                elif step == 1:
                    ins = tt(rt["l"][:], rt["l"][:], wide(r1[:, 0, :]), ALU.subtract)
                elif step == 2:
                    ins = red(r1[:, 1, :], rt["e"][:], AX_X, ALU.add)
                elif step == 3:
                    ins = nc.vector.reciprocal(r1[:, 2, :], r1[:, 1, :])
                elif step == 4:
                    ins = tt(rt["p"][:], rt["e"][:], wide(r1[:, 2, :]), ALU.mult)
                elif step in (5, 11):
                    ins = red(r1[:, 3 + i, :], left[:], AX_X, ALU.max)
                elif step in (6, 12):
                    ins = tt(q[:], left[:], wide(r1[:, 3 + i, :]), ALU.is_equal)
                elif step in (7, 13):
                    ins = tt(v[:], q[:], rank[:].unsqueeze(1).broadcast_to([P, NT, NE]), ALU.mult)
                elif step in (8, 14):
                    ins = red(r1[:, 4 + i, :], v[:], AX_X, ALU.max)
                elif step in (9, 15):
                    ins = tt(q[:], v[:], wide(r1[:, 4 + i, :]), ALU.is_equal)
                elif step == 10:
                    ins = nc.vector.scalar_tensor_tensor(rt["sel"][:], q[:], -2.0, rt["p"][:], ALU.mult, ALU.add)
                elif step == 16:
                    ins = tt(rt["e"][:], rt["q1"][:], rt["q2"][:], ALU.add)
                elif step == 17:
                    ins = tt(r1[:, 0, :], r1[:, 3, :], r1[:, 5, :], ALU.add)
                elif step == 18:
                    ins = nc.vector.tensor_scalar(r1[:, 1, :], r1[:, 0, :], 1e-20, None, ALU.add)
                elif step == 19:
                    ins = nc.vector.reciprocal(r1[:, 2, :], r1[:, 1, :])
                elif step == 20:
                    ins = tt(rt["s1"][:], rt["p"][:], rt["e"][:], ALU.mult)
                else:
                    ins = tt(rt["l"][:], rt["s1"][:], wide(r1[:, 2, :]), ALU.mult)
                ins.then_inc(rt_done, 1)

            def multiply(l, g):
                if l == 0:
                    nc.vector.tensor_tensor(Q[g][:, 0, :], group(m.K, g), group(m.R, g), ALU.mult).then_inc(q_done, 1)
                    return
                dve.wait_ge(r_done, g + 1)
                dve.wait_ge(odd_zero, g + 1)
                q, k, r = (v.rearrange("p (n two) -> p n two", two=2) for v in (Q[g][:, 1, :], group(m.K, g),
                                                                               group(m.R, g)))
                nc.vector.tensor_tensor(q[:, :, 0], k[:, :, 0], r[:, :, 1], ALU.mult).then_inc(q_done, 1)

            for g in range(NCH):
                multiply(0, g)
                scale_r(0, g)
                multiply(1, g)
            dve.wait_ge(mask_in, 48)
            for g in range(NCH):
                scale_r(1, g)
                take_level(0, g)
                take_level(1, g)
            for l in range(2, NL):
                for g in range(NCH):
                    scale_r(l, g)
                    take_level(l, g)
                    if (l - 2) * NCH + g < NSTEP:
                        route((l - 2) * NCH + g)
            for g in range(NCH):
                dve.wait_ge(u_ps, g + 1)
                u = bank[6 + g % 2]
                if g >= 2:
                    dve.wait_ge(ty_ps, g - 1)
                if g == 0:
                    dve.wait_ge(tot_done, NCH * len(HALVES))
                nc.vector.tensor_copy(ST[g % 2][:, 1, :], u[:, 0:LD]).then_inc(st_done, 1)
                for c in range(1, NC - 1):
                    dve.wait_ge(st_done, g * (NC - 1) + c)
                    nc.vector.scalar_tensor_tensor(ST[g % 2][:, c + 1, :], ST[g % 2][:, c, :], TOT[128][:, g, c:c + 1],
                                                   u[:, c * LD:(c + 1) * LD], ALU.mult, ALU.add).then_inc(st_done, 1)
                if g >= 1:
                    low_y(dve, g - 1)
            low_y(dve, NCH - 1)
            m.once_normed(dve, 0)
            for i in range(2):
                m.low_w(dve, i)
            for n in range(0, NT, 2):
                dve.wait_ge(so_ps, n // 2 + 1)
                nc.vector.tensor_copy(m.s[:, n:n + 2, :], bank[4 + n // 2 % 4].rearrange("p (n e) -> p n e", n=2)
                                      ).then_inc(so_done, 1)

        @block.tensor
        def _(pe):
            def level(l, g):
                k = l * NCH + g
                if k >= 4:
                    pe.wait_ge(lev_take, k - 3)
                if l >= 1:
                    pe.wait_ge(r_done, (l - 1) * NCH + g + 1)
                if l >= 2:
                    pe.wait_ge(k_done, (l - 2) * NCH + g + 1)
                kk, rr, ps = group(m.K, g), group(m.R, g), lbanks(l, g)
                if l == 2:
                    pe.wait_ge(r2_in, NH * (g + 1))
                    pe.wait_ge(r2_zero, NH * (g + 1))
                if l == SMALL + 1:
                    pe.wait_ge(r_back, NH * (g + 1))
                if l <= SMALL:
                    for c in range(NC):
                        for q in range(4):
                            t = c * CH + q * QB
                            mm = nc.tensor.matmul(both_heads(l, g)[QB * q:QB * (q + 1), c, :, :], kk[:, t:t + QB],
                                                  R2[g][:, :, t:t + QB], start=True, stop=True)
                    mm.then_inc(lev_ps, 1)
                    return
                for n in range(NS):
                    h, c = divmod(n, NC)
                    ch = slice(h * LD, (h + 1) * LD)
                    if l == SMALL + 1:
                        for q in (0, 2):
                            t = c * CH + q * QB
                            mm = nc.tensor.matmul(ps[QB * q:QB * (q + 1), n, 0:QB], kk[ch, t:t + QB],
                                                  rr[ch, t + QB:t + 2 * QB], start=True, stop=True)
                    else:
                        t = c * CH
                        mm = nc.tensor.matmul(ps[0:2 * QB, n, :],
                                              kk[ch, t:t + 2 * QB], rr[ch, t + 2 * QB:t + CH], start=True, stop=True)
                mm.then_inc(lev_ps, 1)

            def turn_k(g):
                pe.wait_ge(k_done, (NL - 2) * NCH + g + 1)
                if g >= 1:
                    pe.wait_ge(kt_done, g)
                for c in range(NC):
                    mm = nc.tensor.transpose(bank[4 + c // 4][:, c % 4 * P:(c % 4 + 1) * P],
                                             group(m.K, g)[:, c * CH:(c + 1) * CH], m.ident1[:])
                mm.then_inc(kt_ps, 1)

            def update(g):
                ct, bb = divmod(g, B)
                pe.wait_ge(kt_done, g + 1)
                if g >= 2:
                    pe.wait_ge(st_done, (g - 1) * (NC - 1))
                for c in range(NC - 1):
                    for h in range(NH):
                        ch = slice(h * LD, (h + 1) * LD)
                        mm = nc.tensor.matmul(bank[6 + g % 2][ch, c * LD:(c + 1) * LD], kT[g % 2][:, c, ch],
                                              m.V[:, bb * NC + c, ct * P + h * LD:ct * P + (h + 1) * LD],
                                              start=True, stop=True)
                mm.then_inc(u_ps, 1)

            def output(g):
                ct, bb = divmod(g, B)
                pe.wait_ge(st_done, (g + 1) * (NC - 1))
                pe.wait_ge(ad_put, 4 * (g + 1))
                pe.wait_ge(r_done, (NL - 1) * NCH + g + 1)
                if g >= 2:
                    pe.wait_ge(tyl_done, g - 1)
                else:
                    pe.wait_ge(ct_ready, 1)
                for c in range(NC):
                    for h in range(NH):
                        ch = slice(h * LD, (h + 1) * LD)
                        out = m.psum[ch, 2 * (g % 2) + c // 4, c % 4 * CH:(c % 4 + 1) * CH]
                        mm = nc.tensor.matmul(out, m.V[:, bb * NC + c, ct * P + h * LD:ct * P + (h + 1) * LD],
                                              A[g][:, h * NC + c, :], start=True, stop=(c == 0))
                        if c:
                            mm = nc.tensor.matmul(out, ST[g % 2][ch, c, :], group(m.R, g)[ch, c * CH:(c + 1) * CH],
                                                  start=False, stop=True)
                mm.then_inc(ty_ps, 1)

            def tokens_weights(l, g):
                pe.wait_ge(q_done, 2 * g + l + 1)
                for c in range(NC):
                    out = bank[2 * g + l][:, 0:NS].rearrange("p (h c) -> p h c", h=NH)[:, :, c]
                    for q in range(4):
                        t = c * CH + q * QB
                        mm = nc.tensor.matmul(out[QB * q:QB * (q + 1), :], Q[g][:, l, t:t + QB], heads[:],
                                              start=True, stop=True)
                mm.then_inc(lev_ps, 1)

            pe.wait_ge(heads_ready, 1 + NH)
            for g in range(NCH):
                for l in range(2):
                    tokens_weights(l, g)
            for l in range(2, NL):
                for g in range(NCH):
                    level(l, g)
            pe.wait_ge(lev_take, NL * NCH - 2)
            pe.wait_ge(rt_done, NSTEP)
            for n in range(NT):
                mm = nc.tensor.transpose(bank[n // 4][0:NE, n % 4 * P:(n % 4 + 1) * P], rt["l"][:, n, :], m.ident1[:])
            mm.then_inc(ct_ps, 1)
            pe.wait_ge(lev_take, NL * NCH)
            turn_k(0)
            turn_k(1)
            update(0)
            for g in range(NCH):
                if g + 1 < NCH:
                    update(g + 1)
                if g + 2 < NCH:
                    turn_k(g + 2)
                output(g)
            for n in range(NT):
                if n == 0:
                    pe.wait_ge(tyl_done, NCH - 1)
                if n == NT // 2:
                    pe.wait_ge(tyl_done, NCH)
                if n >= 8 and n % 2 == 0:
                    pe.wait_ge(so_done, n // 2 - 3)
                tok = slice(n * P, (n + 1) * P)
                mm = three(nc, bank[4 + n // 2 % 4][:, n % 2 * E:(n % 2 + 1) * E],
                           [(yh[:, kc, tok], yl[:, kc, tok], m.woh1[:, kc, :], m.wol1[:, kc, :]) for kc in range(KC)])
                if n % 2:
                    mm.then_inc(so_ps, 1)


def experts_stage(nc, m, a):
    at, sem, bank = m.at, m.sem, m.bank
    b = m.base
    xl = at("x1_l", [P, KC, T], F32R, b); b += KC * T * 4
    b += NT * E * 4
    xh = at("x1_h", [P, KC, T], F32R, b); b += KC * T * 4
    xa = m.xa1; b += TPB * E * 4
    comb = at("comb_b", [P, 4, BLK], F32, b); b += 4 * BLK * 4
    gate = at("m_gate", [P, TPB, E], F32, b); b += TPB * E * 4
    assert b <= m.p3
    b = m.p3
    wh, wl = m.wh, m.wl; b += NMC * WP * 4
    hh = at("m_hh", [P, 3, BLK], F32R, b); b += 3 * BLK * 4
    hl = at("m_hl", [P, 3, BLK], F32R, b); b += 3 * BLK * 4
    sg = at("m_silu", [P, 2, BLK], F32, b); b += 2 * BLK * 4
    hf = at("m_h_f", [P, 3, BLK], F32, b); b += 3 * BLK * 4
    assert b <= m.rt_at + 9 * NT * NE * 4, b
    gs = gate

    xa_ready, wh_ready, wl_ready = m.e_xa, m.e_wh, m.e_wl
    names = ("e_t_ps", "e_xh", "e_xl", "e_gu_ps", "e_silu", "e_h", "e_hc", "e_hi", "e_lo",
             "e_down", "e_gate", "e_gs", "e_x", "e_out")
    (t_ps, xh_ready, xl_ready, gu_ps, silu_done, h_done, hc_done, hi_done, lo_done,
     down_done, gate_done, gs_done, x_done, x_out) = (sem(n) for n in names)
    comb_in = [sem(f"comb_in{i}") for i in range(4)]

    NX = sum(c < NEC for c in ORDER)
    TURN_AT = 6

    def ncomb(k):
        return k // NMC * NX + sum(c < NEC for c in ORDER[:k % NMC + 1])

    def slot(tb, i):
        return place(tb, i) % 2 * 2

    def place(tb, i):
        return 1 + tb * (NMC + 1) + i + (i >= TURN_AT and tb < NB - 1)

    def turn_place(g):
        return 0 if g == 0 else 1 + (g - 1) * (NMC + 1) + TURN_AT

    WHAT = {}
    for tb in range(NB):
        WHAT[turn_place(tb)] = ("x", tb)
        for i in range(NMC):
            WHAT[place(tb, i)] = ("h", tb * NMC + i)

    def wgu(t, w, kc, c):
        i = (2 * w + kc) * P
        return t[:, c, i:i + P]

    with nc.Block() as block:
        def store(sp, tb):
            sp.wait_ge(x_done, tb + 1)
            ts = slice(tb * TPB, (tb + 1) * TPB)
            sp.dma_start(a["out"].rearrange("(n p) f -> p n f", p=P)[:, ts, :], m.x[:, ts, :]).then_inc(x_out, 16)

        @block.sync
        def _(sp):
            for tb in range(NB):
                for c in range(NEC):
                    j = tb * NEC + c
                    if j >= 4:
                        sp.wait_ge(hc_done, j - 3)
                    lo = c * P
                    while lo < (c + 1) * P:
                        e = lo // EI
                        hi = min((c + 1) * P, (e + 1) * EI)
                        sp.dma_start(comb[lo - c * P:hi - c * P, j % 4, :],
                                     m.comb_rows[e:e + 1, tb * BLK:(tb + 1) * BLK].broadcast_to([hi - lo, BLK])
                                     ).then_inc(comb_in[j % 4], 16)
                        lo = hi
                if tb >= 1:
                    store(sp, tb - 1)
            store(sp, NB - 1)
            sp.wait_ge(x_out, 16 * NB)

        def pieces_in(j):
            def count(i):
                c = i % NEC
                return (c * P + P - 1) // EI - c * P // EI + 1
            return sum(count(i) for i in range(j % 4, j + 1, 4))

        @block.gpsimd
        def _(pool):
            for tb in range(NB):
                for c in ORDER:
                    if c >= NEC:
                        continue
                    j = tb * NEC + c
                    k = tb * NMC + ORDER.index(c)
                    pool.wait_ge(comb_in[j % 4], 16 * pieces_in(j))
                    pool.wait_ge(h_done, k + 1)
                    nc.gpsimd.tensor_tensor(hf[:, k % 3, :], hf[:, k % 3, :], comb[:, j % 4, :],
                                            ALU.mult).then_inc(hc_done, 1)

        @block.scalar
        def _(act):
            def high(k):
                act.wait_ge(h_done, k + 1)
                if ORDER[k % NMC] < NEC:
                    act.wait_ge(hc_done, ncomb(k))
                if k >= 3:
                    act.wait_ge(down_done, k - 2)
                nc.scalar.activation(hh[:, k % 3, :], hf[:, k % 3, :], ACT.Copy).then_inc(hi_done, 1)

            def high_x(g):
                s = turn_place(g) % 2 * 2
                for kc in range(KC):
                    act.wait_ge(t_ps, g * KC + kc + 1)
                    nc.scalar.activation(xh[:, kc, g * BLK:(g + 1) * BLK], bank[s + kc], ACT.Copy).then_inc(xh_ready, 1)

            def gate_out(tb):
                act.wait_ge(down_done, (tb + 1) * NMC)
                if tb >= 1:
                    act.wait_ge(x_done, tb)
                nc.scalar.activation(gate[:], m.psum[:, 4:8, 0:E], ACT.Silu).then_inc(gate_done, 1)

            high_x(0)
            for tb in range(NB):
                for i in range(NMC):
                    k = tb * NMC + i
                    if i == TURN_AT and tb + 1 < NB:
                        high_x(tb + 1)
                    act.wait_ge(gu_ps, k + 1)
                    if k >= 2:
                        act.wait_ge(h_done, k - 1)
                    nc.scalar.activation(sg[:, k % 2, :], bank[slot(tb, i)], ACT.Silu).then_inc(silu_done, 1)
                    if k >= 1:
                        high(k - 1)
                    if tb == 0 and i + 2 < NMC:
                        m.high_w(i + 2)
                    if i == 1 and tb >= 1:
                        gate_out(tb - 1)
            high(NB * NMC - 1)
            gate_out(NB - 1)

        @block.vector
        def _(dve):
            def low_x(g):
                cols = slice(g * BLK, (g + 1) * BLK)
                s = turn_place(g) % 2 * 2
                for kc in range(KC):
                    dve.wait_ge(xh_ready, g * KC + kc + 1)
                    nc.vector.tensor_tensor(xl[:, kc, cols], bank[s + kc], xh[:, kc, cols],
                                            ALU.subtract).then_inc(xl_ready, 1)

            def low_h(k):
                dve.wait_ge(hi_done, k + 1)
                if k >= 3:
                    dve.wait_ge(down_done, k - 2)
                nc.vector.tensor_tensor(hl[:, k % 3, :], hf[:, k % 3, :], hh[:, k % 3, :],
                                        ALU.subtract).then_inc(lo_done, 1)

            def add_gated(tb):
                ts = slice(tb * TPB, (tb + 1) * TPB)
                dve.wait_ge(gate_done, tb + 1)
                nc.vector.tensor_tensor(gs[:], gate[:], m.s[:, ts, :], ALU.mult).then_inc(gs_done, 1)
                dve.wait_ge(gs_done, tb + 1)
                nc.vector.tensor_tensor(m.x[:, ts, :], m.x[:, ts, :], gs[:], ALU.add).then_inc(x_done, 1)

            low_x(0)
            for tb in range(NB):
                for i in range(NMC):
                    k = tb * NMC + i
                    if i == TURN_AT and tb + 1 < NB:
                        low_x(tb + 1)
                    dve.wait_ge(silu_done, k + 1)
                    if k >= 3:
                        dve.wait_ge(lo_done, k - 2)
                    nc.vector.tensor_tensor(hf[:, k % 3, :], bank[slot(tb, i) + 1], sg[:, k % 2, :],
                                            ALU.mult).then_inc(h_done, 1)
                    if k >= 1:
                        low_h(k - 1)
                    if tb == 0 and i + 2 < NMC:
                        m.low_w(dve, i + 2)
                    if i == TURN_AT - 2 and tb + 1 < NB:
                        dve.wait_ge(t_ps, KC * (tb + 1))
                        m.once_normed(dve, tb + 1)
                    if i == 1 and tb >= 1:
                        add_gated(tb - 1)
            low_h(NB * NMC - 1)
            add_gated(NB - 1)

        @block.tensor
        def _(pe):
            def slot_free(q):
                if q >= 2:
                    what, k = WHAT[q - 2]
                    if what == "x":
                        pe.wait_ge(xl_ready, KC * (k + 1))
                    else:
                        pe.wait_ge(h_done, k + 1)
                return q % 2 * 2

            def turn(g):
                s = slot_free(turn_place(g))
                pe.wait_ge(xa_ready, TPB * (g + 1))
                for kc in range(KC):
                    for i in range(TPB):
                        mm = nc.tensor.transpose(bank[s + kc][:, i * P:(i + 1) * P], xa[:, i, kc * P:(kc + 1) * P],
                                                 m.ident1[:])
                    mm.then_inc(t_ps, 1)

            def up(tb, i):
                c = ORDER[i]
                cols = slice(tb * BLK, (tb + 1) * BLK)
                s = slot_free(place(tb, i))
                if tb == 0:
                    pe.wait_ge(wl_ready, i + 1)
                if i == 0:
                    pe.wait_ge(xl_ready, KC * (tb + 1))
                for w in range(2):
                    mm = three(nc, bank[s + w], [(wgu(wh, w, kc, c), wgu(wl, w, kc, c), xh[:, kc, cols], xl[:, kc, cols])
                                                 for kc in range(KC)])
                mm.then_inc(gu_ps, 1)

            def down(tb, i):
                c = ORDER[i]
                k = tb * NMC + i
                pe.wait_ge(lo_done, k + 1)
                if i == 0 and tb >= 1:
                    pe.wait_ge(gate_done, tb)
                for j in range(TPB):
                    tok = slice(j * P, (j + 1) * P)
                    mm = three(nc, bank[4 + j][:, 0:E], [(hh[:, k % 3, tok], hl[:, k % 3, tok],
                                                          wh[:, c, 4 * P:], wl[:, c, 4 * P:])],
                               start=(i == 0), stop=(i == NMC - 1))
                mm.then_inc(down_done, 1)

            turn(0)
            for tb in range(NB):
                for i in range(NMC):
                    if i == TURN_AT and tb + 1 < NB:
                        turn(tb + 1)
                    up(tb, i)
                    if tb * NMC + i >= 2:
                        down(*divmod(tb * NMC + i - 2, NMC))
            down(NB - 1, NMC - 2)
            down(NB - 1, NMC - 1)


def kernel(**inputs):
    import numpy as np
    import concourse.bacc as bacc
    from concourse.bass_utils import run_bass_kernel_spmd

    i = {n: np.asarray(v) for n, v in inputs.items()}

    def rows(*arrays):
        return np.concatenate(arrays, 0)

    def columns(v):
        return v.reshape(KC, P).T

    q_rows = [(u * HALF + d) * HEADS + h for u in range(2) for h in range(HEADS) for d in range(HALF)]
    k_rows, k_rows_turned = ([((u + turn) % 2 * HALF + d) * KV + kv for u in range(2) for kv in range(KV)
                              for d in range(HALF)] for turn in range(2))
    v_rows = [d * KV + kv for kv in range(KV) for d in range(HD)]

    freq = np.float32(1.0) / np.float32(10000.0) ** (np.arange(HALF, dtype=np.float32) * np.float32(2.0) / np.float32(HD))
    angle = np.arange(S, dtype=np.float32)[:, None] * freq[None, :]
    cos = np.tile(np.cos(angle).T, (P // HALF, 1))
    sin = np.tile(np.sin(angle).T, (P // HALF, 1))
    sin_k = sin.copy()
    sin_k[:P // 2] *= -1
    masks = np.zeros((P, SMALL + 1, QB), np.int32)
    u, t = (np.arange(P) % QB)[:, None], np.arange(QB)[None, :]
    for level in range(SMALL):
        h = 1 << level
        masks[:, level + 1, :] = (u // (2 * h) == t // (2 * h)) & (u % (2 * h) < h) & (t % (2 * h) >= h)

    def gap(v, n):
        return np.zeros((n, v.shape[1]), v.dtype)

    down_idx = i["L0_ffn_down_idx"].T
    pad = NMC * P - MI
    pieces = []
    for name in ("gate", "up"):
        w = rows(i[f"L1_ffn_expert_{name}"].reshape(NE * EI, E), i[f"L1_ffn_shared_{name}"])
        w = rows(w, gap(w, pad)).T.reshape(KC, P, NMC, P)
        pieces += [w[kc] for kc in range(KC)]
    w = rows(i["L1_ffn_expert_down"].transpose(0, 2, 1).reshape(NE * EI, E), i["L1_ffn_shared_down"].T)
    pieces.append(rows(w, gap(w, pad)).reshape(NMC, P, E).transpose(1, 0, 2))
    experts_w = np.concatenate(pieces, 2).reshape(P, NMC * WP)
    arrays = dict(
        x=i["L0_attn_x"].reshape(T, E), ident=np.eye(P, dtype=np.float32),
        wqkv=rows(i["L0_attn_W_Q"][q_rows], i["L0_attn_W_K"][k_rows], i["L0_attn_W_K"][k_rows_turned],
                  i["L0_attn_W_V"][v_rows]).T,
        cos=cos, sin=sin, sink=sin_k, wo=i["L0_attn_W_O"].T, lut=i["L0_ffn_lut"],
        gu_idx=rows(i["L0_ffn_gate_idx"], i["L0_ffn_up_idx"]).T,
        down_idx=rows(down_idx, gap(down_idx, NI * P - INTER)),
        wx_t=i["L1_attn_Wx"].T, ww=i["L1_attn_Ww"], wk=i["L1_attn_Wk"], wr=i["L1_attn_Wr"], wv=i["L1_attn_Wv"],
        wout=i["L1_attn_Wout"], gamma=columns(i["L1_attn_gamma"]), beta=columns(i["L1_attn_beta"]),
        bw=columns(i["L1_attn_bw"]), masks=masks, diag=(u == t).astype(np.float32),
        gate_w_t=i["L1_ffn_gate_w"].T, rank=np.tile(np.arange(NE, 0, -1, dtype=np.float32), (P, 1)), experts_w=experts_w)
    arrays = {n: np.ascontiguousarray(v) for n, v in arrays.items()}

    nc = bacc.Bacc("TRN2", target_bir_lowering=False, num_devices=1)
    a = {n: nc.dram_tensor(n, v.shape, mybir.dt.from_np(v.dtype), kind="ExternalInput").ap()
         for n, v in arrays.items()}
    a["out"] = nc.dram_tensor("out", (T, E), F32, kind="ExternalOutput").ap()
    program(nc, a)
    result = run_bass_kernel_spmd(nc, [arrays], core_ids=[0])
    return result.results[0]["out"].reshape(B, S, E)
```
